# Optimizing a Trainium2 kernel written in Bass

```python
import numpy as np
import jax
import jax.numpy as jnp

def _softmax(x, axis=-1):
    return jax.nn.softmax(x, axis=axis)

def _gelu(x):
    return jax.nn.gelu(x, approximate=True)

def _silu(x):
    return jax.nn.silu(x)

def _sigmoid(x):
    return jax.nn.sigmoid(x)

def _layernorm(x, axis=-1, eps=1e-05):
    m = jnp.mean(x, axis=axis, keepdims=True)
    v = jnp.var(x, axis=axis, keepdims=True)
    return (x - m) / jnp.sqrt(v + eps)

def _scatter_add(tgt, idx, src, axis=0):
    return tgt.at[idx].add(src)

def _segment_sum(src, seg, n):
    return jax.ops.segment_sum(src, seg, n)
kernel_name = 'mk_perceiver_d4_seqx_r4_28198d'

def setup_inputs(seed: int=0):
    np.random.seed(seed)
    _w = jnp.asarray

    def _rec_inputs():
        import jax
        import jax.numpy as jnp
        _rk = jax.random.key(seed)
        x = -0.0003929 + 0.9999 * jax.random.normal(jax.random.fold_in(_rk, 1), (32, 32, 256), jnp.float32)
        _lenS = 32 - jax.random.randint(jax.random.fold_in(_rk, 7), (32,), 0, max(1, 32 // 4) + 1, jnp.int32)
        _lenS2 = 257 - jax.random.randint(jax.random.fold_in(_rk, 8), (32,), 0, max(1, 257 // 4) + 1, jnp.int32)
        _ctx_768P = jax.random.normal(jax.random.fold_in(_rk, 11), (32, 16, 192), jnp.float32)
        _ctx_768c = jax.random.dirichlet(jax.random.fold_in(_rk, 511), 0.3 * jnp.ones((16,), jnp.float32), (32, 257))
        _ctx_768t = jnp.einsum('bsk,bkd->bsd', _ctx_768c, _ctx_768P)
        _ctx_768t = _ctx_768t * jax.lax.rsqrt(jnp.mean(jnp.square(_ctx_768t)) + 1e-12) * 0.953939
        ctx_768 = 2.09791e-05 + 1.00001 * (_ctx_768t + 0.3 * jax.random.normal(jax.random.fold_in(_rk, 611), (32, 257, 192), jnp.float32))
        return (x, ctx_768)
    x, ctx_768 = _rec_inputs()

    def _L0_xattn_setup():
        import jax, jax.numpy as jnp
        import numpy as np
        HEADS = 16
        DIM_HEAD = 64
        SCALE = DIM_HEAD ** (-0.5)
        key = jax.random.key(seed)
        ks = jax.random.split(key, 7)
        B, SQ, SKV, QD, CD, ID = (4, 1024, 256, 256, 192, HEADS * DIM_HEAD)
        s = lambda d: 1.0 / np.sqrt(d)
        return {'x': jax.random.normal(ks[0], (B, SQ, QD), jnp.float32), 'context': jax.random.normal(ks[1], (B, SKV, CD), jnp.float32), 'Wq': jax.random.normal(ks[2], (QD, ID), jnp.float32) * s(QD), 'Wk': jax.random.normal(ks[3], (CD, ID), jnp.float32) * s(CD), 'Wv': jax.random.normal(ks[4], (CD, ID), jnp.float32) * s(CD), 'Wo': jax.random.normal(ks[5], (ID, QD), jnp.float32) * s(ID), 'bo': jnp.zeros((QD,), jnp.float32)}
    _L0_xattn_all = _L0_xattn_setup()
    _L0_xattn_in = {k: v for k, v in _L0_xattn_all.items() if k in ('Wq', 'Wk', 'Wv', 'Wo', 'bo')}
    del _L0_xattn_all

    def _L0_attn_setup():
        import jax, jax.numpy as jnp
        import numpy as np
        D_MODEL = 256
        NHEAD = 16
        D_K = D_MODEL // NHEAD
        MAX_REL = 256
        key = jax.random.key(seed)
        ks = jax.random.split(key, 6)
        B, S = (4, 512)
        s = 1.0 / np.sqrt(D_MODEL)
        x = jax.random.normal(ks[0], (B, S, D_MODEL), dtype=jnp.float32)
        W_qkv = jax.random.normal(ks[1], (D_MODEL, 3 * D_MODEL), dtype=jnp.float32) * s
        b_qkv = jnp.zeros((3 * D_MODEL,), dtype=jnp.float32)
        W_out = jax.random.normal(ks[2], (D_MODEL, D_MODEL), dtype=jnp.float32) * s
        b_out = jnp.zeros((D_MODEL,), dtype=jnp.float32)
        rel_bias = jax.random.normal(ks[3], (2 * MAX_REL + 1, NHEAD), dtype=jnp.float32) * 0.02
        return {'x': x, 'W_qkv': W_qkv, 'b_qkv': b_qkv, 'W_out': W_out, 'b_out': b_out, 'rel_bias': rel_bias}
    _L0_attn_all = _L0_attn_setup()
    _L0_attn_in = {k: v for k, v in _L0_attn_all.items() if k in ('W_qkv', 'b_qkv', 'W_out', 'b_out', 'rel_bias')}
    del _L0_attn_all

    def _L0_ffn_setup():
        import jax, jax.numpy as jnp
        import numpy as np
        BLOCK = 16
        _GRID = jnp.array([0.0, 0.5, 1.0, 1.5, 2.0, 3.0, 4.0, 6.0], dtype=jnp.float32)
        _MID = jnp.array([0.25, 0.75, 1.25, 1.75, 2.5, 3.5, 5.0], dtype=jnp.float32)

        def fp4_quant_dequant(x):
            shape = x.shape
            xb = x.reshape(shape[:-1] + (shape[-1] // BLOCK, BLOCK))
            scale = jnp.max(jnp.abs(xb), axis=-1, keepdims=True) / 6.0
            scale = jnp.maximum(scale, jnp.float32(1e-12))
            xn = xb / scale
            idx = jnp.searchsorted(_MID, jnp.abs(xn))
            q = _GRID[idx] * jnp.sign(xn) * scale
            return q.reshape(shape)

        def fp4_linear(x, w):
            xq = fp4_quant_dequant(x)
            wq = fp4_quant_dequant(w)
            return jnp.einsum('bsk,nk->bsn', xq, wq)
        key = jax.random.key(seed)
        k1, k2, k3, k4 = jax.random.split(key, 4)
        H, I = (256, 704)
        x = jax.random.normal(k1, (4, 1024, H), dtype=jnp.float32)
        w_gate = jax.random.normal(k2, (I, H), dtype=jnp.float32) * 0.02
        w_up = jax.random.normal(k3, (I, H), dtype=jnp.float32) * 0.02
        w_down = jax.random.normal(k4, (H, I), dtype=jnp.float32) * 0.02
        return {'x': x, 'w_gate': w_gate, 'w_up': w_up, 'w_down': w_down}
    _L0_ffn_all = _L0_ffn_setup()
    _L0_ffn_in = {k: v for k, v in _L0_ffn_all.items() if k in ('w_gate', 'w_up', 'w_down')}
    del _L0_ffn_all

    def _L1_xattn_setup():
        import jax, jax.numpy as jnp
        import numpy as np
        NUM_HEADS = 16
        CLAMP = 10000.0
        key = jax.random.key(seed)
        ks = jax.random.split(key, 8)
        B, Nq, Nkv, Cq, Ckv = (4, 512, 512, 256, 192)
        s_q = 1.0 / np.sqrt(Cq)
        s_kv = 1.0 / np.sqrt(Ckv)
        return {'query': jax.random.normal(ks[0], (B, Nq, Cq), jnp.float32), 'key_value': jax.random.normal(ks[1], (B, Nkv, Ckv), jnp.float32), 'Wq': jax.random.normal(ks[2], (Cq, Cq), jnp.float32) * s_q, 'bq': jnp.zeros((Cq,), jnp.float32), 'Wk': jax.random.normal(ks[3], (Ckv, Cq), jnp.float32) * s_kv, 'bk': jnp.zeros((Cq,), jnp.float32), 'Wv': jax.random.normal(ks[4], (Ckv, Cq), jnp.float32) * s_kv, 'bv': jnp.zeros((Cq,), jnp.float32), 'Wo': jax.random.normal(ks[5], (Cq, Cq), jnp.float32) * s_q, 'bo': jnp.zeros((Cq,), jnp.float32)}
    _L1_xattn_all = _L1_xattn_setup()
    _L1_xattn_in = {k: v for k, v in _L1_xattn_all.items() if k in ('Wq', 'bq', 'Wk', 'bk', 'Wv', 'bv', 'Wo', 'bo')}
    del _L1_xattn_all

    def _L1_attn_setup():
        import jax, jax.numpy as jnp
        import numpy as np
        B, S, C = (32, 256, 256)
        key = jax.random.key(seed)
        ks = jax.random.split(key, 4)
        scale = 1.0 / np.sqrt(C)
        x = jax.random.normal(ks[0], (B, S, C), dtype=jnp.float32)
        Wq = jax.random.normal(ks[1], (C, C), dtype=jnp.float32) * scale
        Wk = jax.random.normal(ks[2], (C, C), dtype=jnp.float32) * scale
        Wv = jax.random.normal(ks[3], (C, C), dtype=jnp.float32) * scale
        gamma = jnp.zeros((1,), dtype=jnp.float32)
        return {'x': x, 'Wq': Wq, 'Wk': Wk, 'Wv': Wv, 'gamma': gamma}
    _L1_attn_all = _L1_attn_setup()
    _L1_attn_in = {k: v for k, v in _L1_attn_all.items() if k in ('Wq', 'Wk', 'Wv', 'gamma')}
    del _L1_attn_all

    def _L1_ffn_setup():
        import jax, jax.numpy as jnp
        import numpy as np
        key = jax.random.key(seed)
        k1, k2, k3, k4, k5 = jax.random.split(key, 5)
        d_in, d_out, r = (256, 256, 32)
        x = jax.random.normal(k1, (8, 2048, d_in), dtype=jnp.float32)
        W = jax.random.normal(k2, (d_out, d_in), dtype=jnp.float32) * (1.0 / np.sqrt(d_in))
        b = jax.random.normal(k3, (d_out,), dtype=jnp.float32) * 0.01
        V_r = jax.random.normal(k4, (d_in, r), dtype=jnp.float32) * (1.0 / np.sqrt(d_in))
        C = jax.random.normal(k5, (d_out, r), dtype=jnp.float32) * (1.0 / np.sqrt(r))
        return {'x': x, 'W': W, 'b': b, 'V_r': V_r, 'C': C}
    _L1_ffn_all = _L1_ffn_setup()
    _L1_ffn_in = {k: v for k, v in _L1_ffn_all.items() if k in ('W', 'b', 'V_r', 'C')}
    del _L1_ffn_all

    def _L2_xattn_setup():
        import jax, jax.numpy as jnp
        import numpy as np
        HEADS = 16
        DIM_HEAD = 64
        QUERY_DIM = 256
        CONTEXT_DIM = 192
        INNER = HEADS * DIM_HEAD
        SCALE = DIM_HEAD ** (-0.5)
        key = jax.random.key(seed)
        ks = jax.random.split(key, 7)
        B, Sq, Skv = (4, 512, 512)
        x = jax.random.normal(ks[0], (B, Sq, QUERY_DIM), dtype=jnp.float32)
        context = jax.random.normal(ks[1], (B, Skv, CONTEXT_DIM), dtype=jnp.float32)
        w_q = jax.random.normal(ks[2], (QUERY_DIM, INNER), dtype=jnp.float32) / np.sqrt(QUERY_DIM)
        w_k = jax.random.normal(ks[3], (CONTEXT_DIM, INNER), dtype=jnp.float32) / np.sqrt(CONTEXT_DIM)
        w_v = jax.random.normal(ks[4], (CONTEXT_DIM, INNER), dtype=jnp.float32) / np.sqrt(CONTEXT_DIM)
        w_o = jax.random.normal(ks[5], (INNER, QUERY_DIM), dtype=jnp.float32) / np.sqrt(INNER)
        b_o = jax.random.normal(ks[6], (QUERY_DIM,), dtype=jnp.float32) * 0.02
        return {'x': x, 'context': context, 'w_q': w_q, 'w_k': w_k, 'w_v': w_v, 'w_o': w_o, 'b_o': b_o}
    _L2_xattn_all = _L2_xattn_setup()
    _L2_xattn_in = {k: v for k, v in _L2_xattn_all.items() if k in ('w_q', 'w_k', 'w_v', 'w_o', 'b_o')}
    del _L2_xattn_all

    def _L2_attn_setup():
        import jax, jax.numpy as jnp
        import numpy as np
        DIM = 256
        H = 16
        D = DIM // H
        HID = H * D
        N, T = (2, 256)
        key = jax.random.key(seed)
        ks = jax.random.split(key, 6)
        x = jax.random.normal(ks[0], (N, T, DIM), dtype=jnp.float32)
        key_w = jax.random.normal(ks[1], (HID, DIM), dtype=jnp.float32) * DIM ** (-0.5)
        key_b = jax.random.uniform(ks[2], (HID,), minval=-4.0, maxval=4.0, dtype=jnp.float32)
        vq_w = jax.random.normal(ks[3], (2 * HID, DIM), dtype=jnp.float32) * DIM ** (-0.5)
        out_w = jax.random.normal(ks[4], (DIM, HID), dtype=jnp.float32) * HID ** (-0.5)
        out_b = jax.random.normal(ks[5], (DIM,), dtype=jnp.float32) * 0.02
        return {'x': x, 'key_w': key_w, 'key_b': key_b, 'vq_w': vq_w, 'out_w': out_w, 'out_b': out_b}
    _L2_attn_all = _L2_attn_setup()
    _L2_attn_in = {k: v for k, v in _L2_attn_all.items() if k in ('key_w', 'key_b', 'vq_w', 'out_w', 'out_b')}
    del _L2_attn_all

    def _L2_ffn_setup():
        import jax, jax.numpy as jnp
        import numpy as np
        D_MODEL = 256
        FF = 1024
        E = 8
        TOP_K = 2
        CAP_FACTOR = 1.25
        B, T = (4, 512)

        def _moe_forward(x, gate_w, gate_b, w1, b1, w2, b2):
            Bb, Tt, d = x.shape
            S = Bb * Tt
            C = int(CAP_FACTOR * S / E)
            xf = x.reshape(S, d)
            logits = xf @ gate_w + gate_b
            probs = jax.nn.softmax(logits, axis=1)
            topk_p, topk_i = jax.lax.top_k(probs, TOP_K)
            topk_pn = topk_p / jnp.sum(topk_p, axis=1, keepdims=True)
            rows = jnp.arange(S)
            w_te = jnp.zeros((S, E), xf.dtype).at[rows[:, None], topk_i].set(topk_pn)
            mask = jnp.zeros((S, E), bool).at[rows[:, None], topk_i].set(True)
            rank = jnp.cumsum(mask.astype(jnp.int32), axis=0)
            slot = jnp.where(mask & (rank <= C), rank - 1, C)
            e_grid = jnp.broadcast_to(jnp.arange(E), (S, E))
            t_grid = jnp.broadcast_to(rows[:, None], (S, E))
            buf = jnp.full((E, C + 1), S, jnp.int32).at[e_grid, slot].set(t_grid)
            idx = buf[:, :C]
            valid = idx < S
            x_pad = jnp.concatenate([xf, jnp.zeros((1, d), xf.dtype)], axis=0)
            xin = x_pad[idx]
            h = jax.nn.relu(jnp.einsum('ecd,edh->ech', xin, w1) + b1[:, None, :])
            out = jnp.einsum('ech,ehd->ecd', h, w2) + b2[:, None, :]
            w_pad = jnp.concatenate([w_te, jnp.zeros((1, E), xf.dtype)], axis=0)
            tok_w = w_pad[idx, jnp.arange(E)[:, None]]
            out = out * jnp.where(valid, tok_w, 0.0)[:, :, None]
            final = jnp.zeros((S + 1, d), xf.dtype).at[idx.reshape(-1)].add(out.reshape(-1, d))[:S]
            return final.reshape(Bb, Tt, d)
        key = jax.random.key(seed)
        ks = jax.random.split(key, 7)
        s = 0.02
        return {'x': jax.random.normal(ks[0], (B, T, D_MODEL), jnp.float32), 'gate_w': jax.random.normal(ks[1], (D_MODEL, E), jnp.float32) * s, 'gate_b': jnp.zeros((E,), jnp.float32), 'w1': jax.random.normal(ks[2], (E, D_MODEL, FF), jnp.float32) * s, 'b1': jnp.zeros((E, FF), jnp.float32), 'w2': jax.random.normal(ks[3], (E, FF, D_MODEL), jnp.float32) * s, 'b2': jnp.zeros((E, D_MODEL), jnp.float32)}
    _L2_ffn_all = _L2_ffn_setup()
    _L2_ffn_in = {k: v for k, v in _L2_ffn_all.items() if k in ('gate_w', 'gate_b', 'w1', 'b1', 'w2', 'b2')}
    del _L2_ffn_all

    def _L3_xattn_setup():
        import jax, jax.numpy as jnp
        import numpy as np
        EPS = 1e-05

        def layernorm(x, g, b):
            mu = jnp.mean(x, axis=-1, keepdims=True)
            var = jnp.mean(jnp.square(x - mu), axis=-1, keepdims=True)
            return (x - mu) * jax.lax.rsqrt(var + EPS) * g + b
        key = jax.random.key(seed)
        ks = jax.random.split(key, 12)
        B, L1, L2 = (8, 512, 512)
        D1, D2, E = (256, 192, 256)
        s1, s2, se = (D1 ** (-0.5), D2 ** (-0.5), E ** (-0.5))
        return {'modality1': jax.random.normal(ks[0], (B, L1, D1), jnp.float32), 'modality2': jax.random.normal(ks[1], (B, L2, D2), jnp.float32), 'ln1_g': jnp.ones((D1,), jnp.float32), 'ln1_b': jnp.zeros((D1,), jnp.float32), 'ln2_g': jnp.ones((D2,), jnp.float32), 'ln2_b': jnp.zeros((D2,), jnp.float32), 'Wq': jax.random.normal(ks[2], (D1, E), jnp.float32) * s1, 'bq': jax.random.normal(ks[3], (E,), jnp.float32) * 0.01, 'Wk': jax.random.normal(ks[4], (D2, E), jnp.float32) * s2, 'bk': jax.random.normal(ks[5], (E,), jnp.float32) * 0.01, 'Wv': jax.random.normal(ks[6], (D2, E), jnp.float32) * s2, 'bv': jax.random.normal(ks[7], (E,), jnp.float32) * 0.01, 'Wo': jax.random.normal(ks[8], (E, D1), jnp.float32) * se, 'bo': jax.random.normal(ks[9], (D1,), jnp.float32) * 0.01}
    _L3_xattn_all = _L3_xattn_setup()
    _L3_xattn_in = {k: v for k, v in _L3_xattn_all.items() if k in ('ln1_g', 'ln1_b', 'ln2_g', 'ln2_b', 'Wq', 'bq', 'Wk', 'bk', 'Wv', 'bv', 'Wo', 'bo')}
    del _L3_xattn_all

    def _L3_attn_setup():
        import jax, jax.numpy as jnp
        import numpy as np
        BASE_THETA = 0.5
        K_DOP = 0.2
        K_NOR = 0.15
        K_SERO = 0.1
        DIM = 256
        key = jax.random.key(seed)
        ks = jax.random.split(key, 9)
        scale = 1.0 / np.sqrt(DIM)
        x = jax.random.normal(ks[0], (2, 512, DIM), dtype=jnp.float32)
        Wq = jax.random.normal(ks[1], (DIM, DIM), dtype=jnp.float32) * scale
        bq = jnp.zeros((DIM,), dtype=jnp.float32)
        Wk = jax.random.normal(ks[2], (DIM, DIM), dtype=jnp.float32) * scale
        bk = jnp.zeros((DIM,), dtype=jnp.float32)
        Wv = jax.random.normal(ks[3], (DIM, DIM), dtype=jnp.float32) * scale
        bv = jnp.zeros((DIM,), dtype=jnp.float32)
        Wo = jax.random.normal(ks[4], (DIM, DIM), dtype=jnp.float32) * scale
        bo = jnp.zeros((DIM,), dtype=jnp.float32)
        return {'x': x, 'Wq': Wq, 'bq': bq, 'Wk': Wk, 'bk': bk, 'Wv': Wv, 'bv': bv, 'Wo': Wo, 'bo': bo}
    _L3_attn_all = _L3_attn_setup()
    _L3_attn_in = {k: v for k, v in _L3_attn_all.items() if k in ('Wq', 'bq', 'Wk', 'bk', 'Wv', 'bv', 'Wo', 'bo')}
    del _L3_attn_all

    def _L3_ffn_setup():
        import jax, jax.numpy as jnp
        import numpy as np
        B, T, D, H, E, K = (2, 512, 256, 1024, 8, 2)
        EPS = 1e-12

        def moe_forward(x, Wg, bg, W1, b1, W2, b2):
            gates = jax.nn.softmax(x @ Wg + bg, axis=-1)
            _, top_idx = jax.lax.top_k(gates, K)
            mask = jax.nn.one_hot(top_idx, E, dtype=gates.dtype).sum(axis=-2)
            g = gates * mask
            g = g / jnp.maximum(jnp.sum(jnp.abs(g), axis=-1, keepdims=True), EPS)
            h = jnp.einsum('btd,edh->bteh', x, W1) + b1[None, None]
            h = jax.nn.gelu(h, approximate=False)
            eo = jnp.einsum('bteh,ehd->bted', h, W2) + b2[None, None]
            return jnp.einsum('bte,bted->btd', g, eo)
        key = jax.random.key(seed)
        ks = jax.random.split(key, 8)
        s_d = 1.0 / np.sqrt(D)
        s_h = 1.0 / np.sqrt(H)
        return {'x': jax.random.normal(ks[0], (B, T, D), dtype=jnp.float32), 'Wg': jax.random.uniform(ks[1], (D, E), jnp.float32, -s_d, s_d), 'bg': jax.random.uniform(ks[2], (E,), jnp.float32, -s_d, s_d), 'W1': jax.random.uniform(ks[3], (E, D, H), jnp.float32, -s_d, s_d), 'b1': jax.random.uniform(ks[4], (E, H), jnp.float32, -s_d, s_d), 'W2': jax.random.uniform(ks[5], (E, H, D), jnp.float32, -s_h, s_h), 'b2': jax.random.uniform(ks[6], (E, D), jnp.float32, -s_h, s_h)}
    _L3_ffn_all = _L3_ffn_setup()
    _L3_ffn_in = {k: v for k, v in _L3_ffn_all.items() if k in ('Wg', 'bg', 'W1', 'b1', 'W2', 'b2')}
    del _L3_ffn_all
    return {'x': x, 'ctx_768': ctx_768, 'L0_xattn_Wq': _L0_xattn_in['Wq'], 'L0_xattn_Wk': _L0_xattn_in['Wk'], 'L0_xattn_Wv': _L0_xattn_in['Wv'], 'L0_xattn_Wo': _L0_xattn_in['Wo'], 'L0_xattn_bo': _L0_xattn_in['bo'], 'L0_attn_W_qkv': _L0_attn_in['W_qkv'], 'L0_attn_b_qkv': _L0_attn_in['b_qkv'], 'L0_attn_W_out': _L0_attn_in['W_out'], 'L0_attn_b_out': _L0_attn_in['b_out'], 'L0_attn_rel_bias': _L0_attn_in['rel_bias'], 'L0_ffn_w_gate': _L0_ffn_in['w_gate'], 'L0_ffn_w_up': _L0_ffn_in['w_up'], 'L0_ffn_w_down': _L0_ffn_in['w_down'], 'L1_xattn_Wq': _L1_xattn_in['Wq'], 'L1_xattn_bq': _L1_xattn_in['bq'], 'L1_xattn_Wk': _L1_xattn_in['Wk'], 'L1_xattn_bk': _L1_xattn_in['bk'], 'L1_xattn_Wv': _L1_xattn_in['Wv'], 'L1_xattn_bv': _L1_xattn_in['bv'], 'L1_xattn_Wo': _L1_xattn_in['Wo'], 'L1_xattn_bo': _L1_xattn_in['bo'], 'L1_attn_Wq': _L1_attn_in['Wq'], 'L1_attn_Wk': _L1_attn_in['Wk'], 'L1_attn_Wv': _L1_attn_in['Wv'], 'L1_attn_gamma': _L1_attn_in['gamma'], 'L1_ffn_W': _L1_ffn_in['W'], 'L1_ffn_b': _L1_ffn_in['b'], 'L1_ffn_V_r': _L1_ffn_in['V_r'], 'L1_ffn_C': _L1_ffn_in['C'], 'L2_xattn_w_q': _L2_xattn_in['w_q'], 'L2_xattn_w_k': _L2_xattn_in['w_k'], 'L2_xattn_w_v': _L2_xattn_in['w_v'], 'L2_xattn_w_o': _L2_xattn_in['w_o'], 'L2_xattn_b_o': _L2_xattn_in['b_o'], 'L2_attn_key_w': _L2_attn_in['key_w'], 'L2_attn_key_b': _L2_attn_in['key_b'], 'L2_attn_vq_w': _L2_attn_in['vq_w'], 'L2_attn_out_w': _L2_attn_in['out_w'], 'L2_attn_out_b': _L2_attn_in['out_b'], 'L2_ffn_gate_w': _L2_ffn_in['gate_w'], 'L2_ffn_gate_b': _L2_ffn_in['gate_b'], 'L2_ffn_w1': _L2_ffn_in['w1'], 'L2_ffn_b1': _L2_ffn_in['b1'], 'L2_ffn_w2': _L2_ffn_in['w2'], 'L2_ffn_b2': _L2_ffn_in['b2'], 'L3_xattn_ln1_g': _L3_xattn_in['ln1_g'], 'L3_xattn_ln1_b': _L3_xattn_in['ln1_b'], 'L3_xattn_ln2_g': _L3_xattn_in['ln2_g'], 'L3_xattn_ln2_b': _L3_xattn_in['ln2_b'], 'L3_xattn_Wq': _L3_xattn_in['Wq'], 'L3_xattn_bq': _L3_xattn_in['bq'], 'L3_xattn_Wk': _L3_xattn_in['Wk'], 'L3_xattn_bk': _L3_xattn_in['bk'], 'L3_xattn_Wv': _L3_xattn_in['Wv'], 'L3_xattn_bv': _L3_xattn_in['bv'], 'L3_xattn_Wo': _L3_xattn_in['Wo'], 'L3_xattn_bo': _L3_xattn_in['bo'], 'L3_attn_Wq': _L3_attn_in['Wq'], 'L3_attn_bq': _L3_attn_in['bq'], 'L3_attn_Wk': _L3_attn_in['Wk'], 'L3_attn_bk': _L3_attn_in['bk'], 'L3_attn_Wv': _L3_attn_in['Wv'], 'L3_attn_bv': _L3_attn_in['bv'], 'L3_attn_Wo': _L3_attn_in['Wo'], 'L3_attn_bo': _L3_attn_in['bo'], 'L3_ffn_Wg': _L3_ffn_in['Wg'], 'L3_ffn_bg': _L3_ffn_in['bg'], 'L3_ffn_W1': _L3_ffn_in['W1'], 'L3_ffn_b1': _L3_ffn_in['b1'], 'L3_ffn_W2': _L3_ffn_in['W2'], 'L3_ffn_b2': _L3_ffn_in['b2']}

def reference(x, ctx_768, L0_xattn_Wq, L0_xattn_Wk, L0_xattn_Wv, L0_xattn_Wo, L0_xattn_bo, L0_attn_W_qkv, L0_attn_b_qkv, L0_attn_W_out, L0_attn_b_out, L0_attn_rel_bias, L0_ffn_w_gate, L0_ffn_w_up, L0_ffn_w_down, L1_xattn_Wq, L1_xattn_bq, L1_xattn_Wk, L1_xattn_bk, L1_xattn_Wv, L1_xattn_bv, L1_xattn_Wo, L1_xattn_bo, L1_attn_Wq, L1_attn_Wk, L1_attn_Wv, L1_attn_gamma, L1_ffn_W, L1_ffn_b, L1_ffn_V_r, L1_ffn_C, L2_xattn_w_q, L2_xattn_w_k, L2_xattn_w_v, L2_xattn_w_o, L2_xattn_b_o, L2_attn_key_w, L2_attn_key_b, L2_attn_vq_w, L2_attn_out_w, L2_attn_out_b, L2_ffn_gate_w, L2_ffn_gate_b, L2_ffn_w1, L2_ffn_b1, L2_ffn_w2, L2_ffn_b2, L3_xattn_ln1_g, L3_xattn_ln1_b, L3_xattn_ln2_g, L3_xattn_ln2_b, L3_xattn_Wq, L3_xattn_bq, L3_xattn_Wk, L3_xattn_bk, L3_xattn_Wv, L3_xattn_bv, L3_xattn_Wo, L3_xattn_bo, L3_attn_Wq, L3_attn_bq, L3_attn_Wk, L3_attn_bk, L3_attn_Wv, L3_attn_bv, L3_attn_Wo, L3_attn_bo, L3_ffn_Wg, L3_ffn_bg, L3_ffn_W1, L3_ffn_b1, L3_ffn_W2, L3_ffn_b2):
    import jax
    import jax.numpy as jnp

    def _L0_xattn_ref(x, context, Wq, Wk, Wv, Wo, bo):
        import jax, jax.numpy as jnp
        import numpy as np
        HEADS = 16
        DIM_HEAD = 64
        SCALE = DIM_HEAD ** (-0.5)
        b, sq, _ = x.shape

        def split_heads(t):
            return t.reshape(b, -1, HEADS, DIM_HEAD).transpose(0, 2, 1, 3)
        q = split_heads(x @ Wq)
        k = split_heads(context @ Wk)
        v = split_heads(context @ Wv)
        sim = jnp.einsum('bhid,bhjd->bhij', q, k) * SCALE
        attn = jax.nn.softmax(sim, axis=-1)
        out = jnp.einsum('bhij,bhjd->bhid', attn, v)
        out = out.transpose(0, 2, 1, 3).reshape(b, sq, HEADS * DIM_HEAD)
        return out @ Wo + bo

    def _L0_attn_ref(x, W_qkv, b_qkv, W_out, b_out, rel_bias):
        import jax, jax.numpy as jnp
        import numpy as np
        D_MODEL = 256
        NHEAD = 16
        D_K = D_MODEL // NHEAD
        MAX_REL = 256
        B, S, D = x.shape
        qkv = x @ W_qkv + b_qkv
        qkv = qkv.reshape(B, S, 3, NHEAD, D_K)
        q, k, v = (qkv[:, :, 0], qkv[:, :, 1], qkv[:, :, 2])
        scores = jnp.einsum('bihd,bjhd->bhij', q, k) / jnp.sqrt(jnp.float32(D_K))
        idxs = jnp.arange(S)
        rel = jnp.clip(idxs[:, None] - idxs[None, :] + MAX_REL, 0, 2 * MAX_REL)
        bias = rel_bias[rel]
        scores = scores + jnp.transpose(bias, (2, 0, 1))[None]
        attn = jax.nn.softmax(scores, axis=-1)
        out = jnp.einsum('bhij,bjhd->bihd', attn, v).reshape(B, S, D)
        return out @ W_out + b_out

    def _L0_ffn_ref(x, w_gate, w_up, w_down):
        import jax, jax.numpy as jnp
        import numpy as np
        BLOCK = 16
        _GRID = jnp.array([0.0, 0.5, 1.0, 1.5, 2.0, 3.0, 4.0, 6.0], dtype=jnp.float32)
        _MID = jnp.array([0.25, 0.75, 1.25, 1.75, 2.5, 3.5, 5.0], dtype=jnp.float32)

        def fp4_quant_dequant(x):
            shape = x.shape
            xb = x.reshape(shape[:-1] + (shape[-1] // BLOCK, BLOCK))
            scale = jnp.max(jnp.abs(xb), axis=-1, keepdims=True) / 6.0
            scale = jnp.maximum(scale, jnp.float32(1e-12))
            xn = xb / scale
            idx = jnp.searchsorted(_MID, jnp.abs(xn))
            q = _GRID[idx] * jnp.sign(xn) * scale
            return q.reshape(shape)

        def fp4_linear(x, w):
            xq = fp4_quant_dequant(x)
            wq = fp4_quant_dequant(w)
            return jnp.einsum('bsk,nk->bsn', xq, wq)
        gate = fp4_linear(x, w_gate)
        y = fp4_linear(x, w_up)
        h = jax.nn.silu(gate) * y
        return fp4_linear(h, w_down)

    def _L1_xattn_ref(query, key_value, Wq, bq, Wk, bk, Wv, bv, Wo, bo):
        import jax, jax.numpy as jnp
        import numpy as np
        NUM_HEADS = 16
        CLAMP = 10000.0
        B, Nq, Cq = query.shape
        Nkv = key_value.shape[1]
        H = NUM_HEADS
        D = Cq // H
        scale = D ** (-0.5)
        q = (query @ Wq + bq).reshape(B, Nq, H, D).transpose(0, 2, 1, 3)
        k = (key_value @ Wk + bk).reshape(B, Nkv, H, D).transpose(0, 2, 1, 3)
        v = (key_value @ Wv + bv).reshape(B, Nkv, H, D).transpose(0, 2, 1, 3)
        attn = jnp.einsum('bhqd,bhkd->bhqk', q, k) * scale
        attn = jnp.clip(attn, -CLAMP, CLAMP)
        attn = jax.nn.softmax(attn, axis=-1)
        attn = jnp.where(jnp.any(jnp.isnan(attn)), jnp.asarray(1.0 / Nkv, attn.dtype), attn)
        x = jnp.einsum('bhqk,bhkd->bqhd', attn, v).reshape(B, Nq, Cq)
        return x @ Wo + bo

    def _L1_attn_ref(x, Wq, Wk, Wv, gamma):
        import jax, jax.numpy as jnp
        import numpy as np
        B, S, C = (32, 256, 256)
        f = jnp.einsum('bsc,dc->bsd', x, Wq)
        g = jnp.einsum('bsc,dc->bsd', x, Wk)
        h = jnp.einsum('bsc,dc->bsd', x, Wv)
        scores = jnp.einsum('bsd,btd->bst', f, g)
        beta = jax.nn.softmax(scores, axis=1)
        o = gamma[0] * jnp.einsum('bsc,bst->btc', h, beta) + x
        return o

    def _L1_ffn_ref(x, W, b, V_r, C):
        import jax, jax.numpy as jnp
        import numpy as np
        base = jnp.einsum('bsd,od->bso', x, W) + b
        correction = jnp.einsum('bsr,or->bso', jnp.einsum('bsd,dr->bsr', x, V_r), C)
        return base + correction

    def _L2_xattn_ref(x, context, w_q, w_k, w_v, w_o, b_o):
        import jax, jax.numpy as jnp
        import numpy as np
        HEADS = 16
        DIM_HEAD = 64
        QUERY_DIM = 256
        CONTEXT_DIM = 192
        INNER = HEADS * DIM_HEAD
        SCALE = DIM_HEAD ** (-0.5)
        B, Sq, _ = x.shape
        Skv = context.shape[1]
        q = (x @ w_q).reshape(B, Sq, HEADS, DIM_HEAD).transpose(0, 2, 1, 3)
        k = (context @ w_k).reshape(B, Skv, HEADS, DIM_HEAD).transpose(0, 2, 1, 3)
        v = (context @ w_v).reshape(B, Skv, HEADS, DIM_HEAD).transpose(0, 2, 1, 3)
        sim = jnp.einsum('bhid,bhjd->bhij', q, k) * SCALE
        attn = jax.nn.softmax(sim, axis=-1)
        out = jnp.einsum('bhij,bhjd->bhid', attn, v)
        out = out.transpose(0, 2, 1, 3).reshape(B, Sq, INNER)
        return out @ w_o + b_o

    def _L2_attn_ref(x, key_w, key_b, vq_w, out_w, out_b):
        import jax, jax.numpy as jnp
        import numpy as np
        DIM = 256
        H = 16
        D = DIM // H
        HID = H * D
        N, T = (2, 256)
        n, t, dim = x.shape
        vq = x @ vq_w.T
        v, q = jnp.split(vq, 2, axis=-1)
        k = jax.nn.sigmoid(x @ key_w.T + key_b)
        k = k.reshape(n, t, H, D)
        v = v.reshape(n, t, H, D)
        upd = (1.0 - k)[..., :, None] * v[..., None, :]
        decay = k[..., :, None]

        def combine(c1, c2):
            a1, b1 = c1
            a2, b2 = c2
            return (a1 * a2, b1 * a2 + b2)
        _, kv = jax.lax.associative_scan(combine, (decay, upd), axis=1)
        qh = q.reshape(n, t, H, D)
        h = jnp.einsum('nthd,nthde->nthe', qh, kv).reshape(n, t, HID)
        return h @ out_w.T + out_b

    def _L2_ffn_ref(x, gate_w, gate_b, w1, b1, w2, b2):
        import jax, jax.numpy as jnp
        import numpy as np
        D_MODEL = 256
        FF = 1024
        E = 8
        TOP_K = 2
        CAP_FACTOR = 1.25
        B, T = (4, 512)

        def _moe_forward(x, gate_w, gate_b, w1, b1, w2, b2):
            Bb, Tt, d = x.shape
            S = Bb * Tt
            C = int(CAP_FACTOR * S / E)
            xf = x.reshape(S, d)
            logits = xf @ gate_w + gate_b
            probs = jax.nn.softmax(logits, axis=1)
            topk_p, topk_i = jax.lax.top_k(probs, TOP_K)
            topk_pn = topk_p / jnp.sum(topk_p, axis=1, keepdims=True)
            rows = jnp.arange(S)
            w_te = jnp.zeros((S, E), xf.dtype).at[rows[:, None], topk_i].set(topk_pn)
            mask = jnp.zeros((S, E), bool).at[rows[:, None], topk_i].set(True)
            rank = jnp.cumsum(mask.astype(jnp.int32), axis=0)
            slot = jnp.where(mask & (rank <= C), rank - 1, C)
            e_grid = jnp.broadcast_to(jnp.arange(E), (S, E))
            t_grid = jnp.broadcast_to(rows[:, None], (S, E))
            buf = jnp.full((E, C + 1), S, jnp.int32).at[e_grid, slot].set(t_grid)
            idx = buf[:, :C]
            valid = idx < S
            x_pad = jnp.concatenate([xf, jnp.zeros((1, d), xf.dtype)], axis=0)
            xin = x_pad[idx]
            h = jax.nn.relu(jnp.einsum('ecd,edh->ech', xin, w1) + b1[:, None, :])
            out = jnp.einsum('ech,ehd->ecd', h, w2) + b2[:, None, :]
            w_pad = jnp.concatenate([w_te, jnp.zeros((1, E), xf.dtype)], axis=0)
            tok_w = w_pad[idx, jnp.arange(E)[:, None]]
            out = out * jnp.where(valid, tok_w, 0.0)[:, :, None]
            final = jnp.zeros((S + 1, d), xf.dtype).at[idx.reshape(-1)].add(out.reshape(-1, d))[:S]
            return final.reshape(Bb, Tt, d)
        return _moe_forward(x, gate_w, gate_b, w1, b1, w2, b2)

    def _L3_xattn_ref(modality1, modality2, ln1_g, ln1_b, ln2_g, ln2_b, Wq, bq, Wk, bk, Wv, bv, Wo, bo):
        import jax, jax.numpy as jnp
        import numpy as np
        EPS = 1e-05

        def layernorm(x, g, b):
            mu = jnp.mean(x, axis=-1, keepdims=True)
            var = jnp.mean(jnp.square(x - mu), axis=-1, keepdims=True)
            return (x - mu) * jax.lax.rsqrt(var + EPS) * g + b
        E = Wq.shape[1]
        scaling = E ** (-0.5)
        x1 = layernorm(modality1, ln1_g, ln1_b)
        x2 = layernorm(modality2, ln2_g, ln2_b)
        q = x1 @ Wq + bq
        k = x2 @ Wk + bk
        v = x2 @ Wv + bv
        scores = jnp.einsum('bqe,bke->bqk', q, k) * scaling
        attn = jax.nn.softmax(scores, axis=-1)
        ctx = jnp.einsum('bqk,bke->bqe', attn, v)
        return ctx @ Wo + bo

    def _L3_attn_ref(x, Wq, bq, Wk, bk, Wv, bv, Wo, bo):
        import jax, jax.numpy as jnp
        import numpy as np
        BASE_THETA = 0.5
        K_DOP = 0.2
        K_NOR = 0.15
        K_SERO = 0.1
        DIM = 256
        q = jnp.einsum('bsd,ed->bse', x, Wq) + bq
        k = jnp.einsum('bsd,ed->bse', x, Wk) + bk
        v = jnp.einsum('bsd,ed->bse', x, Wv) + bv
        qk = jnp.einsum('bsd,btd->bst', q, k)
        theta = BASE_THETA + K_DOP * jax.nn.sigmoid(qk) + K_NOR * jnp.tanh(qk) + K_SERO * jax.nn.relu(qk)
        attn = jax.nn.softmax(theta, axis=-1)
        out = jnp.einsum('bst,btd->bsd', attn, v)
        return jnp.einsum('bsd,ed->bse', out, Wo) + bo

    def _L3_ffn_ref(x, Wg, bg, W1, b1, W2, b2):
        import jax, jax.numpy as jnp
        import numpy as np
        B, T, D, H, E, K = (2, 512, 256, 1024, 8, 2)
        EPS = 1e-12

        def moe_forward(x, Wg, bg, W1, b1, W2, b2):
            gates = jax.nn.softmax(x @ Wg + bg, axis=-1)
            _, top_idx = jax.lax.top_k(gates, K)
            mask = jax.nn.one_hot(top_idx, E, dtype=gates.dtype).sum(axis=-2)
            g = gates * mask
            g = g / jnp.maximum(jnp.sum(jnp.abs(g), axis=-1, keepdims=True), EPS)
            h = jnp.einsum('btd,edh->bteh', x, W1) + b1[None, None]
            h = jax.nn.gelu(h, approximate=False)
            eo = jnp.einsum('bteh,ehd->bted', h, W2) + b2[None, None]
            return jnp.einsum('bte,bted->btd', g, eo)
        return moe_forward(x, Wg, bg, W1, b1, W2, b2)
    x = x + _L0_xattn_ref(_layernorm(x, axis=-1), ctx_768, L0_xattn_Wq, L0_xattn_Wk, L0_xattn_Wv, L0_xattn_Wo, L0_xattn_bo)
    x = x + _L0_attn_ref(_layernorm(x, axis=-1), L0_attn_W_qkv, L0_attn_b_qkv, L0_attn_W_out, L0_attn_b_out, L0_attn_rel_bias)
    x = x + _L0_ffn_ref(_layernorm(x, axis=-1), L0_ffn_w_gate, L0_ffn_w_up, L0_ffn_w_down)
    x = x + _L1_xattn_ref(_layernorm(x, axis=-1), ctx_768, L1_xattn_Wq, L1_xattn_bq, L1_xattn_Wk, L1_xattn_bk, L1_xattn_Wv, L1_xattn_bv, L1_xattn_Wo, L1_xattn_bo)
    x = x + _L1_attn_ref(_layernorm(x, axis=-1), L1_attn_Wq, L1_attn_Wk, L1_attn_Wv, L1_attn_gamma)
    x = x + _L1_ffn_ref(_layernorm(x, axis=-1), L1_ffn_W, L1_ffn_b, L1_ffn_V_r, L1_ffn_C)
    x = x + _L2_xattn_ref(_layernorm(x, axis=-1), ctx_768, L2_xattn_w_q, L2_xattn_w_k, L2_xattn_w_v, L2_xattn_w_o, L2_xattn_b_o)
    x = x + _L2_attn_ref(_layernorm(x, axis=-1), L2_attn_key_w, L2_attn_key_b, L2_attn_vq_w, L2_attn_out_w, L2_attn_out_b)
    x = x + _L2_ffn_ref(_layernorm(x, axis=-1), L2_ffn_gate_w, L2_ffn_gate_b, L2_ffn_w1, L2_ffn_b1, L2_ffn_w2, L2_ffn_b2)
    x = x + _L3_xattn_ref(_layernorm(x, axis=-1), ctx_768, L3_xattn_ln1_g, L3_xattn_ln1_b, L3_xattn_ln2_g, L3_xattn_ln2_b, L3_xattn_Wq, L3_xattn_bq, L3_xattn_Wk, L3_xattn_bk, L3_xattn_Wv, L3_xattn_bv, L3_xattn_Wo, L3_xattn_bo)
    x = x + _L3_attn_ref(_layernorm(x, axis=-1), L3_attn_Wq, L3_attn_bq, L3_attn_Wk, L3_attn_bk, L3_attn_Wv, L3_attn_bv, L3_attn_Wo, L3_attn_bo)
    x = x + _L3_ffn_ref(_layernorm(x, axis=-1), L3_ffn_Wg, L3_ffn_bg, L3_ffn_W1, L3_ffn_b1, L3_ffn_W2, L3_ffn_b2)
    return x

_drawn_inputs = setup_inputs


def setup_inputs(seed=0):
    import zlib

    import numpy as np

    out = dict(_drawn_inputs(seed))
    spreads = {'L0_xattn_bo': (0.0, 0.1),
     'L0_attn_b_qkv': (0.0, 0.1),
     'L0_attn_b_out': (0.0, 0.1),
     'L1_xattn_bq': (0.0, 0.4),
     'L1_xattn_bk': (0.0, 2.0),
     'L1_xattn_bv': (0.0, 0.1),
     'L1_xattn_bo': (0.0, 0.1),
     'L2_ffn_gate_b': (0.0, 0.418),
     'L2_ffn_b1': (0.0, 0.8),
     'L2_ffn_b2': (0.0, 0.619),
     'L3_xattn_ln1_g': (1.0, 0.6),
     'L3_xattn_ln1_b': (0.0, 0.8),
     'L3_xattn_ln2_g': (1.0, 0.572),
     'L3_xattn_ln2_b': (0.0, 0.294),
     'L3_attn_bq': (0.0, 0.8),
     'L3_attn_bk': (0.0, 2.0),
     'L3_attn_bv': (0.0, 0.381),
     'L3_attn_bo': (0.0, 0.364)}
    factors = {'L0_attn_rel_bias': 8.0,
     'L1_ffn_b': 8.0,
     'L2_xattn_b_o': 5.741,
     'L2_attn_out_b': 8.0,
     'L2_ffn_gate_w': 2.88,
     'L2_ffn_w1': 3.756,
     'L2_ffn_w2': 3.035,
     'L3_xattn_bq': 64.0,
     'L3_xattn_bk': 64.0,
     'L3_xattn_bv': 25.333,
     'L3_xattn_bo': 23.763,
     'L3_ffn_bg': 8.0,
     'L3_ffn_b1': 27.665,
     'L3_ffn_b2': 8.0}
    for name, (base, spread) in spreads.items():
        noise = np.random.default_rng([zlib.crc32(name.encode()), seed]).standard_normal(out[name].shape)
        drawn = base * np.exp(spread * noise) if base else spread * noise
        out[name] = jnp.asarray(drawn.astype(out[name].dtype))
    for name, factor in factors.items():
        out[name] = (out[name] * factor).astype(out[name].dtype)
    return out
```

```python
from contextlib import ExitStack

import numpy as np
import concourse.bass as bass
from concourse import mybir

ALU = mybir.AluOpType
ACT = mybir.ActivationFunctionType
F32 = mybir.dt.float32
U32 = mybir.dt.uint32
BF16 = mybir.dt.bfloat16
AX = mybir.AxisListType

P = 128
BATCH, SEQ, D = 32, 32, 256
TOKENS = BATCH * SEQ
TILES = TOKENS // P
PER_TILE = P // SEQ
CD = D // P
HALF = 512
EPS = 1e-5
STAGES = list(range(12))


class Core:

    def __init__(self, nc, ctx, dram):
        self.nc, self.dram = nc, dram
        self.x = ctx.enter_context(nc.sbuf_tensor("x", [P, TILES, D], F32))
        self.xn = ctx.enter_context(nc.sbuf_tensor("xn", [P, TILES, D], F32))
        self.xnT = ctx.enter_context(nc.sbuf_tensor("xnT", [P, CD, TOKENS], F32))
        self.ident = ctx.enter_context(nc.sbuf_tensor("ident", [P, P], F32))
        self.ones = ctx.enter_context(nc.sbuf_tensor("ones", [1, HALF], F32))
        self.neghalf = ctx.enter_context(nc.sbuf_tensor("neghalf", [P, TILES], F32))
        self.bank = [ctx.enter_context(nc.psum_tensor(f"bank{i}", [P, 512], F32)) for i in range(8)]


class Stage:

    def __init__(self, core, ctx, name):
        self.core, self.ctx, self.name, self.sems = core, ctx, name, []
        ctx.callback(self.end)

    def end(self):
        self.core.nc.clear_and_free_semaphores(self.sems)
        self.core.nc.all_engine_barrier()

    def sb(self, name, shape, dt=F32):
        return self.ctx.enter_context(self.core.nc.sbuf_tensor(f"{self.name}_{name}", shape, dt))

    def sem(self, name):
        self.sems.append(self.core.nc.alloc_semaphore(f"{self.name}_{name}"))
        return self.sems[-1]


class Chain:

    def __init__(self, eng, sem, start=0):
        self.eng, self.sem, self.n, self.start = eng, sem, 0, start

    def __call__(self, instruction):
        self.n += 1
        instruction.then_inc(self.sem, 1)
        self.eng.wait_ge(self.sem, self.start + self.n)


class Norm:
    def __init__(self, st, twice=False):
        self.core, self.twice = st.core, twice
        self.stats = st.sb("ln_stats", [P, TILES, 6])
        self.mv = st.sb("ln_mv", [P, TILES, 2])
        self.veps = st.sb("ln_veps", [P, TILES])
        self.rstd = st.sb("ln_rstd", [P, TILES])
        self.stats_done = st.sem("ln_stats_done")
        self.mv_ready = st.sem("ln_mv_ready")
        self.veps_done = st.sem("ln_veps_done")
        self.rstd_ready = st.sem("ln_rstd_ready")
        self.xn_ready = st.sem("ln_xn_ready")
        self.turned = st.sem("ln_turned")
        self.xnT_ready = st.sem("ln_xnT_ready")

    def dve(self, dve):
        nc, xn = self.core.nc, self.core.xn
        for n in range(2 if self.twice else 1):
            x = xn if n else self.core.x
            for t in range(TILES):
                if n:
                    dve.wait_ge(self.xn_ready, t + 1)
                nc.vector.bn_stats(self.stats[:, t, :], x[:, t, :]).then_inc(self.stats_done, 1)
            if n:
                dve.wait_ge(self.xn_ready, TILES)
            for t in range(TILES):
                dve.wait_ge(self.stats_done, n * TILES + t + 1)
                nc.vector.bn_aggr(self.mv[:, t, :], self.stats[:, t, :]).then_inc(self.mv_ready, 1)
            dve.wait_ge(self.rstd_ready, n + 1)
            for t in range(TILES):
                nc.vector.tensor_scalar(xn[:, t, :], x[:, t, :], self.mv[:, t, 0:1], self.rstd[:, t:t + 1],
                                        ALU.subtract, ALU.mult).then_inc(self.xn_ready, 1)

    def pool(self, pool):
        nc = self.core.nc
        for n in range(2 if self.twice else 1):
            pool.wait_ge(self.mv_ready, (n + 1) * TILES)
            if n:
                pool.wait_ge(self.xn_ready, TILES)
            nc.gpsimd.tensor_scalar(self.veps[:, :], self.mv[:, :, 1], EPS, None, ALU.add).then_inc(self.veps_done, 1)
            pool.wait_ge(self.veps_done, n + 1)
            nc.gpsimd.tensor_tensor(self.rstd[:, :], self.veps[:, :], self.core.neghalf[:, :],
                                    ALU.pow).then_inc(self.rstd_ready, 1)

    def pe(self, pe):
        core = self.core
        for t in range(TILES):
            pe.wait_ge(self.xn_ready, (TILES if self.twice else 0) + t + 1)
            for c in range(CD):
                last = core.nc.tensor.transpose(core.bank[2 * (t // 4) + c][:, (t % 4) * P:(t % 4 + 1) * P],
                                                core.xn[:, t, c * P:(c + 1) * P], core.ident[:, :])
            if t % 4 == 3:
                last.then_inc(self.turned, 1)

    def act(self, act):
        core = self.core
        for g in range(TILES // 4):
            act.wait_ge(self.turned, g + 1)
            for c in range(CD):
                core.nc.scalar.copy(core.xnT[:, c, g * HALF:(g + 1) * HALF],
                                    core.bank[2 * g + c][:, :]).then_inc(self.xnT_ready, 1)


def stage_low_rank(core):
    nc, d = core.nc, core.dram
    with ExitStack() as ctx:
        st = Stage(core, ctx, "lowrank")
        ln = Norm(st)
        R = d["L1_ffn_V_r"].shape[1]
        wT = st.sb("wT", [P, CD, D])
        v = st.sb("v", [P, CD, R])
        cT = st.sb("cT", [R, D])
        b = st.sb("b", [1, D])
        xvT = st.sb("xvT", [R, TOKENS])
        loaded = st.sem("loaded")
        xv_done = st.sem("xv_done")
        xv_ready = st.sem("xv_ready")
        y_done = st.sem("y_done")
        x_done = st.sem("x_done")
        block = ctx.enter_context(nc.Block())

        @block.sync
        def _(sp):
            sp.dma_start(wT[:, :, :], d["L1_ffn_W_T"].rearrange("(c p) n -> p c n", p=P)).then_inc(loaded, 16)
            sp.dma_start(v[:, :, :], d["L1_ffn_V_r"].rearrange("(c p) n -> p c n", p=P)).then_inc(loaded, 16)
            sp.dma_start(cT[:, :], d["L1_ffn_C_T"]).then_inc(loaded, 16)
            sp.dma_start(b[:, :], d["L1_ffn_b"].rearrange("(a n) -> a n", a=1)).then_inc(loaded, 16)

        @block.gpsimd
        def _(pool):
            ln.pool(pool)

        @block.tensor
        def _(pe):
            ln.pe(pe)
            pe.wait_ge(loaded, 64)
            for n in range(2):
                pe.wait_ge(ln.xnT_ready, CD * (n + 1))
                for c in range(CD):
                    mm = nc.tensor.matmul(core.bank[4 + n][0:R, :], v[:, c, :],
                                          core.xnT[:, c, n * HALF:(n + 1) * HALF], start=(c == 0), stop=(c == CD - 1))
                mm.then_inc(xv_done, 1)
            for t in range(TILES):
                if t % 4 == 0:
                    pe.wait_ge(xv_ready, t // 4 + 1)
                if t >= 4:
                    pe.wait_ge(x_done, t - 3)
                y = core.bank[t % 4][:, 0:D]
                tok = slice(t * P, (t + 1) * P)
                for c in range(CD):
                    nc.tensor.matmul(y, core.xnT[:, c, tok], wT[:, c, :], start=(c == 0), stop=False)
                nc.tensor.matmul(y, xvT[:, tok], cT[:, :], start=False, stop=False)
                nc.tensor.matmul(y, core.ones[:, 0:P], b[:, :], start=False, stop=True).then_inc(y_done, 1)

        @block.scalar
        def _(act):
            ln.act(act)
            for n in range(2):
                act.wait_ge(xv_done, n + 1)
                nc.scalar.copy(xvT[:, n * HALF:(n + 1) * HALF], core.bank[4 + n][0:R, :]).then_inc(xv_ready, 1)

        @block.vector
        def _(dve):
            ln.dve(dve)
            for t in range(TILES):
                dve.wait_ge(y_done, t + 1)
                nc.vector.tensor_tensor(core.x[:, t, :], core.x[:, t, :], core.bank[t % 4][:, 0:D],
                                        ALU.add).then_inc(x_done, 1)


def stage_cross_attention(core, name, wq, wk, wv, wo, bo, biases, head_dim, clamp):
    nc, d = core.nc, core.dram
    HEADS, GROUP = 16, 4
    KV, CTX = d["ctx_768"].shape[1:]
    C1, C2 = P, CTX - P
    AUG = CTX + 1
    K2 = AUG - C1
    INNER = HEADS * head_dim
    QCH = INNER // P
    HPC = HEADS // QCH
    QM = QCH // 2
    SCALE = head_dim ** -0.5
    whole = head_dim % 32 == 0
    GROUPS = HEADS // GROUP
    UNITS = PER_TILE * GROUPS
    RING = 4
    WEIGHTS = 16 * (8 if biases else 6)
    M_FILLS, OUT_FILLS = 1 + GROUPS, 3
    TURN, PV, SCALE_O, TURN_O = 1, 2, 3, 4
    Q_STEP, V_STEP, WO_STEP = 0, 4, 12
    with ExitStack() as ctx:
        st = Stage(core, ctx, name)
        ln = Norm(st)
        wq_s = st.sb("wq", [P, CD, INNER])
        wo_s = st.sb("wo", [P, QCH, D])
        bo_s = st.sb("bo", [1, D])
        if whole:
            wk_s = st.sb("wk", [P, QCH, AUG])
            wv1 = st.sb("wv1", [P, INNER])
            wv2 = st.sb("wv2", [C2, INNER])
        else:
            wk_s = st.sb("wk", [P, HEADS, AUG])
            wv1 = st.sb("wv1", [P, HEADS, P])
            wv2 = st.sb("wv2", [C2, HEADS, P])
        if biases:
            bq_s = st.sb("bq", [1, INNER])
            bv_s = st.sb("bv", [P, QCH])
        ctxT1 = st.sb("ctxT1", [P, PER_TILE, KV])
        ctxT2 = st.sb("ctxT2", [K2, PER_TILE, KV])
        ctxN = st.sb("ctxN", [P, PER_TILE, 2, AUG])
        ctx_last = st.sb("ctx_last", [P, PER_TILE, AUG])
        qT = st.sb("qT", [P, QCH, P])
        qk1 = st.sb("qk1", [P, 2, PER_TILE, HEADS, SEQ])
        qk2 = st.sb("qk2", [K2, 2, PER_TILE, HEADS, SEQ])
        negmax = st.sb("negmax", [P, RING])
        clamped = st.sb("clamped", [P, 2, KV]) if clamp else None
        probs = st.sb("probs", [P, RING, KV])
        probsT = st.sb("probsT", [P, RING, 2 * P])
        o_sum = st.sb("o_sum", [P, RING, AUG])
        rsum = st.sb("rsum", [P, RING])
        o_norm = st.sb("o_norm", [P, RING, CTX])
        oT1 = st.sb("oT1", [P, 2, HEADS, PER_TILE, SEQ])
        oT2 = st.sb("oT2", [C2, 2, HEADS, PER_TILE, SEQ])
        aT = st.sb("aT", [P, QCH, P])

        weights_loaded = st.sem("weights_loaded")
        ctx_loaded = [st.sem(f"ctx_loaded{b}") for b in range(PER_TILE)]
        m0_filled, m0_free = st.sem("m0_filled"), st.sem("m0_free")
        m1_filled, m1_free = st.sem("m1_filled"), st.sem("m1_free")
        m2_filled, m2_free = st.sem("m2_filled"), st.sem("m2_free")
        scores_done = st.sem("scores_done")
        negmax_ready = st.sem("negmax_ready")
        clamp_done = st.sem("clamp_done")
        probs_ready = st.sem("probs_ready")
        turned = st.sem("turned")
        probsT_ready = st.sem("probsT_ready")
        pv_done = st.sem("pv_done")
        o_summed = st.sem("o_summed")
        rsum_ready = st.sem("rsum_ready")
        o_scaled = st.sem("o_scaled")
        o_turned = st.sem("o_turned")
        oT_ready = st.sem("oT_ready")
        banks = [b[:, :] for b in core.bank]
        SB, TB, OB, OT, M0, M1, M2 = banks[0:2], *banks[2:8]
        block = ctx.enter_context(nc.Block())

        def every_tile(eng, body):
            body(0, 0)
            with eng.Fori(0, TILES // 2 - 1) as i:
                for k in (1, 2):
                    body(i * 2 + k, k % 2)
            body(TILES - 1, 1)
            body(TILES, 0)

        def known(j, n):
            return isinstance(j, int) and j == n

        def wk_of(h, part):
            f = [slice(0, C1), slice(C1, AUG)][part]
            if whole:
                r = slice((h % HPC) * head_dim, (h % HPC + 1) * head_dim)
                return wk_s[r, h // HPC, f], qT[r, h // HPC, :]
            return wk_s[:, h, f], qT[:, h // HPC, :]

        def heads_of(g):
            return range(g // 2 * 8, g // 2 * 8 + 8)

        def qk_of(z, g, odd):
            return [qk1, qk2][g % 2][:, z, :, g // 2 * 8 + odd:g // 2 * 8 + 8:2, :]

        def steps_of(s, j):
            def at(lag):
                u = s - lag
                if u >= 0:
                    return None if known(j, TILES) else (j, u)
                return None if known(j, 0) else (j - 1, u + UNITS)
            return at

        @block.sync
        def _(sp):
            def load(i, b):
                n = bass.ds(i * PER_TILE + b, 1)
                T = d["ctxT"][n].rearrange("a c k -> c (a k)")
                rows = d["ctxA"][n]
                sp.dma_start(ctxT1[:, b, :], T[0:C1, :]).then_inc(ctx_loaded[b], 16)
                sp.dma_start(ctxT2[:, b, :], T[C1:C1 + K2, :]).then_inc(ctx_loaded[b], 16)
                sp.dma_start(ctxN[:, b, :, :], rows[:, 0:2 * P, :].rearrange("a (c p) f -> p (a c) f", p=P)).then_inc(ctx_loaded[b], 16)
                sp.dma_start(ctx_last[:, b, :], rows[:, 2 * P, :].rearrange("a f -> (a f)").partition_broadcast(P)).then_inc(ctx_loaded[b], 16)

            sp.dma_start(wq_s[:, :, :], wq.rearrange("(c p) n -> p c n", p=P)).then_inc(weights_loaded, 16)
            if whole:
                sp.dma_start(wk_s[:, :, :], wk.rearrange("(c p) f -> p c f", p=P)).then_inc(weights_loaded, 16)
                sp.dma_start(wv1[:, :], wv[0:C1, :]).then_inc(weights_loaded, 16)
                sp.dma_start(wv2[:, :], wv[C1:CTX, :]).then_inc(weights_loaded, 16)
            else:
                sp.dma_start(wk_s[:, :, :], wk.rearrange("h p f -> p h f")).then_inc(weights_loaded, 16)
                sp.dma_start(wv1[:, :, :], wv[0:C1]).then_inc(weights_loaded, 16)
                sp.dma_start(wv2[:, :, :], wv[C1:CTX]).then_inc(weights_loaded, 16)
            for b in range(PER_TILE):
                load(0, b)
            sp.dma_start(wo_s[:, :, :], wo.rearrange("(c p) n -> p c n", p=P)).then_inc(weights_loaded, 16)
            sp.dma_start(bo_s[:, :], bo.rearrange("(a n) -> a n", a=1)).then_inc(weights_loaded, 16)
            if biases:
                sp.dma_start(bq_s[:, :], biases[0].rearrange("(a n) -> a n", a=1)).then_inc(weights_loaded, 16)
                sp.dma_start(bv_s[:, :], biases[1]).then_inc(weights_loaded, 16)
            with sp.Fori(1, TILES) as i:
                for b in range(PER_TILE):
                    sp.wait_ge(o_summed, (i - 1) * UNITS + GROUPS * (b + 1) + RING)
                    load(i, b)

        @block.gpsimd
        def _(pool):
            ln.pool(pool)

        @block.tensor
        def _(pe):
            ln.pe(pe)
            pe.wait_ge(weights_loaded, WEIGHTS)
            pe.wait_ge(ln.xnT_ready, 2 * CD)

            def queries(j, m, chunks):
                bank, filled, free = [(M0, m0_filled, m0_free), (M1, m1_filled, m1_free)][m]
                for k in chunks:
                    ch = m * QM + k
                    if k == 0:
                        pe.wait_ge(free, j * M_FILLS + 1)
                    for c in range(CD):
                        mm = nc.tensor.matmul(bank[:, k * P:(k + 1) * P], wq_s[:, c, ch * P:(ch + 1) * P],
                                              core.xnT[:, c, bass.ds(j * P, P)], start=(c == 0), stop=(c == CD - 1 and not biases))
                    if biases:
                        mm = nc.tensor.matmul(bank[:, k * P:(k + 1) * P], bq_s[:, ch * P:(ch + 1) * P],
                                              core.ones[:, 0:P], start=False, stop=True)
                    if k == QM - 1:
                        mm.then_inc(filled, 1)

            def to_context(j, n):
                g, odd = divmod(n, 2)
                bank, filled, free = [(M0, m0_filled, m0_free), (M1, m1_filled, m1_free)][odd]
                if n == 0:
                    pe.wait_ge(m1_free, j * M_FILLS + 2)
                pe.wait_ge(free, j * M_FILLS + 2 + g)
                for k in range(GROUP):
                    w, q = wk_of(heads_of(g)[2 * k + odd], g % 2)
                    mm = nc.tensor.matmul(bank[0:[P, K2][g % 2], k * P:(k + 1) * P], w, q, start=True, stop=True)
                mm.then_inc(filled, 1)

            def scores(j, z, u):
                b, g = divmod(u, GROUPS)
                if u == 0:
                    pe.wait_ge(m0_free, (j + 1) * M_FILLS + 1)
                    pe.wait_ge(m1_free, (j + 1) * M_FILLS + 1)
                if g == 0:
                    pe.wait_ge(ctx_loaded[b], (j + 1) * 64)
                pe.wait_ge(probs_ready, j * UNITS + u + 1)
                out = SB[u % 2][:, 0:KV]
                nc.tensor.matmul(out, qk1[:, z, b, g * GROUP:(g + 1) * GROUP, :], ctxT1[:, b, :], start=True, stop=False)
                nc.tensor.matmul(out, qk2[:, z, b, g * GROUP:(g + 1) * GROUP, :], ctxT2[:, b, :],
                                 start=False, stop=True).then_inc(scores_done, 1)

            def turn_probs(j, u):
                pe.wait_ge(probs_ready, j * UNITS + u + 1 + 2)
                pe.wait_ge(probsT_ready, j * UNITS + u + 1)
                for c in range(2):
                    mm = nc.tensor.transpose(TB[:, c * P:(c + 1) * P], probs[:, u % RING, c * P:(c + 1) * P], core.ident[:, :])
                mm.then_inc(turned, 1)

            def probs_ctx(j, u):
                pe.wait_ge(probsT_ready, j * UNITS + u + 1 + 1)
                pe.wait_ge(o_summed, j * UNITS + u + RING)
                for c in range(2):
                    mm = nc.tensor.matmul(OB[:, 0:AUG], probsT[:, u % RING, c * P:(c + 1) * P], ctxN[:, u // GROUPS, c, :],
                                          start=(c == 0), stop=(c == 1))
                mm.then_inc(pv_done, 1)

            def turn_out(j, u):
                pe.wait_ge(o_scaled, j * UNITS + u + 1 + RING)
                pe.wait_ge(oT_ready, (j * UNITS + u + 1) * 2)
                nc.tensor.transpose(OT[:, 0:P], o_norm[:, u % RING, 0:C1], core.ident[:, :])
                nc.tensor.transpose(OT[0:C2, P:2 * P], o_norm[:, u % RING, C1:CTX], core.ident[:, :]).then_inc(o_turned, 1)

            def values(j, z, m, heads):
                for h in heads:
                    k = h // HPC - m * QM
                    if h == m * HEADS // 2:
                        pe.wait_ge(oT_ready, (j + 1) * UNITS * 2 + 2)
                        pe.wait_ge(m2_free, j * OUT_FILLS + m + 1)
                    if whole:
                        out = M2[(h % HPC) * head_dim:(h % HPC + 1) * head_dim, k * P:(k + 1) * P]
                        v1, v2 = wv1[:, h * head_dim:(h + 1) * head_dim], wv2[:, h * head_dim:(h + 1) * head_dim]
                        first = last = True
                    else:
                        out, v1, v2 = M2[:, k * P:(k + 1) * P], wv1[:, h, :], wv2[:, h, :]
                        first, last = h % HPC == 0, h % HPC == HPC - 1
                    nc.tensor.matmul(out, v1, oT1[:, z, h, :, :], start=first, stop=False)
                    mm = nc.tensor.matmul(out, v2, oT2[:, z, h, :, :], start=False, stop=last)
                    if h == (m + 1) * HEADS // 2 - 1:
                        mm.then_inc(m2_filled, 1)

            def project(j, part, parts):
                n = max(QCH // parts, 1)
                for c in range(part * n, min((part + 1) * n, QCH)):
                    if c == 0:
                        pe.wait_ge(m2_free, j * OUT_FILLS + 3)
                    nc.tensor.matmul(M2[:, 0:D], aT[:, c, :], wo_s[:, c, :], start=(c == 0), stop=False)
                    if c == QCH - 1:
                        nc.tensor.matmul(M2[:, 0:D], core.ones[:, 0:P], bo_s[:, :], start=False, stop=True).then_inc(m2_filled, 1)

            for m in range(2):
                queries(0, m, range(QM))
            for n in range(2 * GROUPS):
                to_context(0, n)

            def tile(j, z):
                for s in range(UNITS):
                    at = steps_of(s, j)
                    ahead = not known(j, TILES - 1) and not known(j, TILES)
                    behind = not known(j, 0)
                    if at(0):
                        scores(j, z, s)
                    if ahead and s < 4:
                        half = range(QM // 2) if s % 2 == 0 else range(QM // 2, QM)
                        queries(j + 1, s // 2, half)
                    if ahead and 4 <= s < 4 + 2 * GROUPS:
                        to_context(j + 1, s - 4)
                    if at(TURN):
                        turn_probs(*at(TURN))
                    if at(PV):
                        probs_ctx(*at(PV))
                    if behind and V_STEP <= s < V_STEP + 8:
                        n = s - V_STEP
                        values(j - 1, 1 - z, n // 4, range(2 * n, 2 * n + 2))
                    if behind and WO_STEP <= s < WO_STEP + 4:
                        project(j - 1, s - WO_STEP, 4)
                    if at(TURN_O):
                        turn_out(*at(TURN_O))

            every_tile(pe, tile)

        @block.scalar
        def _(act):
            ln.act(act)
            act.sem_inc(m0_free, 1)
            act.sem_inc(m2_free, 1)
            act.sem_inc(probs_ready, 2)
            act.sem_inc(o_scaled, RING)
            act.sem_inc(o_turned, RING)
            act.sem_inc(oT_ready, 2)
            if biases:
                act.wait_ge(weights_loaded, WEIGHTS)

            def queries(j):
                act.wait_ge(m0_filled, j * M_FILLS + 1)
                nc.scalar.mul(qT[:, 0:QM, :], M0[:, 0:QM * P].rearrange("p (j n) -> p j n", n=P), SCALE).then_inc(m0_free, 1)

            def to_context(j, z, g):
                act.wait_ge(m0_filled, j * M_FILLS + 2 + g)
                nc.scalar.copy(qk_of(z, g, 0), M0[0:[P, K2][g % 2], :].rearrange("p (j b q) -> p b j q", j=GROUP, q=SEQ)).then_inc(m0_free, 1)

            def exp(j, u):
                act.wait_ge(negmax_ready, j * UNITS + u + 1)
                act.wait_ge(o_summed, j * UNITS + u + 1)
                src = clamped[:, u % 2, :] if clamp else SB[u % 2][:, 0:KV]
                nc.scalar.activation(probs[:, u % RING, :], src, ACT.Exp, bias=negmax[:, u % RING:u % RING + 1]).then_inc(probs_ready, 1)

            def scale_out(j, u):
                act.wait_ge(rsum_ready, j * UNITS + u + 1)
                act.wait_ge(o_turned, j * UNITS + u + 1)
                nc.scalar.mul(o_norm[:, u % RING, :], o_sum[:, u % RING, 0:CTX], rsum[:, u % RING:u % RING + 1]).then_inc(o_scaled, 1)

            def turned_out(j, z, u):
                b, g = divmod(u, GROUPS)
                heads = slice(g * GROUP, (g + 1) * GROUP)
                act.wait_ge(o_turned, j * UNITS + u + 1 + RING)
                nc.scalar.copy(oT1[:, z, heads, b, :], OT[:, 0:P].rearrange("p (h q) -> p h q", q=SEQ)).then_inc(oT_ready, 1)
                nc.scalar.copy(oT2[:, z, heads, b, :], OT[0:C2, P:2 * P].rearrange("p (h q) -> p h q", q=SEQ)).then_inc(oT_ready, 1)

            def values(j, m):
                act.wait_ge(m2_filled, j * OUT_FILLS + m + 1)
                to, of = aT[:, m * QM:(m + 1) * QM, :], M2[:, 0:QM * P].rearrange("p (j n) -> p j n", n=P)
                if biases:
                    nc.scalar.activation(to, of, ACT.Identity, bias=bv_s[:, m:m + 1]).then_inc(m2_free, 1)
                else:
                    nc.scalar.copy(to, of).then_inc(m2_free, 1)

            queries(0)
            for g in range(GROUPS):
                to_context(0, 0, g)

            def tile(j, z):
                for s in range(UNITS):
                    at = steps_of(s, j)
                    ahead = not known(j, TILES - 1) and not known(j, TILES)
                    behind = not known(j, 0)
                    if at(SCALE_O):
                        scale_out(*at(SCALE_O))
                    if at(0):
                        exp(j, s)
                    if ahead and s == 1:
                        queries(j + 1)
                    if ahead and 4 <= s < 4 + 2 * GROUPS and s % 2 == 0:
                        to_context(j + 1, 1 - z, (s - 4) // 2)
                    if behind and s in (V_STEP + 3, V_STEP + 7):
                        values(j - 1, (s - V_STEP) // 4)
                    if at(TURN_O):
                        t, u = at(TURN_O)
                        turned_out(t, z if s >= TURN_O else 1 - z, u)

            every_tile(act, tile)

        @block.vector
        def _(dve):
            ln.dve(dve)
            dve.sem_inc(m1_free, 1)
            dve.sem_inc(probsT_ready, 1)
            dve.sem_inc(o_summed, RING)

            def queries(j):
                dve.wait_ge(m1_filled, j * M_FILLS + 1)
                nc.vector.tensor_scalar(qT[:, QM:QCH, :], M1[:, 0:QM * P].rearrange("p (j n) -> p j n", n=P), SCALE, None,
                                        ALU.mult).then_inc(m1_free, 1)

            def to_context(j, z, g):
                dve.wait_ge(m1_filled, j * M_FILLS + 2 + g)
                nc.vector.tensor_copy(qk_of(z, g, 1), M1[0:[P, K2][g % 2], :].rearrange("p (j b q) -> p b j q", j=GROUP, q=SEQ)).then_inc(m1_free, 1)

            def largest(j, u):
                dve.wait_ge(scores_done, j * UNITS + u + 1)
                src = SB[u % 2][:, 0:KV]
                if clamp:
                    nc.vector.tensor_scalar(clamped[:, u % 2, :], src, -clamp, clamp, ALU.max, ALU.min).then_inc(clamp_done, 1)
                    dve.wait_ge(clamp_done, j * UNITS + u + 1)
                    src = clamped[:, u % 2, :]
                nc.vector.tensor_reduce(negmax[:, u % RING:u % RING + 1], src, AX.X, ALU.max, negate=True).then_inc(negmax_ready, 1)

            def turned_probs(j, u):
                dve.wait_ge(turned, j * UNITS + u + 1)
                nc.vector.tensor_copy(probsT[:, u % RING, :], TB[:, 0:2 * P]).then_inc(probsT_ready, 1)

            def sum_out(j, u):
                dve.wait_ge(pv_done, j * UNITS + u + 1)
                dve.wait_ge(o_scaled, j * UNITS + u + 1)
                nc.vector.scalar_tensor_tensor(o_sum[:, u % RING, :], ctx_last[:, u // GROUPS, :], probs[:, u % RING, KV - 1:KV],
                                               OB[:, 0:AUG], ALU.mult, ALU.add).then_inc(o_summed, 1)
                dve.wait_ge(o_summed, j * UNITS + u + 1 + RING)
                nc.vector.reciprocal(rsum[:, u % RING:u % RING + 1], o_sum[:, u % RING, CTX:AUG]).then_inc(rsum_ready, 1)

            def add(j):
                dve.wait_ge(m2_filled, (j + 1) * OUT_FILLS)
                xi = core.x[:, bass.ds(j, 1), :].rearrange("p a n -> p (a n)")
                nc.vector.tensor_tensor(xi, xi, M2[:, 0:D], ALU.add).then_inc(m2_free, 1)

            queries(0)
            for g in range(GROUPS):
                to_context(0, 0, g)

            def tile(j, z):
                for s in range(UNITS):
                    at = steps_of(s, j)
                    ahead = not known(j, TILES - 1) and not known(j, TILES)
                    behind = not known(j, 0)
                    if at(0):
                        largest(j, s)
                    if at(TURN):
                        turned_probs(*at(TURN))
                    if at(PV):
                        sum_out(*at(PV))
                    if ahead and s == 3:
                        queries(j + 1)
                    if ahead and 4 <= s < 4 + 2 * GROUPS and s % 2 == 1:
                        to_context(j + 1, 1 - z, (s - 4) // 2)
                    if behind and s == WO_STEP + 3:
                        add(j - 1)

            every_tile(dve, tile)


def stage_xattn0(core):
    d = core.dram
    stage_cross_attention(core, "xattn0", d["L0_xattn_Wq"], d["L0_xattn_Wk_T"], d["L0_xattn_Wv"], d["L0_xattn_Wo"],
                          d["L0_xattn_bo"], None, 64, None)


def stage_xattn1(core):
    d = core.dram
    stage_cross_attention(core, "xattn1", d["L1_xattn_Wq"], d["L1_wk_heads"], d["L1_wv_heads"], d["L1_xattn_Wo"],
                          d["L1_xattn_bo"], (d["L1_xattn_bq"], d["L1_xattn_bv_cols"]), 16, 10000.0)


def stage_xattn2(core):
    d = core.dram
    stage_cross_attention(core, "xattn2", d["L2_xattn_w_q"], d["L2_xattn_w_k_T"], d["L2_xattn_w_v"], d["L2_xattn_w_o"],
                          d["L2_xattn_b_o"], None, 64, None)


def stage_attn0(core):
    nc, d = core.nc, core.dram
    HEADS, HD = 16, 16
    HPC = P // HD
    SCALE = HD ** -0.5
    with ExitStack() as ctx:
        st = Stage(core, ctx, "attn0")
        ln = Norm(st)
        w = st.sb("w", [P, CD, 3 * D])
        wo = st.sb("wo", [P, CD, D])
        b_cols = st.sb("b_cols", [P, 6])
        bv = st.sb("bv", [1, D])
        bo = st.sb("bo", [1, D])
        rel = st.sb("rel", [P, HEADS, SEQ])
        head_of = st.sb("head_of", [P, HPC])
        qT = st.sb("qT", [P, CD, TOKENS])
        kT = st.sb("kT", [P, CD, TOKENS])
        v = st.sb("v", [P, TILES, D])
        k_heads = st.sb("k_heads", [P, 2, CD, PER_TILE, HPC, SEQ])
        s_rel = st.sb("s_rel", [P, 2, HEADS, SEQ])
        s_max = st.sb("s_max", [P, 2, HEADS])
        s_sub = st.sb("s_sub", [P, 2, HEADS, SEQ])
        probs = st.sb("probs", [P, 2, HEADS, SEQ])
        probsT = st.sb("probsT", [P, 2, HEADS, P])
        rsum = st.sb("rsum", [P, 2, HEADS])
        psum = st.sb("psum", [P, 2, HEADS])
        o = st.sb("o", [P, 2, D])
        oT = st.sb("oT", [P, 2, CD, P])
        loaded = st.sem("loaded")
        qk_done, qk_ready = st.sem("qk_done"), st.sem("qk_ready")
        v_done, v_ready = st.sem("v_done"), st.sem("v_ready")
        k0_ready, k1_ready = st.sem("k0_ready"), st.sem("k1_ready")
        scores_done = st.sem("scores_done")
        sub_ready = st.sem("sub_ready")
        probs_ready = st.sem("probs_ready")
        probsT_zero = st.sem("probsT_zero")
        probsT_ready = st.sem("probsT_ready")
        pv_done = st.sem("pv_done")
        o_ready = st.sem("o_ready")
        o_turned = st.sem("o_turned")
        oT_ready = st.sem("oT_ready")
        y_done = st.sem("y_done")
        x_done = st.sem("x_done")
        steps = st.sem("dve_steps")
        bank = [b[:, :] for b in core.bank]
        LOADS = 7
        block = ctx.enter_context(nc.Block())

        def spread_keys(eng, t, c):
            k = kT[:, c, t * P:(t + 1) * P].rearrange("p (b k) -> p b k", b=PER_TILE).unsqueeze(2)
            m = head_of[:, :].unsqueeze(1).unsqueeze(3)
            full = [P, PER_TILE, HPC, SEQ]
            return eng.tensor_tensor(k_heads[:, t % 2, c], k.broadcast_to(full), m.broadcast_to(full), ALU.mult)

        @block.sync
        def _(sp):
            sp.dma_start(w[:, :, :], d["L0_attn_W_qkv"].rearrange("(c p) n -> p c n", p=P)).then_inc(loaded, 16)
            sp.dma_start(wo[:, :, :], d["L0_attn_W_out"].rearrange("(c p) n -> p c n", p=P)).then_inc(loaded, 16)
            sp.dma_start(b_cols[:, :], d["L0_attn_b_qkv_cols"]).then_inc(loaded, 16)
            sp.dma_start(bv[:, :], d["L0_attn_b_qkv"][2 * D:3 * D].rearrange("(a n) -> a n", a=1)).then_inc(loaded, 16)
            sp.dma_start(bo[:, :], d["L0_attn_b_out"].rearrange("(a n) -> a n", a=1)).then_inc(loaded, 16)
            sp.dma_start(rel[:, :, :], d["L0_rel"]).then_inc(loaded, 16)
            sp.dma_start(head_of[:, :], d["head_of"]).then_inc(loaded, 16)

        @block.gpsimd
        def _(pool):
            ln.pool(pool)
            nc.gpsimd.memset(probsT[:, :, :, :], 0.0).then_inc(probsT_zero, 1)
            pool.wait_ge(loaded, 16 * LOADS)
            for t in range(TILES):
                pool.wait_ge(qk_ready, 4 if t < 4 else 8)
                if t >= 2:
                    pool.wait_ge(scores_done, t - 1)
                spread_keys(nc.gpsimd, t, 1).then_inc(k1_ready, 1)

        @block.tensor
        def _(pe):
            ln.pe(pe)
            pe.wait_ge(loaded, 16 * LOADS)
            for n in range(2):
                pe.wait_ge(ln.xnT_ready, CD * (n + 1))
                for f in range(4):
                    k = 4 * n + f
                    if k >= 2:
                        pe.wait_ge(qk_ready, k - 1)
                    for c in range(CD):
                        mm = nc.tensor.matmul(bank[4 + k % 2], w[:, c, f * P:(f + 1) * P], core.xnT[:, c, n * HALF:(n + 1) * HALF],
                                              start=(c == 0), stop=(c == CD - 1))
                    mm.then_inc(qk_done, 1)
                    if k >= 2:
                        pe.wait_ge(v_ready, k - 1)
                    out = bank[6 + k % 2][:, 0:D]
                    for c in range(CD):
                        nc.tensor.matmul(out, core.xnT[:, c, k * P:(k + 1) * P], w[:, c, 2 * D:3 * D], start=(c == 0), stop=False)
                    nc.tensor.matmul(out, core.ones[:, 0:P], bv[:, :], start=False, stop=True).then_inc(v_done, 1)
            pe.wait_ge(qk_ready, 8)
            pe.wait_ge(v_ready, 8)
            for s in range(TILES + 3):
                if s < TILES:
                    t = s
                    pe.wait_ge(k0_ready, t + 1)
                    pe.wait_ge(k1_ready, t + 1)
                    if t >= 2:
                        pe.wait_ge(sub_ready, t - 1)
                    for c in range(CD):
                        for b in range(PER_TILE):
                            q = qT[:, c, t * P + b * SEQ:t * P + (b + 1) * SEQ]
                            mm = nc.tensor.matmul(bank[t % 2][b * SEQ:(b + 1) * SEQ, c * D:(c + 1) * D], q, k_heads[:, t % 2, c, b],
                                                  start=True, stop=True, tile_position=(0, b * SEQ))
                    mm.then_inc(scores_done, 1)
                if 1 <= s <= TILES:
                    t = s - 1
                    pe.wait_ge(probsT_ready, t + 1)
                    if t >= 2:
                        pe.wait_ge(o_ready, t - 1)
                    for h in range(HEADS):
                        mm = nc.tensor.matmul(bank[2 + t % 2][:, h * HD:(h + 1) * HD], probsT[:, t % 2, h, :],
                                              v[:, t, h * HD:(h + 1) * HD], start=True, stop=True)
                    mm.then_inc(pv_done, 1)
                if 2 <= s <= TILES + 1:
                    t = s - 2
                    pe.wait_ge(o_ready, t + 1)
                    if t >= 2:
                        pe.wait_ge(oT_ready, t - 1)
                    for c in range(CD):
                        mm = nc.tensor.transpose(bank[4 + t % 2][:, c * P:(c + 1) * P], o[:, t % 2, c * P:(c + 1) * P], core.ident[:, :])
                    mm.then_inc(o_turned, 1)
                if s >= 3:
                    t = s - 3
                    pe.wait_ge(oT_ready, t + 1)
                    if t >= 2:
                        pe.wait_ge(x_done, t - 1)
                    y = bank[6 + t % 2][:, 0:D]
                    for c in range(CD):
                        nc.tensor.matmul(y, oT[:, t % 2, c, :], wo[:, c, :], start=(c == 0), stop=False)
                    nc.tensor.matmul(y, core.ones[:, 0:P], bo[:, :], start=False, stop=True).then_inc(y_done, 1)

        @block.scalar
        def _(act):
            ln.act(act)
            for t in range(TILES):
                act.wait_ge(v_done, t + 1)
                nc.scalar.copy(v[:, t, :], bank[6 + t % 2][:, 0:D]).then_inc(v_ready, 1)
            for s in range(TILES + 2):
                if s < TILES:
                    t = s
                    act.wait_ge(sub_ready, t + 1)
                    if t >= 2:
                        act.wait_ge(probsT_ready, t - 1)
                    nc.scalar.activation(probs[:, t % 2], s_sub[:, t % 2], ACT.Exp).then_inc(probs_ready, 1)
                if s >= 2:
                    t = s - 2
                    act.wait_ge(o_turned, t + 1)
                    if t >= 2:
                        act.wait_ge(y_done, t - 1)
                    nc.scalar.copy(oT[:, t % 2], bank[4 + t % 2][:, 0:D].rearrange("p (c n) -> p c n", c=CD)).then_inc(oT_ready, 1)

        @block.vector
        def _(dve):
            ln.dve(dve)
            step = Chain(dve, steps)
            dve.wait_ge(loaded, 16 * LOADS)
            for k in range(8):
                n, f = divmod(k, 4)
                dve.wait_ge(qk_done, k + 1)
                to = [qT, kT][f // 2][:, f % 2, n * HALF:(n + 1) * HALF]
                nc.vector.tensor_scalar(to, bank[4 + k % 2], b_cols[:, f:f + 1], SCALE if f < 2 else 1.0,
                                        ALU.add, ALU.mult).then_inc(qk_ready, 1)
            dve.wait_ge(qk_ready, 8)
            dve.wait_ge(probsT_zero, 1)
            for s in range(TILES + 3):
                if s < TILES:
                    t = s
                    if t >= 2:
                        dve.wait_ge(scores_done, t - 1)
                    spread_keys(nc.vector, t, 0).then_inc(k0_ready, 1)
                if 1 <= s <= TILES:
                    t = s - 1
                    z = t % 2
                    dve.wait_ge(scores_done, t + 1)
                    step(nc.vector.tensor_tensor(s_rel[:, z], bank[z].rearrange("p (h k) -> p h k", h=HEADS), rel[:, :, :], ALU.add))
                    step(nc.vector.tensor_reduce(s_max[:, z], s_rel[:, z], AX.X, ALU.max))
                    if t >= 2:
                        dve.wait_ge(probs_ready, t - 1)
                    nc.vector.tensor_tensor(s_sub[:, z], s_rel[:, z], s_max[:, z].unsqueeze(2).broadcast_to([P, HEADS, SEQ]),
                                            ALU.subtract).then_inc(sub_ready, 1)
                    dve.wait_ge(probs_ready, t + 1)
                    if t >= 2:
                        dve.wait_ge(pv_done, t - 1)
                    step(nc.vector.tensor_reduce(psum[:, z], probs[:, z], AX.X, ALU.add))
                    step(nc.vector.reciprocal(rsum[:, z], psum[:, z]))
                    for b in range(PER_TILE):
                        r = slice(b * SEQ, (b + 1) * SEQ)
                        last = nc.vector.transpose(probsT[r, z, :, r], probs[r, z])
                    last.then_inc(probsT_ready, 1)
                if 2 <= s <= TILES + 1:
                    t = s - 2
                    z = t % 2
                    dve.wait_ge(pv_done, t + 1)
                    if t >= 2:
                        dve.wait_ge(o_turned, t - 1)
                    nc.vector.tensor_tensor(o[:, z].rearrange("p (h e) -> p h e", h=HEADS),
                                            bank[2 + z][:, 0:D].rearrange("p (h e) -> p h e", h=HEADS),
                                            rsum[:, z].unsqueeze(2).broadcast_to([P, HEADS, HD]), ALU.mult).then_inc(o_ready, 1)
                if s >= 3:
                    t = s - 3
                    dve.wait_ge(y_done, t + 1)
                    nc.vector.tensor_tensor(core.x[:, t, :], core.x[:, t, :], bank[6 + t % 2][:, 0:D], ALU.add).then_inc(x_done, 1)


def stage_one_head(core, name, wq, wk, wv, wo, b_qk, bv, bo, gamma):
    nc, d = core.nc, core.dram
    soft_theta = gamma is None
    with ExitStack() as ctx:
        st = Stage(core, ctx, name)
        ln = Norm(st)
        w = st.sb("w", [P, CD, 3 * D])
        qT = st.sb("qT", [P, CD, TOKENS])
        kT = st.sb("kT", [P, CD, TOKENS])
        v = st.sb("v", [P, TILES, D])
        sub = st.sb("sub", [P, TILES, SEQ])
        smax = st.sb("smax", [P, TILES])
        probs = st.sb("probs", [P, TILES, SEQ])
        psum = st.sb("psum", [P, TILES])
        rsum = st.sb("rsum", [P, TILES])
        probsT = st.sb("probsT", [P, TILES, P])
        loaded = st.sem("loaded")
        qk_done, qk_ready = st.sem("qk_done"), st.sem("qk_ready")
        v_done, v_ready = st.sem("v_done"), st.sem("v_ready")
        scores_done = st.sem("scores_done")
        sub_ready = st.sem("sub_ready")
        probs_ready = st.sem("probs_ready")
        probsT_zero = st.sem("probsT_zero")
        probsT_ready = st.sem("probsT_ready")
        pv_done = st.sem("pv_done")
        x_done = st.sem("x_done")
        steps = st.sem("dve_steps")
        if soft_theta:
            wo_s, bo_s, bv_s, b_s = st.sb("wo", [P, CD, D]), st.sb("bo", [1, D]), st.sb("bv", [1, D]), st.sb("b", [P, 2 * CD])
            th_half, th_full = st.sb("th_half", [P, TILES * SEQ]), st.sb("th_full", [P, TILES * SEQ])
            relu, theta = st.sb("relu", [P, TILES * SEQ]), st.sb("theta", [P, TILES * SEQ])
            o, oT = st.sb("o", [P, 2, D]), st.sb("oT", [P, 2, CD, P])
            tanh_ready, o_ready, o_turned = st.sem("tanh_ready"), st.sem("o_ready"), st.sem("o_turned")
            oT_ready, y_done = st.sem("oT_ready"), st.sem("y_done")
            LOADS = 8
        else:
            gamma_s, x_plus, rgamma = st.sb("gamma", [P, 1]), st.sb("x_plus", [P, TILES, D]), st.sb("rgamma", [P, TILES])
            x_plus_ready = st.sem("x_plus_ready")
            LOADS = 4
        bank = [b[:, :] for b in core.bank]
        S = bank[0][:, 0:TILES * SEQ]
        block = ctx.enter_context(nc.Block())

        @block.sync
        def _(sp):
            for n, m in enumerate([wq, wk, wv]):
                sp.dma_start(w[:, :, n * D:(n + 1) * D], m.rearrange("(c p) n -> p c n", p=P)).then_inc(loaded, 16)
            if soft_theta:
                sp.dma_start(wo_s[:, :, :], wo.rearrange("(c p) n -> p c n", p=P)).then_inc(loaded, 16)
                sp.dma_start(bo_s[:, :], bo.rearrange("(a n) -> a n", a=1)).then_inc(loaded, 16)
                sp.dma_start(bv_s[:, :], bv.rearrange("(a n) -> a n", a=1)).then_inc(loaded, 16)
                for n in range(2):
                    sp.dma_start(b_s[:, n * CD:(n + 1) * CD], b_qk[n]).then_inc(loaded, 16)
            else:
                sp.dma_start(gamma_s[:, :], gamma.partition_broadcast(P)).then_inc(loaded, 16)

        @block.gpsimd
        def _(pool):
            ln.pool(pool)
            nc.gpsimd.memset(probsT[:, :, :], 0.0).then_inc(probsT_zero, 1)
            if not soft_theta:
                pool.wait_ge(ln.xn_ready, TILES)
                nc.gpsimd.tensor_tensor(x_plus[:, :, :], core.x[:, :, :], core.xn[:, :, :], ALU.add).then_inc(x_plus_ready, 1)

        @block.tensor
        def _(pe):
            ln.pe(pe)
            pe.wait_ge(loaded, 16 * LOADS)
            for n in range(2):
                pe.wait_ge(ln.xnT_ready, CD * (n + 1))
                for f in range(4):
                    k = 4 * n + f
                    if k >= 2:
                        pe.wait_ge(qk_ready, k - 1)
                    for c in range(CD):
                        mm = nc.tensor.matmul(bank[4 + k % 2], w[:, c, f * P:(f + 1) * P], core.xnT[:, c, n * HALF:(n + 1) * HALF],
                                              start=(c == 0), stop=(c == CD - 1))
                    mm.then_inc(qk_done, 1)
                    if k >= 2:
                        pe.wait_ge(v_ready, k - 1)
                    out = bank[6 + k % 2][:, 0:D]
                    for c in range(CD):
                        mm = nc.tensor.matmul(out, core.xnT[:, c, k * P:(k + 1) * P], w[:, c, 2 * D:3 * D], start=(c == 0),
                                              stop=(c == CD - 1 and not soft_theta))
                    if soft_theta:
                        mm = nc.tensor.matmul(out, core.ones[:, 0:P], bv_s[:, :], start=False, stop=True)
                    mm.then_inc(v_done, 1)
            pe.wait_ge(qk_ready, 8)
            pe.wait_ge(v_ready, 8)
            for t in range(TILES):
                for c in range(CD):
                    for b in range(PER_TILE):
                        own = slice(t * P + b * SEQ, t * P + (b + 1) * SEQ)
                        mm = nc.tensor.matmul(S[b * SEQ:(b + 1) * SEQ, t * SEQ:(t + 1) * SEQ], qT[:, c, own], kT[:, c, own],
                                              start=(c == 0), stop=(c == CD - 1), tile_position=(0, b * SEQ))
            mm.then_inc(scores_done, 1)
            pe.wait_ge(probsT_ready, 1)
            for s in range(TILES + (2 if soft_theta else 0)):
                if s < TILES:
                    t = s
                    if t >= 2:
                        pe.wait_ge(o_ready if soft_theta else x_done, t - 1)
                    nc.tensor.matmul(bank[2 + t % 2][:, 0:D], probsT[:, t, :], v[:, t, :], start=True, stop=True).then_inc(pv_done, 1)
                if soft_theta and 1 <= s <= TILES:
                    t = s - 1
                    pe.wait_ge(o_ready, t + 1)
                    if t >= 2:
                        pe.wait_ge(oT_ready, t - 1)
                    for c in range(CD):
                        mm = nc.tensor.transpose(bank[4 + t % 2][:, c * P:(c + 1) * P], o[:, t % 2, c * P:(c + 1) * P], core.ident[:, :])
                    mm.then_inc(o_turned, 1)
                if soft_theta and s >= 2:
                    t = s - 2
                    pe.wait_ge(oT_ready, t + 1)
                    if t >= 2:
                        pe.wait_ge(x_done, t - 1)
                    y = bank[6 + t % 2][:, 0:D]
                    for c in range(CD):
                        nc.tensor.matmul(y, oT[:, t % 2, c, :], wo_s[:, c, :], start=(c == 0), stop=False)
                    nc.tensor.matmul(y, core.ones[:, 0:P], bo_s[:, :], start=False, stop=True).then_inc(y_done, 1)

        @block.scalar
        def _(act):
            ln.act(act)
            for t in range(TILES):
                act.wait_ge(v_done, t + 1)
                nc.scalar.copy(v[:, t, :], bank[6 + t % 2][:, 0:D]).then_inc(v_ready, 1)
            if soft_theta:
                act.wait_ge(scores_done, 1)
                nc.scalar.activation(th_half[:, :], S, ACT.Tanh, scale=0.5).then_inc(tanh_ready, 1)
                nc.scalar.activation(th_full[:, :], S, ACT.Tanh).then_inc(tanh_ready, 1)
            act.wait_ge(sub_ready, 1)
            nc.scalar.activation(probs[:, :, :], sub[:, :, :], ACT.Exp).then_inc(probs_ready, 1)
            if soft_theta:
                for t in range(TILES):
                    act.wait_ge(o_turned, t + 1)
                    if t >= 2:
                        act.wait_ge(y_done, t - 1)
                    nc.scalar.copy(oT[:, t % 2], bank[4 + t % 2][:, 0:D].rearrange("p (c n) -> p c n", c=CD)).then_inc(oT_ready, 1)

        @block.vector
        def _(dve):
            ln.dve(dve)
            step = Chain(dve, steps)
            dve.wait_ge(loaded, 16 * LOADS)
            for k in range(8):
                n, f = divmod(k, 4)
                dve.wait_ge(qk_done, k + 1)
                to = [qT, kT][f // 2][:, f % 2, n * HALF:(n + 1) * HALF]
                if soft_theta:
                    nc.vector.tensor_scalar(to, bank[4 + k % 2], b_s[:, f:f + 1], None, ALU.add).then_inc(qk_ready, 1)
                else:
                    nc.vector.tensor_copy(to, bank[4 + k % 2]).then_inc(qk_ready, 1)
            dve.wait_ge(scores_done, 1)
            logits = S
            if soft_theta:
                dve.wait_ge(tanh_ready, 2)
                step(nc.vector.tensor_scalar(relu[:, :], S, 0.0, 0.1, ALU.max, ALU.mult))
                step(nc.vector.tensor_scalar(theta[:, :], th_half[:, :], 0.1, 0.6, ALU.mult, ALU.add))
                step(nc.vector.scalar_tensor_tensor(theta[:, :], th_full[:, :], 0.15, theta[:, :], ALU.mult, ALU.add))
                step(nc.vector.tensor_tensor(theta[:, :], theta[:, :], relu[:, :], ALU.add))
                logits = theta[:, :]
            logits = logits.rearrange("p (t k) -> p t k", t=TILES)
            step(nc.vector.tensor_reduce(smax[:, :], logits, AX.X, ALU.max))
            nc.vector.tensor_tensor(sub[:, :, :], logits, smax[:, :].unsqueeze(2).broadcast_to([P, TILES, SEQ]),
                                    ALU.subtract).then_inc(sub_ready, 1)
            dve.wait_ge(probs_ready, 1)
            dve.wait_ge(probsT_zero, 1)
            for b in range(PER_TILE):
                r = slice(b * SEQ, (b + 1) * SEQ)
                last = nc.vector.transpose(probsT[r, :, r], probs[r, :, :])
            last.then_inc(probsT_ready, 1)
            step(nc.vector.tensor_reduce(psum[:, :], probs[:, :, :], AX.X, ALU.add))
            step(nc.vector.reciprocal(rsum[:, :], psum[:, :]))
            if not soft_theta:
                step(nc.vector.tensor_scalar(rgamma[:, :], rsum[:, :], gamma_s[:, 0:1], None, ALU.mult))
                dve.wait_ge(x_plus_ready, 1)
                for t in range(TILES):
                    dve.wait_ge(pv_done, t + 1)
                    nc.vector.scalar_tensor_tensor(core.x[:, t, :], bank[2 + t % 2][:, 0:D], rgamma[:, t:t + 1], x_plus[:, t, :],
                                                   ALU.mult, ALU.add).then_inc(x_done, 1)
                return
            for s in range(TILES + 2):
                if s < TILES:
                    t = s
                    dve.wait_ge(pv_done, t + 1)
                    if t >= 2:
                        dve.wait_ge(o_turned, t - 1)
                    nc.vector.tensor_scalar(o[:, t % 2], bank[2 + t % 2][:, 0:D], rsum[:, t:t + 1], None, ALU.mult).then_inc(o_ready, 1)
                if s >= 2:
                    t = s - 2
                    dve.wait_ge(y_done, t + 1)
                    nc.vector.tensor_tensor(core.x[:, t, :], core.x[:, t, :], bank[6 + t % 2][:, 0:D], ALU.add).then_inc(x_done, 1)


def stage_attn1(core):
    d = core.dram
    stage_one_head(core, "attn1", d["L1_attn_Wk_T"], d["L1_attn_Wq_T"], d["L1_attn_Wv_T"], None, None, None, None, d["L1_attn_gamma"])


def stage_attn3(core):
    d = core.dram
    stage_one_head(core, "attn3", d["L3_attn_Wq_T"], d["L3_attn_Wk_T"], d["L3_attn_Wv_T"], d["L3_attn_Wo_T"],
                   (d["L3_attn_bq_cols"], d["L3_attn_bk_cols"]), d["L3_attn_bv"], d["L3_attn_bo"], None)


class Fp4:
    BLOCK = 16
    SIXTH = 1.0 / 6.0

    def __init__(self, st, n):
        self.nc, blocks = st.core.nc, n // self.BLOCK
        self.amax, self.scale = st.sb("fp4_amax", [P, blocks]), st.sb("fp4_scale", [P, blocks])
        self.rscale, self.half = st.sb("fp4_rscale", [P, blocks]), st.sb("fp4_half", [P, blocks])
        self.mag = st.sb("fp4_mag", [P, n])
        self.high, self.low = st.sb("fp4_high", [P, n], BF16), st.sb("fp4_low", [P, n], BF16)

    def __call__(self, dve, step, src, size, sign, sign_ready, item, out, n):
        nc, blocks = self.nc, n // self.BLOCK
        by_block = lambda a: a.rearrange("p (k i) -> p k i", i=self.BLOCK)
        wide = lambda a: a[:, 0:blocks].unsqueeze(2).broadcast_to([P, blocks, self.BLOCK])
        mag, high, low = self.mag[:, 0:n], self.high[:, 0:n], self.low[:, 0:n]
        step(nc.vector.tensor_reduce(self.amax[:, 0:blocks], by_block(src), AX.X, ALU.max, apply_absolute_value=True))
        step(nc.vector.tensor_scalar(self.scale[:, 0:blocks], self.amax[:, 0:blocks], self.SIXTH, 1e-12, ALU.mult, ALU.max))
        step(nc.vector.reciprocal(self.rscale[:, 0:blocks], self.scale[:, 0:blocks]))
        step(nc.vector.tensor_scalar(self.half[:, 0:blocks], self.scale[:, 0:blocks], 0.5, None, ALU.mult))
        dve.wait_ge(sign_ready, 2 * item + 1)
        step(nc.vector.tensor_tensor(by_block(mag), by_block(size), wide(self.rscale), ALU.mult))
        step(nc.vector.tensor_scalar(high, mag, 5.0, 2.0, ALU.is_gt, ALU.mult))
        step(nc.vector.scalar_tensor_tensor(high, mag, 3.5, high, ALU.is_gt, ALU.add))
        step(nc.vector.scalar_tensor_tensor(high, mag, 2.5, high, ALU.is_gt, ALU.add))
        step(nc.vector.tensor_scalar(low, mag, 1.75, None, ALU.is_gt))
        for mid in (1.25, 0.75, 0.25):
            step(nc.vector.scalar_tensor_tensor(low, mag, mid, low, ALU.is_gt, ALU.add))
        step(nc.vector.scalar_tensor_tensor(high, high, 2.0, low, ALU.mult, ALU.add))
        dve.wait_ge(sign_ready, 2 * item + 2)
        step(nc.vector.tensor_tensor(low, high, sign, ALU.mult))
        return nc.vector.tensor_tensor(by_block(out), by_block(low), wide(self.half), ALU.mult)


def stage_fp4_ffn(core):
    nc, d = core.nc, core.dram
    FF = d["L0_ffn_w_gate"].shape[0]
    WG = 2 * FF // P
    WN = WG * D
    FCH = -(-FF // P)
    LAST = FF - (FCH - 1) * P
    HN = FF // 2
    XN = TILES // 2 * D
    with ExitStack() as ctx:
        st = Stage(core, ctx, "fp4")
        ln = Norm(st)
        fp4 = Fp4(st, max(FF * 2, XN))
        w = st.sb("w", [P, WN + CD * FF])
        w_size = st.sb("w_size", [P, WN + CD * FF])
        w_sign = st.sb("w_sign", [P, WN + CD * FF], BF16)
        x_size = st.sb("x_size", [P, TILES * D])
        x_sign = st.sb("x_sign", [P, TILES * D], BF16)
        wguT = st.sb("wguT", [P, CD, 2 * FF])
        wdT = st.sb("wdT", [P, FCH, D])
        xqT = st.sb("xqT", [P, CD, TOKENS])
        gated = st.sb("gated", [P, FF])
        h = st.sb("h", [P, FF])
        h_size = st.sb("h_size", [P, FF])
        h_sign = st.sb("h_sign", [P, FF], BF16)
        hq = st.sb("hq", [P, 2, FF])
        hT = st.sb("hT", [P, 2, FCH, P])
        loaded = st.sem("loaded")
        w_sign_ready, x_sign_ready, h_sign_ready = st.sem("w_sign_ready"), st.sem("x_sign_ready"), st.sem("h_sign_ready")
        wq_ready, xq_ready, hq_ready = st.sem("wq_ready"), st.sem("xq_ready"), st.sem("hq_ready")
        turned, turned_ready = st.sem("turned"), st.sem("turned_ready")
        gu_done, silu_ready, h_ready = st.sem("gu_done"), st.sem("silu_ready"), st.sem("h_ready")
        h_turned, hT_ready = st.sem("h_turned"), st.sem("hT_ready")
        y_done, x_done = st.sem("y_done"), st.sem("x_done")
        steps = st.sem("dve_steps")
        bank = [b[:, :] for b in core.bank]
        w_up = w[:, 0:WN].rearrange("p (j k) -> p j k", k=D)
        w_down = w[:, WN:].rearrange("p (j k) -> p j k", k=FF)
        WCHUNK = FF * 2
        WCHUNKS = (WN + CD * FF) // WCHUNK

        jobs = []
        for g in range(TILES // 4):
            for c in range(CD):
                jobs.append(([core.xn[:, t, c * P:(c + 1) * P] for t in range(4 * g, 4 * g + 4)], xqT[:, c, g * HALF:(g + 1) * HALF], P))
        XJOBS = len(jobs)
        for c in range(CD):
            for j in range(0, WG, 4):
                e = min(j + 4, WG)
                jobs.append(([w_up[:, k, c * P:(c + 1) * P] for k in range(j, e)], wguT[:, c, j * P:e * P], P))
        for k in range(FCH):
            r = P if k < FCH - 1 else LAST
            jobs.append(([w_down[:, j, k * P:k * P + r] for j in range(CD)], wdT[0:r, k, :], r))
        block = ctx.enter_context(nc.Block())

        @block.sync
        def _(sp):
            sp.dma_start(w_up[:, :, :], d["L0_ffn_up"].rearrange("(j p) k -> p j k", p=P)).then_inc(loaded, 16)
            sp.dma_start(w_down[:, :, :], d["L0_ffn_w_down"].rearrange("(j p) k -> p j k", p=P)).then_inc(loaded, 16)

        @block.gpsimd
        def _(pool):
            ln.pool(pool)

        @block.tensor
        def _(pe):
            for n, (sources, to, rows) in enumerate(jobs):
                if n == 0:
                    pe.wait_ge(xq_ready, 2)
                if n == XJOBS:
                    pe.wait_ge(wq_ready, WCHUNKS)
                if n >= 2:
                    pe.wait_ge(turned_ready, n - 1)
                for k, source in enumerate(sources):
                    mm = nc.tensor.transpose(bank[6 + n % 2][0:rows, k * P:(k + 1) * P], source, core.ident[:, :])
                mm.then_inc(turned, 1)
            pe.wait_ge(turned_ready, len(jobs))
            for s in range(TILES + 2):
                if s < TILES:
                    t = s
                    if t >= 1:
                        pe.wait_ge(silu_ready, 2 * t)
                        pe.wait_ge(h_ready, t)
                    for k in range(4):
                        for c in range(CD):
                            mm = nc.tensor.matmul(bank[k][:, 0:HN], xqT[:, c, t * P:(t + 1) * P], wguT[:, c, k * HN:(k + 1) * HN],
                                                  start=(c == 0), stop=(c == CD - 1))
                    mm.then_inc(gu_done, 1)
                if 1 <= s <= TILES:
                    t = s - 1
                    pe.wait_ge(hq_ready, t + 1)
                    if t >= 1:
                        pe.wait_ge(hT_ready, 2 * t)
                    for k in range(FCH):
                        r = P if k < FCH - 1 else LAST
                        mm = nc.tensor.transpose(bank[5 + k // 4][0:r, (k % 4) * P:(k % 4 + 1) * P], hq[:, t % 2, k * P:k * P + r], core.ident[:, :])
                    mm.then_inc(h_turned, 1)
                if s >= 2:
                    t = s - 2
                    pe.wait_ge(hT_ready, 2 * (t + 1))
                    if t >= 2:
                        pe.wait_ge(x_done, t - 1)
                    y = bank[4 if t % 2 == 0 else 7][:, 0:D]
                    for k in range(FCH):
                        r = P if k < FCH - 1 else LAST
                        mm = nc.tensor.matmul(y, hT[0:r, t % 2, k, :], wdT[0:r, k, :], start=(k == 0), stop=(k == FCH - 1))
                    mm.then_inc(y_done, 1)

        @block.scalar
        def _(act):
            act.wait_ge(loaded, 32)
            nc.scalar.activation(w_size[:, :], w[:, :], ACT.Abs).then_inc(w_sign_ready, 1)
            nc.scalar.sign(w_sign[:, :], w[:, :]).then_inc(w_sign_ready, 1)
            act.wait_ge(ln.xn_ready, TILES)
            flat = core.xn[:, :, :].rearrange("p t k -> p (t k)")
            nc.scalar.activation(x_size[:, :], flat, ACT.Abs).then_inc(x_sign_ready, 1)
            nc.scalar.sign(x_sign[:, :], flat).then_inc(x_sign_ready, 1)
            for n, (sources, to, rows) in enumerate(jobs):
                act.wait_ge(turned, n + 1)
                nc.scalar.copy(to, bank[6 + n % 2][0:rows, 0:len(sources) * P]).then_inc(turned_ready, 1)
            for s in range(TILES + 1):
                if s < TILES:
                    t = s
                    act.wait_ge(gu_done, t + 1)
                    if t >= 1:
                        act.wait_ge(h_ready, t)
                    for k in range(2):
                        nc.scalar.activation(gated[:, k * HN:(k + 1) * HN], bank[k][:, 0:HN], ACT.Silu).then_inc(silu_ready, 1)
                if s >= 1:
                    t = s - 1
                    act.wait_ge(h_turned, t + 1)
                    if t >= 2:
                        act.wait_ge(y_done, t - 1)
                    nc.scalar.copy(hT[:, t % 2, 0:4, :], bank[5].rearrange("p (k n) -> p k n", k=4)).then_inc(hT_ready, 1)
                    for k in range(4, FCH):
                        r = P if k < FCH - 1 else LAST
                        cp = nc.scalar.copy(hT[0:r, t % 2, k, :], bank[6][0:r, (k % 4) * P:(k % 4 + 1) * P])
                    cp.then_inc(hT_ready, 1)
                if s < TILES:
                    act.wait_ge(h_ready, s + 1)
                    nc.scalar.activation(h_size[:, :], h[:, :], ACT.Abs).then_inc(h_sign_ready, 1)
                    nc.scalar.sign(h_sign[:, :], h[:, :]).then_inc(h_sign_ready, 1)

        @block.vector
        def _(dve):
            step = Chain(dve, steps)
            ln.dve(dve)
            dve.wait_ge(ln.xn_ready, TILES)
            flat = core.xn[:, :, :].rearrange("p t k -> p (t k)")
            for k in range(2):
                r = slice(k * XN, (k + 1) * XN)
                step(fp4(dve, step, flat[:, r], x_size[:, r], x_sign[:, r], x_sign_ready, 0, flat[:, r], XN))
                dve.sem_inc(xq_ready, 1)
            dve.wait_ge(loaded, 32)
            for k in range(WCHUNKS):
                r = slice(k * WCHUNK, (k + 1) * WCHUNK)
                step(fp4(dve, step, w[:, r], w_size[:, r], w_sign[:, r], w_sign_ready, 0, w[:, r], WCHUNK))
                dve.sem_inc(wq_ready, 1)
            for s in range(TILES + 2):
                if s < TILES:
                    t = s
                    dve.wait_ge(silu_ready, 2 * (t + 1))
                    if t >= 1:
                        dve.wait_ge(h_sign_ready, 2 * t)
                    for k in range(2):
                        mul = nc.vector.tensor_tensor(h[:, k * HN:(k + 1) * HN], gated[:, k * HN:(k + 1) * HN], bank[2 + k][:, 0:HN], ALU.mult)
                        if k == 1:
                            mul.then_inc(h_ready, 1)
                    dve.wait_ge(h_ready, t + 1)
                    if t >= 2:
                        dve.wait_ge(h_turned, t - 1)
                    fp4(dve, step, h[:, :], h_size[:, :], h_sign[:, :], h_sign_ready, t, hq[:, t % 2, :], FF).then_inc(hq_ready, 1)
                    dve.wait_ge(hq_ready, t + 1)
                if s >= 2:
                    t = s - 2
                    dve.wait_ge(y_done, t + 1)
                    yb = bank[4 if t % 2 == 0 else 7][:, 0:D]
                    nc.vector.tensor_tensor(core.x[:, t, :], core.x[:, t, :], yb, ALU.add).then_inc(x_done, 1)


def stage_scan(core):
    nc, d = core.nc, core.dram
    HD = 16
    HALVES = CD * 2
    RING = 2
    with ExitStack() as ctx:
        st = Stage(core, ctx, "scan")
        ln = Norm(st)
        w = st.sb("w", [P, CD, 3 * D])
        wo = st.sb("wo", [P, CD, D])
        bk = st.sb("bk", [P, CD])
        bo = st.sb("bo", [1, D])
        spread = st.sb("spread", [P, HD, P])
        gather = st.sb("gather", [P, HD, P])
        decay = st.sb("decay", [P, CD * TOKENS])
        rest = st.sb("rest", [P, CD * TOKENS])
        vT = st.sb("vT", [P, CD * TOKENS])
        qT = st.sb("qT", [P, CD * TOKENS])
        q_now = st.sb("q_now", [P, HALF])
        update = st.sb("update", [P, RING, HALF])
        state = st.sb("state", [P, RING, HALF])
        product = st.sb("product", [P, RING, HALF])
        hT = st.sb("hT", [P, CD, TOKENS])
        loaded = st.sem("loaded")
        k_done, k_ready, rest_ready, decay_ready = st.sem("k_done"), st.sem("k_ready"), st.sem("rest_ready"), st.sem("decay_ready")
        vq_done, vq_ready = st.sem("vq_done"), st.sem("vq_ready")
        spread_done, update_ready = st.sem("spread_done"), st.sem("update_ready")
        state_ready = st.sem("state_ready")
        product_ready = st.sem("product_ready")
        gathered = st.sem("gathered")
        hT_ready = st.sem("hT_ready")
        q_now_ready = st.sem("q_now_ready")
        y_done, x_done = st.sem("y_done"), st.sem("x_done")
        bank = [b[:, :] for b in core.bank]
        block = ctx.enter_context(nc.Block())

        @block.sync
        def _(sp):
            sp.dma_start(w[:, :, 0:D], d["L2_attn_key_w_T"].rearrange("(c p) n -> p c n", p=P)).then_inc(loaded, 16)
            sp.dma_start(w[:, :, D:3 * D], d["L2_attn_vq_w_T"].rearrange("(c p) n -> p c n", p=P)).then_inc(loaded, 16)
            sp.dma_start(bk[:, :], d["L2_attn_key_b_cols"]).then_inc(loaded, 16)
            sp.dma_start(bo[:, :], d["L2_attn_out_b"].rearrange("(a n) -> a n", a=1)).then_inc(loaded, 16)
            sp.dma_start(spread[:, :, :], d["spread"]).then_inc(loaded, 16)
            sp.dma_start(gather[:, :, :], d["gather"]).then_inc(loaded, 16)
            sp.dma_start(wo[:, :, :], d["L2_attn_out_w_T"].rearrange("(c p) n -> p c n", p=P)).then_inc(loaded, 16)

        @block.gpsimd
        def _(pool):
            ln.pool(pool)
            pool.sem_inc(product_ready, RING)
            with pool.Fori(0, HALVES) as i:
                pool.wait_ge(q_now_ready, i + 1)
                for e in range(HD):
                    pool.wait_ge(state_ready, i * HD + e + 1)
                    pool.wait_ge(gathered, i * HD + e + 1)
                    nc.gpsimd.tensor_tensor(product[:, e % RING, :], state[:, e % RING, :], q_now[:, :], ALU.mult).then_inc(product_ready, 1)

        @block.tensor
        def _(pe):
            ln.pe(pe)
            pe.wait_ge(loaded, 16 * 7)
            for n in range(2):
                pe.wait_ge(ln.xnT_ready, CD * (n + 1))
                for f in range(6):
                    if f < 2:
                        k, done, ready, b0 = 2 * n + f, k_done, k_ready, 4
                    else:
                        k, done, ready, b0 = 4 * n + f - 2, vq_done, vq_ready, 6
                    if k >= 2:
                        pe.wait_ge(ready, k - 1)
                    for c in range(CD):
                        mm = nc.tensor.matmul(bank[b0 + k % 2], w[:, c, f * P:(f + 1) * P], core.xnT[:, c, n * HALF:(n + 1) * HALF],
                                              start=(c == 0), stop=(c == CD - 1))
                    mm.then_inc(done, 1)
            pe.wait_ge(vq_ready, 8)
            with pe.Fori(0, HALVES) as i:
                now = bass.ds(i * HALF, HALF)
                for e in range(HD + 2):
                    if e < HD:
                        pe.wait_ge(update_ready, i * HD + e + 1)
                        nc.tensor.matmul(bank[e % 2], spread[:, e, :], vT[:, now], start=True, stop=True).then_inc(spread_done, 1)
                    if e == 2:
                        pe.wait_ge(hT_ready, i + 1)
                    if e >= 2:
                        pe.wait_ge(product_ready, i * HD + e - 2 + 1 + RING)
                        nc.tensor.matmul(bank[2], gather[:, e - 2, :], product[:, (e - 2) % RING, :], start=(e == 2),
                                         stop=(e == HD + 1)).then_inc(gathered, 1)
            pe.wait_ge(hT_ready, HALVES + 1)
            for t in range(TILES):
                if t >= 4:
                    pe.wait_ge(x_done, t - 3)
                y = bank[4 + t % 4][:, 0:D]
                for c in range(CD):
                    nc.tensor.matmul(y, hT[:, c, t * P:(t + 1) * P], wo[:, c, :], start=(c == 0), stop=False)
                nc.tensor.matmul(y, core.ones[:, 0:P], bo[:, :], start=False, stop=True).then_inc(y_done, 1)

        @block.scalar
        def _(act):
            ln.act(act)
            act.sem_inc(gathered, RING)
            act.sem_inc(hT_ready, 1)
            act.wait_ge(loaded, 16 * 7)
            for n in range(2):
                for c in range(CD):
                    act.wait_ge(k_done, 2 * n + c + 1)
                    at = c * TOKENS + n * HALF
                    nc.scalar.activation(decay[:, at:at + HALF], bank[4 + c], ACT.Sigmoid, bias=bk[:, c:c + 1]).then_inc(k_ready, 1)
                for f in range(4):
                    act.wait_ge(vq_done, 4 * n + f + 1)
                    at = (f % 2) * TOKENS + n * HALF
                    nc.scalar.copy([vT, qT][f // 2][:, at:at + HALF], bank[6 + f % 2]).then_inc(vq_ready, 1)
            act.wait_ge(vq_ready, 8)
            with act.Fori(0, HALVES) as i:
                act.wait_ge(product_ready, i * HD + RING)
                nc.scalar.copy(q_now[:, :], qT[:, bass.ds(i * HALF, HALF)]).then_inc(q_now_ready, 1)
                act.wait_ge(gathered, (i + 1) * HD + RING)
                nc.scalar.copy(hT[:, :, :].rearrange("p c n -> p (c n)")[:, bass.ds(i * HALF, HALF)], bank[2]).then_inc(hT_ready, 1)

        @block.vector
        def _(dve):
            ln.dve(dve)
            dve.sem_inc(update_ready, 2)
            dve.wait_ge(k_ready, 2 * CD)
            nc.vector.tensor_scalar(rest[:, :], decay[:, :], -1.0, 1.0, ALU.mult, ALU.add).then_inc(rest_ready, 1)
            dve.wait_ge(rest_ready, 1)
            nc.vector.memset(decay[:, :].rearrange("p (b s) -> p b s", s=SEQ)[:, :, 0:1], 0.0).then_inc(decay_ready, 1)
            dve.wait_ge(decay_ready, 1)
            with dve.Fori(0, HALVES) as i:
                now = bass.ds(i * HALF, HALF)
                for e in range(HD):
                    dve.wait_ge(spread_done, i * HD + e + 1)
                    nc.vector.tensor_tensor(update[:, e % RING, :], rest[:, now], bank[e % 2], ALU.mult).then_inc(update_ready, 1)
                    dve.wait_ge(update_ready, i * HD + e + 1 + 2)
                    dve.wait_ge(product_ready, i * HD + e + 1)
                    nc.vector.tensor_tensor_scan(state[:, e % RING, :], decay[:, now], update[:, e % RING, :], 0.0,
                                                 ALU.mult, ALU.add).then_inc(state_ready, 1)
            for t in range(TILES):
                dve.wait_ge(y_done, t + 1)
                nc.vector.tensor_tensor(core.x[:, t, :], core.x[:, t, :], bank[4 + t % 4][:, 0:D], ALU.add).then_inc(x_done, 1)


class Gate:

    def __init__(self, st, experts, wg, bg, logits):
        self.core, self.E, self.wg_dram, self.bg_dram, self.logits = st.core, experts, wg, bg, logits
        full = [P, TILES, experts]
        self.wg, self.bg = st.sb("gate_w", [P, CD, experts]), st.sb("gate_b", [1, experts])
        self.number = st.sb("gate_number", [P, experts])
        self.sub, self.probs, self.mask = st.sb("gate_sub", full), st.sb("gate_probs", full), st.sb("gate_mask", full)
        self.second, self.weight = st.sb("gate_second", full), st.sb("gate_weight", full)
        self.most, self.total = st.sb("gate_most", [P, TILES]), st.sb("gate_total", [P, TILES])
        self.top, self.index = st.sb("gate_top", [P, TILES, 8]), st.sb("gate_index", [P, TILES, 8], U32)
        self.place = st.sb("gate_place", [P, TILES, 8])
        self.loaded = st.sem("gate_loaded")
        self.logits_done, self.sub_ready = st.sem("gate_logits_done"), st.sem("gate_sub_ready")
        self.exp_ready, self.ready = st.sem("gate_exp_ready"), st.sem("gate_ready")

    def sp(self, sp):
        sp.dma_start(self.wg[:, :, :], self.wg_dram.rearrange("(c p) e -> p c e", p=P)).then_inc(self.loaded, 16)
        sp.dma_start(self.bg[:, :], self.bg_dram.rearrange("(a e) -> a e", a=1)).then_inc(self.loaded, 16)
        sp.dma_start(self.number[:, :], self.core.dram["number"][0:self.E].partition_broadcast(P)).then_inc(self.loaded, 16)

    def pe(self, pe):
        core, nc = self.core, self.core.nc
        pe.wait_ge(self.loaded, 48)
        for t in range(TILES):
            out = self.logits[:, t * self.E:(t + 1) * self.E]
            for c in range(CD):
                nc.tensor.matmul(out, core.xnT[:, c, t * P:(t + 1) * P], self.wg[:, c, :], start=(c == 0), stop=False)
            mm = nc.tensor.matmul(out, core.ones[:, 0:P], self.bg[:, :], start=False, stop=True)
        mm.then_inc(self.logits_done, 1)

    def act(self, act):
        act.wait_ge(self.sub_ready, 1)
        self.core.nc.scalar.activation(self.probs[:, :, :], self.sub[:, :, :], ACT.Exp).then_inc(self.exp_ready, 1)

    def dve(self, dve, step):
        nc, full = self.core.nc, [P, TILES, self.E]
        by_token = lambda a: a.unsqueeze(2).broadcast_to(full)
        dve.wait_ge(self.loaded, 48)
        dve.wait_ge(self.logits_done, 1)
        logits = self.logits.rearrange("p (t e) -> p t e", t=TILES)
        step(nc.vector.tensor_reduce(self.most[:, :], logits, AX.X, ALU.max))
        nc.vector.tensor_tensor(self.sub[:, :, :], logits, by_token(self.most[:, :]), ALU.subtract).then_inc(self.sub_ready, 1)
        dve.wait_ge(self.exp_ready, 1)
        step(nc.vector.tensor_reduce(self.total[:, :], self.probs[:, :, :], AX.X, ALU.add))
        step(nc.vector.reciprocal(self.total[:, :], self.total[:, :]))
        step(nc.vector.tensor_tensor(self.probs[:, :, :], self.probs[:, :, :], by_token(self.total[:, :]), ALU.mult))
        for t in range(TILES):
            step(nc.vector.max(self.top[:, t, :], self.probs[:, t, :]))
        for t in range(TILES):
            step(nc.vector.max_index(self.index[:, t, :], self.top[:, t, :], self.probs[:, t, :]))
        step(nc.vector.tensor_copy(self.place[:, :, :], self.index[:, :, :]))
        number = self.number[:, :].unsqueeze(1).broadcast_to(full)
        step(nc.vector.tensor_tensor(self.mask[:, :, :], number, by_token(self.place[:, :, 0]), ALU.is_equal))
        step(nc.vector.tensor_tensor(self.second[:, :, :], number, by_token(self.place[:, :, 1]), ALU.is_equal))
        step(nc.vector.tensor_tensor(self.mask[:, :, :], self.mask[:, :, :], self.second[:, :, :], ALU.add))
        step(nc.vector.tensor_tensor(self.weight[:, :, :], self.probs[:, :, :], self.mask[:, :, :], ALU.mult))
        step(nc.vector.tensor_reduce(self.total[:, :], self.weight[:, :, :], AX.X, ALU.add))
        step(nc.vector.tensor_scalar(self.total[:, :], self.total[:, :], 1e-12, None, ALU.max))
        step(nc.vector.reciprocal(self.total[:, :], self.total[:, :]))
        step(nc.vector.tensor_tensor(self.weight[:, :, :], self.weight[:, :, :], by_token(self.total[:, :]), ALU.mult))
        dve.sem_inc(self.ready, 1)


def stage_moe_capacity(core):
    nc, d = core.nc, core.dram
    E, _, FF = d["L2_ffn_w1"].shape
    CAPACITY = int(1.25 * TOKENS / E)
    SLOTS = E * CAPACITY
    FCH = FF // P
    HC = CAPACITY // 2
    PARTS = SLOTS // HC
    TRIPLE = 3 * CAPACITY
    groups = [(s, min(s + TRIPLE, SLOTS)) for s in range(0, SLOTS, TRIPLE)]
    with ExitStack() as ctx:
        st = Stage(core, ctx, "moecap")
        ln = Norm(st)
        bank = [b[:, :] for b in core.bank]
        gate = Gate(st, E, d["L2_ffn_gate_w"], d["L2_ffn_gate_b"], bank[6][:, 0:TILES * E])
        up_to = st.sb("up_to", [P, 2, P])
        slot_number = st.sb("slot_number", [P, CAPACITY])
        before = st.sb("before", [P, TILES, E])
        keep, slot = st.sb("keep", [P, TILES, E]), st.sb("slot", [P, TILES, E])
        hot, hot_w = st.sb("hot", [P, 2, SLOTS]), st.sb("hot_w", [P, 2, SLOTS])
        hot_wT = st.sb("hot_wT", [HC, PARTS, TOKENS])
        xinT = st.sb("xinT", [P, CD, SLOTS])
        w1, w2 = st.sb("w1", [P, 2, CD, FF]), st.sb("w2", [P, 2, FCH, D])
        b1, b2 = st.sb("b1", [P, 2, FCH]), st.sb("b2", [1, 2, D])
        hT = st.sb("hT", [P, 2, FCH, CAPACITY])
        y_slots = st.sb("y_slots", [HC, PARTS, D])
        loaded = st.sem("loaded")
        w_loaded = [st.sem(f"w_loaded{k}") for k in range(2)]
        ranked, hot_ready, gathered, hot_turned = st.sem("ranked"), st.sem("hot_ready"), st.sem("gathered"), st.sem("hot_turned")
        before_ready, hot_wT_ready, xinT_ready = st.sem("before_ready"), st.sem("hot_wT_ready"), st.sem("xinT_ready")
        up_done = st.sem("up_done")
        hT_ready = st.sem("hT_ready")
        down_done = st.sem("down_done")
        y_slots_ready = st.sem("y_slots_ready")
        y_done, x_done = st.sem("y_done"), st.sem("x_done")
        steps = st.sem("dve_steps")
        block = ctx.enter_context(nc.Block())

        @block.sync
        def _(sp):
            gate.sp(sp)
            sp.dma_start(up_to[:, :, :], d["up_to"]).then_inc(loaded, 16)
            sp.dma_start(slot_number[:, :], d["number"][0:CAPACITY].partition_broadcast(P)).then_inc(loaded, 16)

            def load(e, k):
                e = bass.ds(e, 1)
                sp.dma_start(w1[:, k], d["L2_ffn_w1"][e].rearrange("a (c p) f -> p (a c) f", p=P)).then_inc(w_loaded[k], 16)
                sp.dma_start(w2[:, k], d["L2_ffn_w2"][e].rearrange("a (c p) n -> p (a c) n", p=P)).then_inc(w_loaded[k], 16)
                sp.dma_start(b1[:, k], d["L2_ffn_b1_cols"][e].rearrange("a p f -> p (a f)")).then_inc(w_loaded[k], 16)
                sp.dma_start(b2[:, k], d["L2_ffn_b2"][e]).then_inc(w_loaded[k], 16)

            for k in range(2):
                load(k, k)
            with sp.Fori(1, E // 2) as i:
                for k in range(2):
                    sp.wait_ge(down_done, (i - 1) * 4 + 2 * (k + 1))
                    load(i * 2 + k, k)

        @block.gpsimd
        def _(pool):
            ln.pool(pool)

        @block.tensor
        def _(pe):
            ln.pe(pe)
            pe.wait_ge(ln.xnT_ready, 2 * CD)
            gate.pe(pe)
            pe.wait_ge(loaded, 32)
            pe.wait_ge(before_ready, 1)
            rank = bank[7][:, 0:TILES * E]
            nc.tensor.matmul(rank, up_to[:, 0, :], gate.mask[:, :, :], start=True, stop=False)
            nc.tensor.matmul(rank, up_to[:, 1, :], before[:, :, :], start=False, stop=True).then_inc(ranked, 1)
            for t in range(TILES):
                pe.wait_ge(hot_ready, t + 1)
                for c in range(CD):
                    for g, (a, b) in enumerate(groups):
                        mm = nc.tensor.matmul(bank[3 * c + g][:, 0:b - a], core.xn[:, t, c * P:(c + 1) * P], hot[:, t % 2, a:b],
                                              start=(t == 0), stop=(t == TILES - 1))
                mm.then_inc(gathered, 1)
                for g in range(PARTS // 4):
                    k = t * PARTS // 4 + g
                    if k >= 2:
                        pe.wait_ge(hot_wT_ready, k - 1)
                    for j in range(4):
                        s = (4 * g + j) * HC
                        mm = nc.tensor.transpose(bank[6 + k % 2][0:HC, j * P:(j + 1) * P], hot_w[:, t % 2, s:s + HC], core.ident[:, :])
                    mm.then_inc(hot_turned, 1)
            pe.wait_ge(xinT_ready, 2 * len(groups))
            with pe.Fori(0, E // 2) as i:
                for k in range(2):
                    pe.wait_ge(w_loaded[k], (i + 1) * 64)
                    for f in range(FCH):
                        n = k * FCH + f
                        pe.wait_ge(hT_ready, i * 2 * FCH + n + 1)
                        for c in range(CD):
                            mm = nc.tensor.matmul(bank[n % 4][:, 0:CAPACITY], w1[:, k, c, f * P:(f + 1) * P],
                                                  xinT[:, c, bass.ds((i * 2 + k) * CAPACITY, CAPACITY)], start=(c == 0), stop=(c == CD - 1))
                        mm.then_inc(up_done, 1)
                    for s in range(2):
                        pe.wait_ge(y_slots_ready, i * 4 + 2 * k + s + 1)
                        pe.wait_ge(hT_ready, i * 2 * FCH + (k + 1) * FCH + 4)
                        out = bank[4 + s][0:HC, 0:D]
                        for f in range(FCH):
                            nc.tensor.matmul(out, hT[:, k, f, s * HC:(s + 1) * HC], w2[:, k, f, :], start=(f == 0), stop=False)
                        nc.tensor.matmul(out, core.ones[:, 0:HC], b2[:, k, :], start=False, stop=True).then_inc(down_done, 1)
            pe.wait_ge(y_slots_ready, PARTS + 2)
            for t in range(TILES):
                if t >= 4:
                    pe.wait_ge(x_done, t - 3)
                for p in range(PARTS):
                    mm = nc.tensor.matmul(bank[t % 4][:, 0:D], hot_wT[:, p, t * P:(t + 1) * P], y_slots[:, p, :],
                                          start=(p == 0), stop=(p == PARTS - 1))
                mm.then_inc(y_done, 1)

        @block.scalar
        def _(act):
            ln.act(act)
            gate.act(act)
            act.sem_inc(hT_ready, 4)
            for t in range(TILES):
                for g in range(PARTS // 4):
                    k = t * PARTS // 4 + g
                    act.wait_ge(hot_turned, k + 1)
                    nc.scalar.copy(hot_wT[:, 4 * g:4 * g + 4, t * P:(t + 1) * P],
                                   bank[6 + k % 2][0:HC, :].rearrange("p (j n) -> p j n", j=4)).then_inc(hot_wT_ready, 1)
            act.wait_ge(gathered, TILES)
            for c in range(CD):
                for g, (a, b) in enumerate(groups):
                    nc.scalar.copy(xinT[:, c, a:b], bank[3 * c + g][:, 0:b - a]).then_inc(xinT_ready, 1)
            act.wait_ge(loaded, 32)
            with act.Fori(0, E // 2) as i:
                for k in range(2):
                    for f in range(FCH):
                        n = k * FCH + f
                        act.wait_ge(up_done, i * 2 * FCH + n + 1)
                        nc.scalar.activation(hT[:, k, f, :], bank[n % 4][:, 0:CAPACITY], ACT.Relu,
                                             bias=b1[:, k, f:f + 1]).then_inc(hT_ready, 1)

        @block.vector
        def _(dve):
            ln.dve(dve)
            step = Chain(dve, steps)
            gate.dve(dve, step)
            step(nc.vector.memset(before[:, 0, :], 0.0))
            for t in range(1, TILES):
                add = nc.vector.tensor_tensor(before[:, t, :], before[:, t - 1, :], gate.mask[:, t - 1, :], ALU.add)
                if t < TILES - 1:
                    step(add)
            add.then_inc(before_ready, 1)
            dve.wait_ge(loaded, 32)
            dve.wait_ge(ranked, 1)
            rank = bank[7][:, 0:TILES * E].rearrange("p (t e) -> p t e", t=TILES)
            step(nc.vector.scalar_tensor_tensor(keep[:, :, :], rank, float(CAPACITY), gate.mask[:, :, :], ALU.is_le, ALU.mult))
            step(nc.vector.tensor_tensor(slot[:, :, :], rank, keep[:, :, :], ALU.mult))
            step(nc.vector.tensor_scalar(slot[:, :, :], slot[:, :, :], -1.0, None, ALU.add))
            for t in range(TILES):
                if t >= 2:
                    dve.wait_ge(gathered, t - 1)
                    dve.wait_ge(hot_turned, (t - 1) * PARTS // 4)
                for e in range(E):
                    r = slice(e * CAPACITY, (e + 1) * CAPACITY)
                    nc.vector.tensor_scalar(hot[:, t % 2, r], slot_number[:, :], slot[:, t, e:e + 1], None, ALU.is_equal)
                    last = nc.vector.tensor_scalar(hot_w[:, t % 2, r], slot_number[:, :], slot[:, t, e:e + 1], gate.weight[:, t, e:e + 1],
                                                   ALU.is_equal, ALU.mult)
                last.then_inc(hot_ready, 1)
            dve.sem_inc(y_slots_ready, 2)
            with dve.Fori(0, E // 2) as i:
                for n in range(4):
                    dve.wait_ge(down_done, i * 4 + n + 1)
                    nc.vector.tensor_copy(y_slots[:, bass.ds(i * 4 + n, 1), :].rearrange("p a n -> p (a n)"),
                                          bank[4 + n % 2][0:HC, 0:D]).then_inc(y_slots_ready, 1)
            for t in range(TILES):
                dve.wait_ge(y_done, t + 1)
                nc.vector.tensor_tensor(core.x[:, t, :], core.x[:, t, :], bank[t % 4][:, 0:D], ALU.add).then_inc(x_done, 1)


def stage_moe(core):
    nc, d = core.nc, core.dram
    E, _, FF = d["L3_ffn_W1"].shape
    FCH = FF // P
    HALVES = TOKENS // HALF
    T_HALF = TILES // HALVES
    UPS, DOWNS = HALVES * FCH, TILES
    with ExitStack() as ctx:
        st = Stage(core, ctx, "moe")
        ln = Norm(st)
        bank = [b[:, :] for b in core.bank]
        gate = Gate(st, E, d["L3_ffn_Wg"], d["L3_ffn_bg"], bank[6][:, 0:TILES * E])
        w1, w2 = st.sb("w1", [P, 2, CD, FF]), st.sb("w2", [P, 2, FCH, D])
        b1, b2 = st.sb("b1", [P, 2, FCH]), st.sb("b2", [1, 2, D])
        hT = st.sb("hT", [P, HALVES, FCH, HALF])
        share = st.sb("share", [P, 2, TILES])
        w_loaded = [st.sem(f"w_loaded{k}") for k in range(2)]
        up_done = st.sem("up_done")
        hT_ready = st.sem("hT_ready")
        share_ready = st.sem("share_ready")
        down_done = st.sem("down_done")
        added = st.sem("added")
        steps = st.sem("dve_steps")
        block = ctx.enter_context(nc.Block())

        @block.sync
        def _(sp):
            gate.sp(sp)

            def load(e, k):
                e = bass.ds(e, 1)
                sp.dma_start(w1[:, k], d["L3_ffn_W1"][e].rearrange("a (c p) f -> p (a c) f", p=P)).then_inc(w_loaded[k], 16)
                sp.dma_start(w2[:, k], d["L3_ffn_W2"][e].rearrange("a (c p) n -> p (a c) n", p=P)).then_inc(w_loaded[k], 16)
                sp.dma_start(b1[:, k], d["L3_ffn_b1_cols"][e].rearrange("a p f -> p (a f)")).then_inc(w_loaded[k], 16)
                sp.dma_start(b2[:, k], d["L3_ffn_b2"][e]).then_inc(w_loaded[k], 16)

            for k in range(2):
                load(k, k)
            with sp.Fori(1, E // 2) as i:
                for k in range(2):
                    sp.wait_ge(down_done, ((i - 1) * 2 + k + 1) * DOWNS + TILES)
                    load(i * 2 + k, k)

        @block.gpsimd
        def _(pool):
            ln.pool(pool)

        @block.tensor
        def _(pe):
            ln.pe(pe)
            pe.wait_ge(ln.xnT_ready, 2 * CD)
            gate.pe(pe)
            pe.wait_ge(gate.ready, 1)

            def up(i, k, n):
                for f in range(FCH):
                    u = n * FCH + f
                    pe.wait_ge(hT_ready, (i * 2 + k) * UPS + u + 1)
                    for c in range(CD):
                        mm = nc.tensor.matmul(bank[u % 4], w1[:, k, c, f * P:(f + 1) * P], core.xnT[:, c, n * HALF:(n + 1) * HALF],
                                              start=(c == 0), stop=(c == CD - 1))
                    mm.then_inc(up_done, 1)

            def down(i, k, n):
                pe.wait_ge(hT_ready, (i * 2 + k) * UPS + (n + 1) * FCH + 4)
                for t in range(n * T_HALF, (n + 1) * T_HALF):
                    pe.wait_ge(added, (i * 2 + k) * DOWNS + t + 1)
                    out = bank[4 + t % 2][:, 0:D]
                    for f in range(FCH):
                        nc.tensor.matmul(out, hT[:, n, f, t % T_HALF * P:(t % T_HALF + 1) * P], w2[:, k, f, :], start=(f == 0), stop=False)
                    nc.tensor.matmul(out, core.ones[:, 0:P], b2[:, k, :], start=False, stop=True).then_inc(down_done, 1)

            with pe.Fori(0, E // 2) as i:
                for k in range(2):
                    pe.wait_ge(w_loaded[k], (i + 1) * 64)
                    for n in range(HALVES):
                        up(i, k, n)
                        if n >= 1:
                            down(i, k, n - 1)
                    down(i, k, HALVES - 1)

        @block.scalar
        def _(act):
            ln.act(act)
            gate.act(act)
            act.sem_inc(hT_ready, 4)
            with act.Fori(0, E // 2) as i:
                for k in range(2):
                    for u in range(UPS):
                        n, f = divmod(u, FCH)
                        act.wait_ge(up_done, (i * 2 + k) * UPS + u + 1)
                        if f == 0:
                            act.wait_ge(down_done, (i * 2 + k) * DOWNS + (n + 1) * T_HALF)
                        nc.scalar.activation(hT[:, n, f, :], bank[u % 4], ACT.Gelu, bias=b1[:, k, f:f + 1]).then_inc(hT_ready, 1)

        @block.vector
        def _(dve):
            ln.dve(dve)
            step = Chain(dve, steps)
            gate.dve(dve, step)
            dve.sem_inc(down_done, TILES)
            dve.sem_inc(added, 2)
            with dve.Fori(0, E // 2) as i:
                for k in range(2):
                    e = i * 2 + k
                    nc.vector.tensor_copy(share[:, k, :].unsqueeze(2), gate.weight[:, :, bass.ds(e, 1)]).then_inc(share_ready, 1)
                    dve.wait_ge(share_ready, e + 1)
                    dve.wait_ge(added, e * DOWNS + 2)
                    for t in range(TILES):
                        dve.wait_ge(down_done, e * DOWNS + t + 1 + TILES)
                        nc.vector.scalar_tensor_tensor(core.x[:, t, :], bank[4 + t % 2][:, 0:D], share[:, k, t:t + 1], core.x[:, t, :],
                                                       ALU.mult, ALU.add).then_inc(added, 1)


def stage_xattn3(core):
    nc, d = core.nc, core.dram
    KV, CTX = d["ctx_768"].shape[1:]
    C1, C2, AUG = P, CTX - P, CTX + 1
    K2 = AUG - C1
    KCH = 3
    KP = -(-KV // KCH)
    LAST = KV - (KCH - 1) * KP
    rows_of = lambda c: KP if c < KCH - 1 else LAST
    SCALE = D ** -0.5
    with ExitStack() as ctx:
        st = Stage(core, ctx, "xattn3")
        ln = Norm(st, twice=True)
        wq, wo = st.sb("wq", [P, CD, D]), st.sb("wo", [P, CD, D])
        wkT = st.sb("wkT", [P, CD, AUG])
        wk1, wk2 = st.sb("wk1", [P, D]), st.sb("wk2", [C2, D])
        wv1, wv2 = st.sb("wv1", [P, D]), st.sb("wv2", [C2, D])
        cols = st.sb("cols", [P, 4 * CD])
        g1, s1 = st.sb("g1", [P, 1]), st.sb("s1", [P, 1])
        g2, s2 = st.sb("g2", [K2, 1]), st.sb("s2", [C2, 1])
        gx, sx = st.sb("gx", [P, CD]), st.sb("sx", [P, CD])
        bo = st.sb("bo", [1, D])
        raw = st.sb("raw", [KP, PER_TILE, KCH, CTX])
        stats = st.sb("stats", [KP, PER_TILE, KCH, 6])
        small = [KP, PER_TILE, KCH]
        mean, msum, diff, dsq = st.sb("mean", small), st.sb("msum", small), st.sb("diff", small), st.sb("dsq", small)
        m2, var, veps, rstd = st.sb("m2", small), st.sb("var", small), st.sb("veps", small), st.sb("rstd", small)
        neghalf = st.sb("neghalf", [KP, PER_TILE, KCH])
        norm = st.sb("norm", [KP, PER_TILE, KCH, AUG])
        nT1, nT2 = st.sb("nT1", [P, PER_TILE, KCH * KP]), st.sb("nT2", [K2, PER_TILE, KCH * KP])
        xT = st.sb("xT", [P, CD, TOKENS])
        qT = st.sb("qT", [P, CD, P])
        qk1, qk2 = st.sb("qk1", [P, P]), st.sb("qk2", [K2, P])
        negmax, rsum = st.sb("negmax", [P, 1]), st.sb("rsum", [P, 1])
        probs = st.sb("probs", [P, KV])
        probsT = st.sb("probsT", [KP, KCH, P])
        o_norm = st.sb("o_norm", [P, CTX])
        oT1, oT2 = st.sb("oT1", [P, P]), st.sb("oT2", [C2, P])
        aT = st.sb("aT", [P, CD, P])

        loaded = st.sem("loaded")
        raw_loaded = [st.sem(f"raw_loaded{b}") for b in range(PER_TILE)]
        raw_zero, norm_one, nT2_one = st.sem("raw_zero"), st.sem("norm_one"), st.sem("nT2_one")
        xT_ready = st.sem("xT_ready")
        shift_done, shift_ready = st.sem("shift_done"), st.sem("shift_ready")
        stats_done, parts_done, mean_ready = st.sem("stats_done"), st.sem("parts_done"), st.sem("mean_ready")
        neghalf_ready, veps_ready, rstd_ready = st.sem("neghalf_ready"), st.sem("veps_ready"), st.sem("rstd_ready")
        norm_ready = st.sem("norm_ready")
        n_turned, nT_ready = st.sem("n_turned"), st.sem("nT_ready")
        q_done, qT_ready, qk_done, qk_ready = st.sem("q_done"), st.sem("qT_ready"), st.sem("qk_done"), st.sem("qk_ready")
        scores_done, negmax_ready, probs_ready = st.sem("scores_done"), st.sem("negmax_ready"), st.sem("probs_ready")
        turned, probsT_ready, pv_done = st.sem("turned"), st.sem("probsT_ready"), st.sem("pv_done")
        rsum_ready, o_ready = st.sem("rsum_ready"), st.sem("o_ready")
        o_turned, oT_ready = st.sem("o_turned"), st.sem("oT_ready")
        a_done, aT_ready = st.sem("a_done"), st.sem("aT_ready")
        y_done, x_done = st.sem("y_done"), st.sem("x_done")
        bank = [b[:, :] for b in core.bank]
        WORK, SCORES, OUT, TURN = bank[4], bank[5], bank[6], bank[7]
        LOADS = 17
        block = ctx.enter_context(nc.Block())

        @block.sync
        def _(sp):
            w = lambda to, of: sp.dma_start(to, of).then_inc(loaded, 16)
            p = "L3_xattn_"
            w(wq[:, :, :], d[p + "Wq"].rearrange("(c p) n -> p c n", p=P))
            w(wo[:, :, :], d[p + "Wo"].rearrange("(c p) n -> p c n", p=P))
            w(wkT[:, :, :], d[p + "Wk_T"].rearrange("(c p) n -> p c n", p=P))
            w(wk1[:, :], d[p + "Wk"][0:C1, :])
            w(wk2[:, :], d[p + "Wk"][C1:CTX, :])
            w(wv1[:, :], d[p + "Wv"][0:C1, :])
            w(wv2[:, :], d[p + "Wv"][C1:CTX, :])
            for n, name in enumerate(["bq", "bk", "bv"]):
                w(cols[:, n * CD:(n + 1) * CD], d[p + name + "_cols"])
            column = lambda name, a, b: d[p + name][a:b].rearrange("(p a) -> p a", a=1)
            w(g1[:, :], column("ln2_g", 0, C1))
            w(s1[:, :], column("ln2_b", 0, C1))
            w(g2[0:C2, :], column("ln2_g", C1, CTX))
            w(s2[:, :], column("ln2_b", C1, CTX))
            w(gx[:, :], d[p + "ln1_g_cols"])
            w(sx[:, :], d[p + "ln1_b_cols"])
            w(bo[:, :], d[p + "bo"].rearrange("(a n) -> a n", a=1))
            sp.wait_ge(raw_zero, 1)

            def load(i, b):
                rows = d["ctx_768"][bass.ds(i * PER_TILE + b, 1)]
                head, tail = rows[:, 0:(KCH - 1) * KP, :], rows[:, (KCH - 1) * KP:KV, :]
                sp.dma_start(raw[:, b, 0:KCH - 1, :], head.rearrange("a (c p) f -> p (a c) f", p=KP)).then_inc(raw_loaded[b], 16)
                sp.dma_start(raw[0:LAST, b, KCH - 1, :], tail.rearrange("a p f -> p (a f)")).then_inc(raw_loaded[b], 16)

            for b in range(PER_TILE):
                load(0, b)
            with sp.Fori(1, TILES) as i:
                for b in range(PER_TILE):
                    sp.wait_ge(norm_ready, (i - 1) * PER_TILE + b + 1)
                    load(i, b)

        @block.gpsimd
        def _(pool):
            ln.pool(pool)
            pool.wait_ge(neghalf_ready, 1)
            with pool.Fori(0, TILES) as i:
                pool.wait_ge(veps_ready, i + 1)
                nc.gpsimd.tensor_tensor(rstd[:, :, :], veps[:, :, :], neghalf[:, :, :], ALU.pow).then_inc(rstd_ready, 1)

        @block.tensor
        def _(pe):
            ln.pe(pe)
            pe.wait_ge(loaded, 16 * LOADS)
            for c in range(CD):
                f = slice(c * P, (c + 1) * P)
                nc.tensor.matmul(bank[4 + c][:, 0:1], wk1[:, f], s1[:, :], start=True, stop=False)
                nc.tensor.matmul(bank[4 + c][:, 0:1], wk2[:, f], s2[:, :], start=False, stop=True).then_inc(shift_done, 1)
            pe.wait_ge(shift_ready, CD)
            pe.wait_ge(xT_ready, 2 * CD)
            pe.wait_ge(nT2_one, 2)
            with pe.Fori(0, TILES) as i:
                for b in range(PER_TILE):
                    pe.wait_ge(norm_ready, i * PER_TILE + b + 1)
                    pe.wait_ge(nT_ready, (i * PER_TILE + b + 1) * 2)
                    for c in range(KCH):
                        nc.tensor.transpose(bank[2 * (b % 2)][:, c * KP:(c + 1) * KP], norm[:, b, c, 0:C1], core.ident[0:KP, 0:KP])
                        mm = nc.tensor.transpose(bank[2 * (b % 2) + 1][0:C2, c * KP:(c + 1) * KP], norm[:, b, c, C1:CTX], core.ident[0:KP, 0:KP])
                    mm.then_inc(n_turned, 1)
                    if b == 0:
                        pe.wait_ge(x_done, i + 1)
                        for j in range(CD):
                            for c in range(CD):
                                mm = nc.tensor.matmul(WORK[:, j * P:(j + 1) * P], wq[:, c, j * P:(j + 1) * P], xT[:, c, bass.ds(i * P, P)],
                                                      start=(c == 0), stop=(c == CD - 1))
                        mm.then_inc(q_done, 1)
                    if b == 1:
                        pe.wait_ge(qT_ready, (i + 1) * CD)
                        for c in range(CD):
                            nc.tensor.matmul(OUT[:, 0:P], wkT[:, c, 0:C1], qT[:, c, :], start=(c == 0), stop=(c == CD - 1))
                        for c in range(CD):
                            mm = nc.tensor.matmul(TURN[0:K2, 0:P], wkT[:, c, C1:AUG], qT[:, c, :], start=(c == 0), stop=(c == CD - 1))
                        mm.then_inc(qk_done, 1)
                pe.wait_ge(qk_ready, (i + 1) * 2)
                for b in range(PER_TILE):
                    pe.wait_ge(nT_ready, (i * PER_TILE + b + 1) * 2 + 4)
                    r = slice(b * SEQ, (b + 1) * SEQ)
                    nc.tensor.matmul(SCORES[r, 0:KV], qk1[:, r], nT1[:, b, 0:KV], start=True, stop=False, tile_position=(0, b * SEQ))
                    mm = nc.tensor.matmul(SCORES[r, 0:KV], qk2[:, r], nT2[:, b, 0:KV], start=False, stop=True, tile_position=(0, b * SEQ))
                mm.then_inc(scores_done, 1)
                pe.wait_ge(probs_ready, i + 1)
                for c in range(KCH):
                    mm = nc.tensor.transpose(TURN[0:rows_of(c), c * P:(c + 1) * P], probs[:, c * KP:c * KP + rows_of(c)], core.ident[:, :])
                mm.then_inc(turned, 1)
                pe.wait_ge(probsT_ready, (i + 1) * 2)
                for b in range(PER_TILE):
                    r = slice(b * SEQ, (b + 1) * SEQ)
                    for c in range(KCH):
                        mm = nc.tensor.matmul(OUT[r, 0:AUG], probsT[0:rows_of(c), c, r], norm[0:rows_of(c), b, c, :], start=(c == 0),
                                              stop=(c == KCH - 1), tile_position=(0, b * SEQ))
                mm.then_inc(pv_done, 1)
                pe.wait_ge(o_ready, i + 1)
                nc.tensor.transpose(TURN[:, 0:P], o_norm[:, 0:C1], core.ident[:, :])
                nc.tensor.transpose(TURN[0:C2, P:2 * P], o_norm[:, C1:CTX], core.ident[:, :]).then_inc(o_turned, 1)
                pe.wait_ge(oT_ready, (i + 1) * 2)
                for j in range(CD):
                    nc.tensor.matmul(WORK[:, j * P:(j + 1) * P], wv1[:, j * P:(j + 1) * P], oT1[:, :], start=True, stop=False)
                    mm = nc.tensor.matmul(WORK[:, j * P:(j + 1) * P], wv2[:, j * P:(j + 1) * P], oT2[:, :], start=False, stop=True)
                mm.then_inc(a_done, 1)
                pe.wait_ge(aT_ready, (i + 1) * CD)
                for c in range(CD):
                    nc.tensor.matmul(WORK[:, 0:D], aT[:, c, :], wo[:, c, :], start=(c == 0), stop=False)
                nc.tensor.matmul(WORK[:, 0:D], core.ones[:, 0:P], bo[:, :], start=False, stop=True).then_inc(y_done, 1)

        @block.scalar
        def _(act):
            act.sem_inc(nT_ready, 4)
            act.sem_inc(scores_done, 1)
            act.sem_inc(pv_done, 1)
            act.wait_ge(loaded, 16 * LOADS)
            for g in range(TILES // 4):
                act.wait_ge(ln.turned, g + 1)
                for c in range(CD):
                    nc.scalar.activation(xT[:, c, g * HALF:(g + 1) * HALF], bank[2 * g + c], ACT.Identity, bias=sx[:, c:c + 1],
                                         scale=gx[:, c:c + 1]).then_inc(xT_ready, 1)
            with act.Fori(0, TILES) as i:
                for b in range(PER_TILE):
                    act.wait_ge(n_turned, i * PER_TILE + b + 1)
                    if b == 0:
                        act.wait_ge(scores_done, i + 1)
                    nc.scalar.copy(nT1[:, b, :], bank[2 * (b % 2)][:, 0:KCH * KP]).then_inc(nT_ready, 1)
                    nc.scalar.copy(nT2[0:C2, b, :], bank[2 * (b % 2) + 1][0:C2, 0:KCH * KP]).then_inc(nT_ready, 1)
                act.wait_ge(negmax_ready, i + 1)
                nc.scalar.activation(probs[:, :], SCORES[:, 0:KV], ACT.Exp, bias=negmax[:, 0:1]).then_inc(probs_ready, 1)
                act.wait_ge(rsum_ready, i + 1)
                nc.scalar.mul(o_norm[:, :], OUT[:, 0:CTX], rsum[:, 0:1]).then_inc(o_ready, 1)
                for c in range(CD):
                    act.wait_ge(a_done, i + 1)
                    nc.scalar.activation(aT[:, c, :], WORK[:, c * P:(c + 1) * P], ACT.Identity,
                                         bias=cols[:, 2 * CD + c:2 * CD + c + 1]).then_inc(aT_ready, 1)

        @block.vector
        def _(dve):
            nc.vector.memset(raw[:, :, :, :], 0.0).then_inc(raw_zero, 1)
            nc.vector.memset(neghalf[:, :, :], -0.5).then_inc(neghalf_ready, 1)
            nc.vector.memset(norm[:, :, :, CTX:AUG], 1.0).then_inc(norm_one, 1)
            nc.vector.memset(nT2[C2:K2, :, :], 1.0).then_inc(nT2_one, 1)
            nc.vector.memset(g2[C2:K2, :], 1.0).then_inc(nT2_one, 1)
            ln.dve(dve)
            dve.sem_inc(x_done, 1)
            dve.wait_ge(loaded, 16 * LOADS)
            for c in range(CD):
                dve.wait_ge(shift_done, CD)
                nc.vector.tensor_tensor(wkT[:, c, CTX:AUG], bank[4 + c][:, 0:1], cols[:, CD + c:CD + c + 1], ALU.add).then_inc(shift_ready, 1)
            dve.wait_ge(norm_one, 1)
            dve.wait_ge(nT2_one, 2)

            def rows_stats(i, b):
                dve.wait_ge(raw_loaded[b], (i + 1) * 32)
                for c in range(KCH):
                    nc.vector.bn_stats(stats[:, b, c, :], raw[:, b, c, :]).then_inc(stats_done, 1)

            with dve.Fori(0, TILES) as i:
                for b in range(PER_TILE):
                    rows_stats(i, b)
                dve.wait_ge(stats_done, (i + 1) * PER_TILE * KCH)
                PARTS = 5
                nc.vector.tensor_tensor(msum[:, :, :], stats[:, :, :, 1], stats[:, :, :, 4], ALU.add).then_inc(parts_done, 1)
                nc.vector.tensor_tensor(diff[:, :, :], stats[:, :, :, 1], stats[:, :, :, 4], ALU.subtract).then_inc(parts_done, 1)
                nc.vector.tensor_tensor(m2[:, :, :], stats[:, :, :, 2], stats[:, :, :, 5], ALU.add).then_inc(parts_done, 1)
                dve.wait_ge(parts_done, i * PARTS + 2)
                nc.vector.scalar_tensor_tensor(dsq[:, :, :], diff[:, :, :], 0.25, diff[:, :, :], ALU.mult, ALU.mult).then_inc(parts_done, 1)
                dve.wait_ge(parts_done, i * PARTS + 4)
                nc.vector.scalar_tensor_tensor(var[:, :, :], m2[:, :, :], 1.0 / CTX, dsq[:, :, :], ALU.mult, ALU.add).then_inc(parts_done, 1)
                dve.wait_ge(parts_done, i * PARTS + 5)
                nc.vector.tensor_scalar(veps[:, :, :], var[:, :, :], EPS, None, ALU.add).then_inc(veps_ready, 1)
                nc.vector.tensor_scalar(mean[:, :, :], msum[:, :, :], 0.5, None, ALU.mult).then_inc(mean_ready, 1)
                dve.wait_ge(mean_ready, i + 1)
                dve.wait_ge(rstd_ready, i + 1)
                dve.wait_ge(pv_done, i + 1)
                for b in range(PER_TILE):
                    for c in range(KCH):
                        last = nc.vector.tensor_scalar(norm[:, b, c, 0:CTX], raw[:, b, c, :], mean[:, b, c:c + 1], rstd[:, b, c:c + 1],
                                                       ALU.subtract, ALU.mult)
                    last.then_inc(norm_ready, 1)
                dve.wait_ge(q_done, i + 1)
                for j in range(CD):
                    nc.vector.tensor_scalar(qT[:, j, :], WORK[:, j * P:(j + 1) * P], cols[:, j:j + 1], SCALE, ALU.add,
                                            ALU.mult).then_inc(qT_ready, 1)
                dve.wait_ge(qk_done, i + 1)
                nc.vector.tensor_scalar(qk1[:, :], OUT[:, 0:P], g1[:, 0:1], None, ALU.mult).then_inc(qk_ready, 1)
                nc.vector.tensor_scalar(qk2[:, :], TURN[0:K2, 0:P], g2[:, 0:1], None, ALU.mult).then_inc(qk_ready, 1)
                dve.wait_ge(scores_done, i + 2)
                nc.vector.tensor_reduce(negmax[:, 0:1], SCORES[:, 0:KV], AX.X, ALU.max, negate=True).then_inc(negmax_ready, 1)
                dve.wait_ge(turned, i + 1)
                nc.vector.tensor_copy(probsT[:, 0:KCH - 1, :], TURN[0:KP, 0:(KCH - 1) * P].rearrange("p (c n) -> p c n", n=P)).then_inc(probsT_ready, 1)
                nc.vector.tensor_copy(probsT[0:LAST, KCH - 1, :], TURN[0:LAST, (KCH - 1) * P:KCH * P]).then_inc(probsT_ready, 1)
                dve.wait_ge(pv_done, i + 2)
                nc.vector.reciprocal(rsum[:, 0:1], OUT[:, CTX:AUG]).then_inc(rsum_ready, 1)
                dve.wait_ge(o_turned, i + 1)
                nc.vector.tensor_scalar(oT1[:, :], TURN[:, 0:P], g1[:, 0:1], s1[:, 0:1], ALU.mult, ALU.add).then_inc(oT_ready, 1)
                nc.vector.tensor_scalar(oT2[:, :], TURN[0:C2, P:2 * P], g2[0:C2, 0:1], s2[:, 0:1], ALU.mult, ALU.add).then_inc(oT_ready, 1)
                dve.wait_ge(y_done, i + 1)
                xi = core.x[:, bass.ds(i, 1), :].rearrange("p a n -> p (a n)")
                nc.vector.tensor_tensor(xi, xi, WORK[:, 0:D], ALU.add).then_inc(x_done, 1)


def program(nc, dram, out, stages):
    with ExitStack() as ctx:
        core = Core(nc, ctx, dram)
        loaded = ctx.enter_context(nc.semaphore("x_loaded"))
        with nc.Block() as block:
            @block.sync
            def _(sp):
                sp.dma_start(core.x[:, :, :], dram["x"].rearrange("(t b) s n -> (b s) t n", t=TILES)).then_inc(loaded, 16)
                sp.dma_start(core.ident[:, :], dram["ident"]).then_inc(loaded, 16)
                sp.wait_ge(loaded, 32)

            @block.vector
            def _(dve):
                nc.vector.memset(core.ones[:, :], 1.0)
                nc.vector.memset(core.neghalf[:, :], -0.5)
        todo = {0: stage_xattn0, 1: stage_attn0, 2: stage_fp4_ffn, 3: stage_xattn1, 4: stage_attn1, 5: stage_low_rank, 6: stage_xattn2, 7: stage_scan, 8: stage_moe_capacity, 9: stage_xattn3, 10: stage_attn3, 11: stage_moe}
        for s in stages:
            todo[s](core)
        stored = ctx.enter_context(nc.semaphore("stored"))
        with nc.Block() as block:
            @block.sync
            def _(sp):
                sp.dma_start(out.rearrange("(t b) s n -> (b s) t n", t=TILES), core.x[:, :, :]).then_inc(stored, 16)
                sp.wait_ge(stored, 16)


def kernel(**inputs):
    import concourse.bacc as _bacc
    from concourse import mybir as _mybir
    from concourse.bass_utils import run_bass_kernel_spmd as _run

    def turn(name):
        return np.ascontiguousarray(np.swapaxes(np.asarray(inputs[name]), -1, -2))

    data = {k: np.ascontiguousarray(np.asarray(v)) for k, v in inputs.items()}
    for name in ["L0_xattn_Wk", "L1_xattn_Wk", "L2_xattn_w_k", "L1_ffn_W", "L1_ffn_C", "L1_attn_Wq", "L1_attn_Wk", "L1_attn_Wv",
                 "L3_attn_Wq", "L3_attn_Wk", "L3_attn_Wv", "L3_attn_Wo"]:
        data[name + "_T"] = turn(name)
    for name in ["L0_xattn_Wk_T", "L2_xattn_w_k_T"]:
        data[name] = np.pad(data[name], ((0, 0), (0, 1)))
    data["ident"] = np.eye(P, dtype=np.float32)

    ctx = data["ctx_768"]
    ones = np.ones(ctx.shape[:2] + (1,), np.float32)
    data["ctxA"] = np.concatenate([ctx, ones], axis=2)
    data["ctxT"] = np.ascontiguousarray(np.swapaxes(data["ctxA"], 1, 2))
    HEADS, HD = 16, 16
    wkT, bk = data["L1_xattn_Wk_T"], data["L1_xattn_bk"]
    wk_heads = np.zeros((HEADS, P, wkT.shape[1] + 1), np.float32)
    wv_heads = np.zeros((wkT.shape[1], HEADS, P), np.float32)
    for h in range(HEADS):
        r, o = slice(h * HD, (h + 1) * HD), slice(h * HD % P, h * HD % P + HD)
        wk_heads[h, o, :-1] = wkT[r]
        wk_heads[h, o, -1] = bk[r]
        wv_heads[:, h, o] = data["L1_xattn_Wv"][:, r]
    data["L1_wk_heads"], data["L1_wv_heads"] = wk_heads, wv_heads
    for name in ["L1_xattn_bv", "L0_attn_b_qkv", "L3_attn_bq", "L3_attn_bk"]:
        data[name + "_cols"] = np.ascontiguousarray(data[name].reshape(-1, P).T)
    rel = np.clip(np.arange(SEQ)[:, None] - np.arange(SEQ)[None, :] + 256, 0, 512)
    data["L0_rel"] = np.ascontiguousarray(np.tile(data["L0_attn_rel_bias"][rel].transpose(0, 2, 1), (PER_TILE, 1, 1)))
    data["head_of"] = np.repeat(np.eye(P // HD, dtype=np.float32), HD, axis=0)
    data["L0_ffn_up"] = np.concatenate([data["L0_ffn_w_gate"], data["L0_ffn_w_up"]], axis=0)
    for name in ["L2_attn_key_w", "L2_attn_vq_w", "L2_attn_out_w"]:
        data[name + "_T"] = turn(name)
    data["L2_attn_key_b_cols"] = np.ascontiguousarray(data["L2_attn_key_b"].reshape(-1, P).T)
    p = np.arange(P)
    same_head = p[:, None] // HD == p[None, :] // HD
    spread = same_head[:, None, :] & (p[:, None, None] % HD == np.arange(HD)[None, :, None])
    data["spread"] = np.ascontiguousarray(spread, dtype=np.float32)
    data["gather"] = np.ascontiguousarray(spread.transpose(2, 1, 0), dtype=np.float32)
    data["number"] = np.arange(512, dtype=np.float32)
    data["up_to"] = np.ascontiguousarray(np.stack([np.triu(np.ones((P, P), np.float32)), np.ones((P, P), np.float32)], axis=1))
    for name in ["L2_ffn_b1", "L3_ffn_b1"]:
        data[name + "_cols"] = np.ascontiguousarray(data[name].reshape(data[name].shape[0], -1, P).transpose(0, 2, 1))
    data["L3_xattn_Wk_T"] = np.pad(turn("L3_xattn_Wk"), ((0, 0), (0, 1)))
    for name in ["bq", "bk", "bv", "ln1_g", "ln1_b"]:
        data[f"L3_xattn_{name}_cols"] = np.ascontiguousarray(data[f"L3_xattn_{name}"].reshape(-1, P).T)

    nc = _bacc.Bacc("TRN2", target_bir_lowering=False, num_devices=1)
    arrays, dram = {}, {}
    for name, a in data.items():
        arrays[f"in_{name}"] = a
        dram[name] = nc.dram_tensor(f"in_{name}", a.shape, _mybir.dt.from_np(a.dtype), kind="ExternalInput").ap()
    out = nc.dram_tensor("out_0_dram", (BATCH, SEQ, D), F32, kind="ExternalOutput").ap()
    program(nc, dram, out, STAGES)
    r = _run(nc, [arrays], core_ids=[0])
    return r.results[0]["out_0_dram"]
```

```python
from contextlib import ExitStack

import numpy as np
import concourse.bass as bass
from concourse import mybir

ALU = mybir.AluOpType
ACT = mybir.ActivationFunctionType
F32 = mybir.dt.float32
F32R = mybir.dt.float32r
U32 = mybir.dt.uint32
BF16 = mybir.dt.bfloat16
AX = mybir.AxisListType

P = 128
BATCH, SEQ, D = 32, 32, 256
TOKENS = BATCH * SEQ
TILES = TOKENS // P
PER_TILE = P // SEQ
CD = D // P
HALF = 512
EPS = 1e-5
STAGES = list(range(12))


class Core:

    def __init__(self, nc, ctx, dram):
        self.nc, self.dram = nc, dram
        self.x = ctx.enter_context(nc.sbuf_tensor("x", [P, TILES, D], F32))
        self.xn = ctx.enter_context(nc.sbuf_tensor("xn", [P, TILES, D], F32))
        self.xnT = ctx.enter_context(nc.sbuf_tensor("xnT", [P, CD, TOKENS], F32))
        self.ident = ctx.enter_context(nc.sbuf_tensor("ident", [P, P], F32))
        self.ones = ctx.enter_context(nc.sbuf_tensor("ones", [1, HALF], F32))
        self.neghalf = ctx.enter_context(nc.sbuf_tensor("neghalf", [P, TILES], F32))
        self.bank = [ctx.enter_context(nc.psum_tensor(f"bank{i}", [P, 512], F32)) for i in range(8)]


class Stage:

    def __init__(self, core, ctx, name):
        self.core, self.ctx, self.name, self.sems = core, ctx, name, []
        ctx.callback(self.end)

    def end(self):
        self.core.nc.clear_and_free_semaphores(self.sems)
        self.core.nc.all_engine_barrier()

    def sb(self, name, shape, dt=F32):
        return self.ctx.enter_context(self.core.nc.sbuf_tensor(f"{self.name}_{name}", shape, dt))

    def sem(self, name):
        self.sems.append(self.core.nc.alloc_semaphore(f"{self.name}_{name}"))
        return self.sems[-1]


class Chain:

    def __init__(self, eng, sem, start=0):
        self.eng, self.sem, self.n, self.start = eng, sem, 0, start

    def __call__(self, instruction):
        self.n += 1
        instruction.then_inc(self.sem, 1)
        self.eng.wait_ge(self.sem, self.start + self.n)


class Norm:
    def __init__(self, st, twice=False):
        self.core, self.twice = st.core, twice
        self.stats = st.sb("ln_stats", [P, TILES, 6])
        self.mv = st.sb("ln_mv", [P, TILES, 2])
        self.veps = st.sb("ln_veps", [P, TILES])
        self.rstd = st.sb("ln_rstd", [P, TILES])
        self.stats_done = st.sem("ln_stats_done")
        self.mv_ready = st.sem("ln_mv_ready")
        self.veps_done = st.sem("ln_veps_done")
        self.rstd_ready = st.sem("ln_rstd_ready")
        self.xn_ready = st.sem("ln_xn_ready")
        self.turned = st.sem("ln_turned")
        self.xnT_ready = st.sem("ln_xnT_ready")

    def dve(self, dve):
        nc, xn = self.core.nc, self.core.xn
        for n in range(2 if self.twice else 1):
            x = xn if n else self.core.x
            for t in range(TILES):
                if n:
                    dve.wait_ge(self.xn_ready, t + 1)
                nc.vector.bn_stats(self.stats[:, t, :], x[:, t, :]).then_inc(self.stats_done, 1)
            if n:
                dve.wait_ge(self.xn_ready, TILES)
            for t in range(TILES):
                dve.wait_ge(self.stats_done, n * TILES + t + 1)
                nc.vector.bn_aggr(self.mv[:, t, :], self.stats[:, t, :]).then_inc(self.mv_ready, 1)
            dve.wait_ge(self.rstd_ready, n + 1)
            for t in range(TILES):
                nc.vector.tensor_scalar(xn[:, t, :], x[:, t, :], self.mv[:, t, 0:1], self.rstd[:, t:t + 1],
                                        ALU.subtract, ALU.mult).then_inc(self.xn_ready, 1)

    def pool(self, pool):
        nc = self.core.nc
        for n in range(2 if self.twice else 1):
            pool.wait_ge(self.mv_ready, (n + 1) * TILES)
            if n:
                pool.wait_ge(self.xn_ready, TILES)
            nc.gpsimd.tensor_scalar(self.veps[:, :], self.mv[:, :, 1], EPS, None, ALU.add).then_inc(self.veps_done, 1)
            pool.wait_ge(self.veps_done, n + 1)
            nc.gpsimd.tensor_tensor(self.rstd[:, :], self.veps[:, :], self.core.neghalf[:, :],
                                    ALU.pow).then_inc(self.rstd_ready, 1)

    def pe(self, pe):
        core = self.core
        for t in range(TILES):
            pe.wait_ge(self.xn_ready, (TILES if self.twice else 0) + t + 1)
            for c in range(CD):
                last = core.nc.tensor.transpose(core.bank[2 * (t // 4) + c][:, (t % 4) * P:(t % 4 + 1) * P],
                                                core.xn[:, t, c * P:(c + 1) * P], core.ident[:, :])
            if t % 4 == 3:
                last.then_inc(self.turned, 1)

    def act(self, act):
        core = self.core
        for g in range(TILES // 4):
            act.wait_ge(self.turned, g + 1)
            for c in range(CD):
                core.nc.scalar.copy(core.xnT[:, c, g * HALF:(g + 1) * HALF],
                                    core.bank[2 * g + c][:, :]).then_inc(self.xnT_ready, 1)


def stage_low_rank(core):
    nc, d = core.nc, core.dram
    with ExitStack() as ctx:
        st = Stage(core, ctx, "lowrank")
        ln = Norm(st)
        R = d["L1_ffn_V_r"].shape[1]
        wT = st.sb("wT", [P, CD, D])
        v = st.sb("v", [P, CD, R])
        cT = st.sb("cT", [R, D])
        b = st.sb("b", [1, D])
        xvT = st.sb("xvT", [R, TOKENS])
        loaded = st.sem("loaded")
        xv_done = st.sem("xv_done")
        xv_ready = st.sem("xv_ready")
        y_done = st.sem("y_done")
        x_done = st.sem("x_done")
        block = ctx.enter_context(nc.Block())

        @block.sync
        def _(sp):
            sp.dma_start(wT[:, :, :], d["L1_ffn_W_T"].rearrange("(c p) n -> p c n", p=P)).then_inc(loaded, 16)
            sp.dma_start(v[:, :, :], d["L1_ffn_V_r"].rearrange("(c p) n -> p c n", p=P)).then_inc(loaded, 16)
            sp.dma_start(cT[:, :], d["L1_ffn_C_T"]).then_inc(loaded, 16)
            sp.dma_start(b[:, :], d["L1_ffn_b"].rearrange("(a n) -> a n", a=1)).then_inc(loaded, 16)

        @block.gpsimd
        def _(pool):
            ln.pool(pool)

        @block.tensor
        def _(pe):
            ln.pe(pe)
            pe.wait_ge(loaded, 64)
            for n in range(2):
                pe.wait_ge(ln.xnT_ready, CD * (n + 1))
                for c in range(CD):
                    mm = nc.tensor.matmul(core.bank[4 + n][0:R, :], v[:, c, :],
                                          core.xnT[:, c, n * HALF:(n + 1) * HALF], start=(c == 0), stop=(c == CD - 1))
                mm.then_inc(xv_done, 1)
            for t in range(TILES):
                if t % 4 == 0:
                    pe.wait_ge(xv_ready, t // 4 + 1)
                if t >= 4:
                    pe.wait_ge(x_done, t - 3)
                y = core.bank[t % 4][:, 0:D]
                tok = slice(t * P, (t + 1) * P)
                for c in range(CD):
                    nc.tensor.matmul(y, core.xnT[:, c, tok], wT[:, c, :], start=(c == 0), stop=False)
                nc.tensor.matmul(y, xvT[:, tok], cT[:, :], start=False, stop=False)
                nc.tensor.matmul(y, core.ones[:, 0:P], b[:, :], start=False, stop=True).then_inc(y_done, 1)

        @block.scalar
        def _(act):
            ln.act(act)
            for n in range(2):
                act.wait_ge(xv_done, n + 1)
                nc.scalar.copy(xvT[:, n * HALF:(n + 1) * HALF], core.bank[4 + n][0:R, :]).then_inc(xv_ready, 1)

        @block.vector
        def _(dve):
            ln.dve(dve)
            for t in range(TILES):
                dve.wait_ge(y_done, t + 1)
                nc.vector.tensor_tensor(core.x[:, t, :], core.x[:, t, :], core.bank[t % 4][:, 0:D],
                                        ALU.add).then_inc(x_done, 1)


def stage_cross_attention(core, name, wq, wk, wv, wo, bo, biases, head_dim, clamp):
    nc, d = core.nc, core.dram
    HEADS, GROUP = 16, 4
    KV, CTX = d["ctx_768"].shape[1:]
    C1, C2 = P, CTX - P
    AUG = CTX + 1
    KE = KV + 1
    stacked = biases is None
    K2 = P if stacked else AUG - C1
    L2 = C2 if stacked else K2
    INNER = HEADS * head_dim
    QCH = INNER // P
    HPC = HEADS // QCH
    QM = QCH // 2
    SCALE = head_dim ** -0.5
    whole = head_dim % 32 == 0
    GROUPS = HEADS // GROUP
    CTX_LOADS = 3 if stacked else 2
    UNITS = PER_TILE * GROUPS
    RING = 4
    M_FILLS, OUT_FILLS = 1 + GROUPS, 3
    EXP, TURN, PV, SCALE_O, TURN_O = 1, 2, 3, 4, 5
    V_WHEN = [0, 1, 2, 3]
    V_STEP, WO_STEP = 5, 13
    with ExitStack() as ctx:
        st = Stage(core, ctx, name)
        ln = Norm(st)
        wq_s = st.sb("wq", [P, CD, INNER])
        wo_s = st.sb("wo", [P, QCH, D])
        bo_s = st.sb("bo", [1, D])
        wk_s = st.sb("wk", [P, QCH if whole else HEADS, 2 * P])
        if whole:
            wv1, wv2 = st.sb("wv1", [P, INNER]), st.sb("wv2", [C2, INNER])
        else:
            wv1, wv2 = st.sb("wv1", [P, HEADS, P]), st.sb("wv2", [C2, HEADS, P])
        if biases:
            bq_s = st.sb("bq", [1, INNER])
            bv_s = st.sb("bv", [P, QCH])
        ctxT1 = st.sb("ctxT1", [P, 2, KV])
        ctxT2 = st.sb("ctxT2", [K2, 2, KV])
        ctxN = st.sb("ctxN", [P, PER_TILE, 2, AUG])
        ctxT1_p = [st.sb(f"ctxT1_{n}", [P, PER_TILE, KE], F32R) for n in ("hi", "lo")]
        ctxT2_p = [st.sb(f"ctxT2_{n}", [rows, PER_TILE, KE], F32R) for n, rows in (("hi", K2), ("lo", L2))]
        ctx_last = st.sb("ctx_last", [P, PER_TILE, AUG])
        zeros = st.sb("zeros", [P, KV])
        qT = st.sb("qT", [P, QCH, P])
        qk1 = [st.sb(f"qk1_{n}", [P, 2, PER_TILE, HEADS, SEQ], F32R) for n in ("hi", "lo")]
        if stacked:
            qk2_both = st.sb("qk2", [P, 2, PER_TILE, HEADS, SEQ], F32R)
            qk2 = [qk2_both[0:C2], qk2_both[C2:P]]
        else:
            qk2 = [st.sb(f"qk2_{n}", [K2, 2, PER_TILE, HEADS, SEQ], F32R)[:] for n in ("hi", "lo")]
        negmax = st.sb("negmax", [P, RING])
        clamped = st.sb("clamped", [P, 2, KV]) if clamp else None
        probs = st.sb("probs", [P, RING, KV])
        probsT = st.sb("probsT", [P, RING, 2 * P])
        o_sum = st.sb("o_sum", [P, RING, AUG])
        rsum = st.sb("rsum", [P, RING])
        o_norm = st.sb("o_norm", [P, RING, CTX])
        oT1 = st.sb("oT1", [P, HEADS, PER_TILE, SEQ])
        oT2 = st.sb("oT2", [C2, HEADS, PER_TILE, SEQ])
        aT = st.sb("aT", [P, QCH, P])

        wq_loaded, wk_loaded = st.sem("wq_loaded"), st.sem("wk_loaded")
        wv_loaded, wo_loaded = st.sem("wv_loaded"), st.sem("wo_loaded")
        zeros_ready = st.sem("zeros_ready")
        ctx_hi_ready = st.sem("ctx_hi_ready")
        ctx_split = st.sem("ctx_split")
        qk_hi_ready = st.sem("qk_hi_ready")
        ctx_loaded = [st.sem(f"ctx_loaded{b}") for b in range(PER_TILE)]
        rows_loaded = [st.sem(f"rows_loaded{b}") for b in range(PER_TILE)]
        m0_filled, m0_free = st.sem("m0_filled"), st.sem("m0_free")
        m1_filled, m1_free = st.sem("m1_filled"), st.sem("m1_free")
        m2_filled, m2_free = st.sem("m2_filled"), st.sem("m2_free")
        scores_done = st.sem("scores_done")
        negmax_ready = st.sem("negmax_ready")
        clamp_done = st.sem("clamp_done")
        probs_ready = st.sem("probs_ready")
        turned = st.sem("turned")
        probsT_ready = st.sem("probsT_ready")
        pv_done = st.sem("pv_done")
        o_summed = st.sem("o_summed")
        rsum_ready = st.sem("rsum_ready")
        o_scaled = st.sem("o_scaled")
        o_turned = st.sem("o_turned")
        oT_ready = st.sem("oT_ready")
        banks = [b[:, :] for b in core.bank]
        SB, TB, OB, OT, M0, M1, M2 = banks[0:2], *banks[2:8]
        block = ctx.enter_context(nc.Block())

        def every_tile(eng, body):
            body(0, 0)
            with eng.Fori(0, TILES // 2 - 1) as i:
                for k in (1, 2):
                    body(i * 2 + k, k % 2)
            body(TILES - 1, 1)
            body(TILES, 0)

        def known(j, n):
            return isinstance(j, int) and j == n

        def wk_of(h, part):
            f = slice(part * P, (part + 1) * P)
            if whole:
                r = slice((h % HPC) * head_dim, (h % HPC + 1) * head_dim)
                return wk_s[r, h // HPC, f], qT[r, h // HPC, :]
            return wk_s[:, h, f], qT[:, h // HPC, :]

        def heads_of(g):
            return range(g // 2 * 8, g // 2 * 8 + 8)

        def qk_of(z, g, odd):
            hi_lo = [qk1[0][:], qk1[1][:]] if g % 2 == 0 else [qk2_both[:], qk2[1]] if stacked else qk2
            return [x[:, z, :, g // 2 * 8 + odd:g // 2 * 8 + 8:2, :] for x in hi_lo]

        def turned_heads(bank, g, lo=False):
            rows = slice(0, P) if g % 2 == 0 else slice(C2 if stacked and lo else 0, K2)
            return bank[rows, :].rearrange("p (j b q) -> p b j q", j=GROUP, q=SEQ)

        def steps_of(s, j):
            def at(lag):
                u = s - lag
                if u >= 0:
                    return None if known(j, TILES) else (j, u)
                return None if known(j, 0) else (j - 1, u + UNITS)
            return at

        @block.sync
        def _(sp):
            def load(i, b):
                n = bass.ds(i * PER_TILE + b, 1)
                T = d["ctxT"][n].rearrange("a c k -> c (a k)")
                sp.dma_start(ctxT1[:, b % 2, :], T[0:C1, :]).then_inc(ctx_loaded[b], 16)
                if stacked:
                    for r in range(2):
                        sp.dma_start(ctxT2[r * C2:(r + 1) * C2, b % 2, :], T[C1:CTX, :]).then_inc(ctx_loaded[b], 16)
                else:
                    sp.dma_start(ctxT2[:, b % 2, :], T[C1:AUG, :]).then_inc(ctx_loaded[b], 16)

            def load_rows(i, b):
                rows = d["ctxA"][bass.ds(i * PER_TILE + b, 1)]
                sp.dma_start(ctxN[:, b, :, :], rows[:, 0:2 * P, :].rearrange("a (c p) f -> p (a c) f", p=P)).then_inc(rows_loaded[b], 16)
                sp.dma_start(ctx_last[:, b, :], rows[:, 2 * P, :].rearrange("a f -> (a f)").partition_broadcast(P)).then_inc(rows_loaded[b], 16)

            sp.dma_start(wq_s[:, :, :], wq.rearrange("(c p) n -> p c n", p=P)).then_inc(wq_loaded, 16)
            if biases:
                sp.dma_start(bq_s[:, :], biases[0].rearrange("(a n) -> a n", a=1)).then_inc(wq_loaded, 16)
            sp.dma_start(wk_s[:, :, :], wk.rearrange("(c p) f -> p c f", p=P)).then_inc(wk_loaded, 16)
            for b in range(PER_TILE):
                if b >= 2:
                    sp.wait_ge(ctx_split, (b - 1) * 2)
                load(0, b)
                load_rows(0, b)
            sp.dma_start(wv1[:], wv[0:C1]).then_inc(wv_loaded, 16)
            sp.dma_start(wv2[:], wv[C1:CTX]).then_inc(wv_loaded, 16)
            if biases:
                sp.dma_start(bv_s[:, :], biases[1]).then_inc(wv_loaded, 16)
            sp.dma_start(wo_s[:, :, :], wo.rearrange("(c p) n -> p c n", p=P)).then_inc(wo_loaded, 16)
            sp.dma_start(bo_s[:, :], bo.rearrange("(a n) -> a n", a=1)).then_inc(wo_loaded, 16)
            with sp.Fori(1, TILES) as i:
                for b in range(PER_TILE):
                    sp.wait_ge(ctx_split, (i * PER_TILE + b - 1) * 2)
                    load(i, b)
                    sp.wait_ge(o_summed, (i - 1) * UNITS + GROUPS * (b + 1) + RING)
                    load_rows(i, b)

        @block.gpsimd
        def _(pool):
            ln.pool(pool)
            nc.gpsimd.memset(zeros[:, :], 0.0).then_inc(zeros_ready, 1)
            for part in [*ctxT1_p, *ctxT2_p]:
                nc.gpsimd.memset(part[:, :, KV:KE].bitcast(F32), 0.0)

            def split(i, b):
                pool.wait_ge(ctx_loaded[b], (i + 1) * 16 * CTX_LOADS)
                chunks = [(ctxT1[:, b % 2, :], *[x[:, b, 0:KV] for x in ctxT1_p]), (ctxT2[:, b % 2, :], *[x[:, b, 0:KV] for x in ctxT2_p])]
                for src, hi, lo in chunks:
                    nc.gpsimd.tensor_tensor(hi, src, zeros[0:src.shape[0], :], ALU.add).then_inc(ctx_hi_ready, 1)
                for n, (src, hi, lo) in enumerate(chunks):
                    pool.wait_ge(ctx_hi_ready, (i * PER_TILE + b) * 2 + n + 1)
                    nc.gpsimd.tensor_tensor(lo, src[0:lo.shape[0]], hi[0:lo.shape[0]], ALU.subtract).then_inc(ctx_split, 1)

            pool.wait_ge(zeros_ready, 1)
            for b in range(PER_TILE):
                split(0, b)
            with pool.Fori(1, TILES) as i:
                for b in range(PER_TILE):
                    pool.wait_ge(o_summed, (i - 1) * UNITS + GROUPS * (b + 1) + RING)
                    split(i, b)

        @block.tensor
        def _(pe):
            ln.pe(pe)
            pe.wait_ge(wq_loaded, 32 if biases else 16)
            pe.wait_ge(ln.xnT_ready, 2 * CD)

            def queries(j, m, chunks):
                bank, filled, free = [(M0, m0_filled, m0_free), (M1, m1_filled, m1_free)][m]
                for k in chunks:
                    ch = m * QM + k
                    if k == 0:
                        pe.wait_ge(free, j * M_FILLS + 1)
                    for c in range(CD):
                        mm = nc.tensor.matmul(bank[:, k * P:(k + 1) * P], wq_s[:, c, ch * P:(ch + 1) * P],
                                              core.xnT[:, c, bass.ds(j * P, P)], start=(c == 0), stop=(c == CD - 1 and not biases))
                    if biases:
                        mm = nc.tensor.matmul(bank[:, k * P:(k + 1) * P], bq_s[:, ch * P:(ch + 1) * P],
                                              core.ones[:, 0:P], start=False, stop=True)
                    if k == QM - 1:
                        mm.then_inc(filled, 1)

            def to_context(j, n):
                g, odd = divmod(n, 2)
                bank, filled, free = [(M0, m0_filled, m0_free), (M1, m1_filled, m1_free)][odd]
                if n == 0:
                    pe.wait_ge(wk_loaded, 16)
                    pe.wait_ge(m1_free, j * M_FILLS + 2)
                pe.wait_ge(free, j * M_FILLS + 2 + g)
                for k in range(GROUP):
                    w, q = wk_of(heads_of(g)[2 * k + odd], g % 2)
                    mm = nc.tensor.matmul(bank[:, k * P:(k + 1) * P], w, q, start=True, stop=True)
                mm.then_inc(filled, 1)

            def scores(j, z, u):
                b, g = divmod(u, GROUPS)
                if u == 0:
                    pe.wait_ge(m0_free, (j + 1) * M_FILLS + 1)
                    pe.wait_ge(m1_free, (j + 1) * M_FILLS + 1)
                if g == 0:
                    pe.wait_ge(ctx_split, (j * PER_TILE + b + 1) * 2)
                pe.wait_ge(probs_ready, j * UNITS + u + 1)
                out = SB[u % 2][:, 0:KE]
                unit = lambda qk: qk[:, z, b, g * GROUP:(g + 1) * GROUP, :]
                products = [(qk1[0], ctxT1_p[0]), (qk1[0], ctxT1_p[1]), (qk1[1], ctxT1_p[0])]
                if stacked:
                    products += [(qk2_both, ctxT2_p[0]), (qk2[0], ctxT2_p[1])]
                else:
                    products += [(qk2[0], ctxT2_p[0]), (qk2[0], ctxT2_p[1]), (qk2[1], ctxT2_p[0])]
                for n, (qk, T) in enumerate(products):
                    mm = nc.tensor.matmul(out, unit(qk), T[:, b, :], start=(n == 0), stop=(n == len(products) - 1))
                mm.then_inc(scores_done, 1)

            def turn_probs(j, u):
                pe.wait_ge(probs_ready, j * UNITS + u + 1 + 2)
                pe.wait_ge(probsT_ready, j * UNITS + u + 1)
                for c in range(2):
                    mm = nc.tensor.transpose(TB[:, c * P:(c + 1) * P], probs[:, u % RING, c * P:(c + 1) * P], core.ident[:, :])
                mm.then_inc(turned, 1)

            def probs_ctx(j, u):
                pe.wait_ge(probsT_ready, j * UNITS + u + 1 + 1)
                pe.wait_ge(o_summed, j * UNITS + u + RING)
                if u % GROUPS == 0:
                    pe.wait_ge(rows_loaded[u // GROUPS], (j + 1) * 32)
                for c in range(2):
                    mm = nc.tensor.matmul(OB[:, 0:AUG], probsT[:, u % RING, c * P:(c + 1) * P], ctxN[:, u // GROUPS, c, :],
                                          start=(c == 0), stop=(c == 1))
                mm.then_inc(pv_done, 1)

            def turn_out(j, u):
                pe.wait_ge(o_scaled, j * UNITS + u + 1 + RING)
                pe.wait_ge(oT_ready, (j * UNITS + u + 1) * 2)
                nc.tensor.transpose(OT[:, 0:P], o_norm[:, u % RING, 0:C1], core.ident[:, :])
                nc.tensor.transpose(OT[0:C2, P:2 * P], o_norm[:, u % RING, C1:CTX], core.ident[:, :]).then_inc(o_turned, 1)

            def values(j, m, heads):
                for h in heads:
                    k = h // HPC - m * QM
                    if h == m * HEADS // 2:
                        pe.wait_ge(wv_loaded, 48 if biases else 32)
                        pe.wait_ge(oT_ready, (j + 1) * UNITS * 2 + 2)
                        pe.wait_ge(m2_free, j * OUT_FILLS + m + 1)
                    if whole:
                        out = M2[(h % HPC) * head_dim:(h % HPC + 1) * head_dim, k * P:(k + 1) * P]
                        v1, v2 = wv1[:, h * head_dim:(h + 1) * head_dim], wv2[:, h * head_dim:(h + 1) * head_dim]
                        first = last = True
                    else:
                        out, v1, v2 = M2[:, k * P:(k + 1) * P], wv1[:, h, :], wv2[:, h, :]
                        first, last = h % HPC == 0, h % HPC == HPC - 1
                    nc.tensor.matmul(out, v1, oT1[:, h, :, :], start=first, stop=False)
                    mm = nc.tensor.matmul(out, v2, oT2[:, h, :, :], start=False, stop=last)
                    if h == (m + 1) * HEADS // 2 - 1:
                        mm.then_inc(m2_filled, 1)

            def project(j, part, parts):
                n = max(QCH // parts, 1)
                for c in range(part * n, min((part + 1) * n, QCH)):
                    if c == 0:
                        pe.wait_ge(wo_loaded, 32)
                        pe.wait_ge(m2_free, j * OUT_FILLS + 3)
                    nc.tensor.matmul(M2[:, 0:D], aT[:, c, :], wo_s[:, c, :], start=(c == 0), stop=False)
                    if c == QCH - 1:
                        nc.tensor.matmul(M2[:, 0:D], core.ones[:, 0:P], bo_s[:, :], start=False, stop=True).then_inc(m2_filled, 1)

            for m in range(2):
                queries(0, m, range(QM))
            for n in range(2 * GROUPS):
                to_context(0, n)

            def tile(j, z):
                for s in range(UNITS):
                    at = steps_of(s, j)
                    ahead = not known(j, TILES - 1) and not known(j, TILES)
                    behind = not known(j, 0)
                    if at(0):
                        scores(j, z, s)
                    if ahead and s < 4:
                        half = range(QM // 2) if s % 2 == 0 else range(QM // 2, QM)
                        queries(j + 1, s // 2, half)
                    if ahead and 4 <= s < 4 + 2 * GROUPS:
                        to_context(j + 1, s - 4)
                    if at(TURN):
                        turn_probs(*at(TURN))
                    if at(PV):
                        probs_ctx(*at(PV))
                    if behind and s - V_STEP in V_WHEN:
                        n = V_WHEN.index(s - V_STEP)
                        values(j - 1, n // 2, range(4 * n, 4 * n + 4))
                    if behind and WO_STEP <= s < WO_STEP + 2:
                        project(j - 1, s - WO_STEP, 2)
                    if at(TURN_O):
                        turn_out(*at(TURN_O))

            every_tile(pe, tile)

        @block.scalar
        def _(act):
            ln.act(act)
            act.sem_inc(m0_free, 1)
            act.sem_inc(m2_free, 1)
            act.sem_inc(probs_ready, 2)
            act.sem_inc(o_scaled, RING)
            act.sem_inc(o_turned, RING)
            act.sem_inc(oT_ready, 2)

            def queries(j):
                act.wait_ge(m0_filled, j * M_FILLS + 1)
                nc.scalar.mul(qT[:, 0:QM, :], M0[:, 0:QM * P].rearrange("p (j n) -> p j n", n=P), SCALE).then_inc(m0_free, 1)

            def to_context(j, z, g, odd):
                bank, filled = [(M0, m0_filled), (M1, m1_filled)][odd]
                act.wait_ge(filled, j * M_FILLS + 2 + g)
                nc.scalar.copy(qk_of(z, g, odd)[0], turned_heads(bank, g)).then_inc(qk_hi_ready, 1)

            def exp(j, u):
                act.wait_ge(negmax_ready, j * UNITS + u + 1)
                act.wait_ge(o_summed, j * UNITS + u + 1)
                src = clamped[:, u % 2, :] if clamp else SB[u % 2][:, 0:KV]
                nc.scalar.activation(probs[:, u % RING, :], src, ACT.Exp, bias=negmax[:, u % RING:u % RING + 1]).then_inc(probs_ready, 1)

            def scale_out(j, u):
                act.wait_ge(rsum_ready, j * UNITS + u + 1)
                act.wait_ge(o_turned, j * UNITS + u + 1)
                nc.scalar.mul(o_norm[:, u % RING, :], o_sum[:, u % RING, 0:CTX], rsum[:, u % RING:u % RING + 1]).then_inc(o_scaled, 1)

            def turned_out(j, u):
                b, g = divmod(u, GROUPS)
                heads = slice(g * GROUP, (g + 1) * GROUP)
                act.wait_ge(o_turned, j * UNITS + u + 1 + RING)
                nc.scalar.copy(oT1[:, heads, b, :], OT[:, 0:P].rearrange("p (h q) -> p h q", q=SEQ)).then_inc(oT_ready, 1)
                nc.scalar.copy(oT2[:, heads, b, :], OT[0:C2, P:2 * P].rearrange("p (h q) -> p h q", q=SEQ)).then_inc(oT_ready, 1)

            def values(j, m):
                if biases:
                    act.wait_ge(wv_loaded, 48)
                act.wait_ge(m2_filled, j * OUT_FILLS + m + 1)
                to, of = aT[:, m * QM:(m + 1) * QM, :], M2[:, 0:QM * P].rearrange("p (j n) -> p j n", n=P)
                if biases:
                    nc.scalar.activation(to, of, ACT.Identity, bias=bv_s[:, m:m + 1]).then_inc(m2_free, 1)
                else:
                    nc.scalar.copy(to, of).then_inc(m2_free, 1)

            queries(0)
            for n in range(2 * GROUPS):
                to_context(0, 0, n // 2, n % 2)

            def tile(j, z):
                for s in range(UNITS):
                    at = steps_of(s, j)
                    ahead = not known(j, TILES - 1) and not known(j, TILES)
                    behind = not known(j, 0)
                    if at(EXP):
                        exp(*at(EXP))
                    if at(SCALE_O):
                        scale_out(*at(SCALE_O))
                    if ahead and s == 1:
                        queries(j + 1)
                    if behind and s - V_STEP - 1 in (V_WHEN[1], V_WHEN[3]):
                        values(j - 1, V_WHEN.index(s - V_STEP - 1) // 2)
                    if ahead and 4 <= s < 4 + 2 * GROUPS:
                        to_context(j + 1, 1 - z, (s - 4) // 2, s % 2)
                    if at(TURN_O):
                        turned_out(*at(TURN_O))

            every_tile(act, tile)

        @block.vector
        def _(dve):
            ln.dve(dve)
            dve.sem_inc(m1_free, 1)
            dve.sem_inc(probsT_ready, 1)
            dve.sem_inc(o_summed, RING)

            def queries(j):
                dve.wait_ge(m1_filled, j * M_FILLS + 1)
                nc.vector.tensor_scalar(qT[:, QM:QCH, :], M1[:, 0:QM * P].rearrange("p (j n) -> p j n", n=P), SCALE, None,
                                        ALU.mult).then_inc(m1_free, 1)

            def to_context(j, z, g, odd):
                bank, free = [(M0, m0_free), (M1, m1_free)][odd]
                hi, lo = qk_of(z, g, odd)
                if stacked and g % 2:
                    hi = lo
                dve.wait_ge(qk_hi_ready, j * 2 * GROUPS + 2 * g + odd + 1)
                for b in range(PER_TILE):
                    done = nc.vector.tensor_tensor(lo[:, b], turned_heads(bank, g, lo=True)[:, b], hi[:, b], ALU.subtract)
                done.then_inc(free, 1)

            def largest(j, u):
                dve.wait_ge(scores_done, j * UNITS + u + 1)
                src = SB[u % 2][:, 0:KV]
                if clamp:
                    nc.vector.tensor_scalar(clamped[:, u % 2, :], src, -clamp, clamp, ALU.max, ALU.min).then_inc(clamp_done, 1)
                    dve.wait_ge(clamp_done, j * UNITS + u + 1)
                    src = clamped[:, u % 2, :]
                nc.vector.tensor_reduce(negmax[:, u % RING:u % RING + 1], src, AX.X, ALU.max, negate=True).then_inc(negmax_ready, 1)

            def turned_probs(j, u):
                dve.wait_ge(turned, j * UNITS + u + 1)
                nc.vector.tensor_copy(probsT[:, u % RING, :], TB[:, 0:2 * P]).then_inc(probsT_ready, 1)

            def sum_out(j, u):
                dve.wait_ge(pv_done, j * UNITS + u + 1)
                dve.wait_ge(o_scaled, j * UNITS + u + 1)
                nc.vector.scalar_tensor_tensor(o_sum[:, u % RING, :], ctx_last[:, u // GROUPS, :], probs[:, u % RING, KV - 1:KV],
                                               OB[:, 0:AUG], ALU.mult, ALU.add).then_inc(o_summed, 1)
                dve.wait_ge(o_summed, j * UNITS + u + 1 + RING)
                nc.vector.reciprocal(rsum[:, u % RING:u % RING + 1], o_sum[:, u % RING, CTX:CTX + 1]).then_inc(rsum_ready, 1)

            def add(j):
                dve.wait_ge(m2_filled, (j + 1) * OUT_FILLS)
                xi = core.x[:, bass.ds(j, 1), :].rearrange("p a n -> p (a n)")
                nc.vector.tensor_tensor(xi, xi, M2[:, 0:D], ALU.add).then_inc(m2_free, 1)

            queries(0)
            for n in range(2 * GROUPS):
                to_context(0, 0, n // 2, n % 2)

            def tile(j, z):
                for s in range(UNITS):
                    at = steps_of(s, j)
                    ahead = not known(j, TILES - 1) and not known(j, TILES)
                    behind = not known(j, 0)
                    if ahead and 5 <= s < 5 + 2 * GROUPS:
                        to_context(j + 1, 1 - z, (s - 5) // 2, 1 - s % 2)
                    if at(0):
                        largest(j, s)
                    if at(TURN):
                        turned_probs(*at(TURN))
                    if at(PV):
                        sum_out(*at(PV))
                    if ahead and s == 3:
                        queries(j + 1)
                    if behind and s == WO_STEP + 2:
                        add(j - 1)

            every_tile(dve, tile)


def stage_xattn0(core):
    d = core.dram
    stage_cross_attention(core, "xattn0", d["L0_xattn_Wq"], d["L0_xattn_Wk_T"], d["L0_xattn_Wv"], d["L0_xattn_Wo"],
                          d["L0_xattn_bo"], None, 64, None)


def stage_xattn1(core):
    d = core.dram
    stage_cross_attention(core, "xattn1", d["L1_xattn_Wq"], d["L1_wk_heads"], d["L1_wv_heads"], d["L1_xattn_Wo"],
                          d["L1_xattn_bo"], (d["L1_xattn_bq"], d["L1_xattn_bv_cols"]), 16, 10000.0)


def stage_xattn2(core):
    d = core.dram
    stage_cross_attention(core, "xattn2", d["L2_xattn_w_q"], d["L2_xattn_w_k_T"], d["L2_xattn_w_v"], d["L2_xattn_w_o"],
                          d["L2_xattn_b_o"], None, 64, None)


def stage_attn0(core):
    nc, d = core.nc, core.dram
    HEADS, HD = 16, 16
    HPC = P // HD
    SCALE = HD ** -0.5
    with ExitStack() as ctx:
        st = Stage(core, ctx, "attn0")
        ln = Norm(st)
        w = st.sb("w", [P, CD, 3 * D])
        wo = st.sb("wo", [P, CD, D])
        b_cols = st.sb("b_cols", [P, 6])
        bv = st.sb("bv", [1, D])
        bo = st.sb("bo", [1, D])
        rel = st.sb("rel", [P, HEADS, SEQ])
        head_of = st.sb("head_of", [P, HPC])
        qT = st.sb("qT", [P, CD, TOKENS])
        kT = st.sb("kT", [P, CD, TOKENS])
        v = st.sb("v", [P, TILES, D])
        k_heads = st.sb("k_heads", [P, 2, CD, PER_TILE, HPC, SEQ])
        s_rel = st.sb("s_rel", [P, 2, HEADS, SEQ])
        s_max = st.sb("s_max", [P, 2, HEADS])
        s_sub = st.sb("s_sub", [P, 2, HEADS, SEQ])
        probs = st.sb("probs", [P, 2, HEADS, SEQ])
        probsT = st.sb("probsT", [P, 2, HEADS, P])
        rsum = st.sb("rsum", [P, 2, HEADS])
        psum = st.sb("psum", [P, 2, HEADS])
        o = st.sb("o", [P, 2, D])
        oT = st.sb("oT", [P, 2, CD, P])
        loaded = st.sem("loaded")
        qk_done, qk_ready = st.sem("qk_done"), st.sem("qk_ready")
        v_done, v_ready = st.sem("v_done"), st.sem("v_ready")
        k0_ready, k1_ready = st.sem("k0_ready"), st.sem("k1_ready")
        scores_done = st.sem("scores_done")
        sub_ready = st.sem("sub_ready")
        probs_ready = st.sem("probs_ready")
        probsT_zero = st.sem("probsT_zero")
        probsT_ready = st.sem("probsT_ready")
        pv_done = st.sem("pv_done")
        o_ready = st.sem("o_ready")
        o_turned = st.sem("o_turned")
        oT_ready = st.sem("oT_ready")
        y_done = st.sem("y_done")
        x_done = st.sem("x_done")
        steps = st.sem("dve_steps")
        bank = [b[:, :] for b in core.bank]
        LOADS = 7
        block = ctx.enter_context(nc.Block())

        def spread_keys(eng, t, c):
            k = kT[:, c, t * P:(t + 1) * P].rearrange("p (b k) -> p b k", b=PER_TILE).unsqueeze(2)
            m = head_of[:, :].unsqueeze(1).unsqueeze(3)
            full = [P, PER_TILE, HPC, SEQ]
            return eng.tensor_tensor(k_heads[:, t % 2, c], k.broadcast_to(full), m.broadcast_to(full), ALU.mult)

        @block.sync
        def _(sp):
            sp.dma_start(w[:, :, :], d["L0_attn_W_qkv"].rearrange("(c p) n -> p c n", p=P)).then_inc(loaded, 16)
            sp.dma_start(wo[:, :, :], d["L0_attn_W_out"].rearrange("(c p) n -> p c n", p=P)).then_inc(loaded, 16)
            sp.dma_start(b_cols[:, :], d["L0_attn_b_qkv_cols"]).then_inc(loaded, 16)
            sp.dma_start(bv[:, :], d["L0_attn_b_qkv"][2 * D:3 * D].rearrange("(a n) -> a n", a=1)).then_inc(loaded, 16)
            sp.dma_start(bo[:, :], d["L0_attn_b_out"].rearrange("(a n) -> a n", a=1)).then_inc(loaded, 16)
            sp.dma_start(rel[:, :, :], d["L0_rel"]).then_inc(loaded, 16)
            sp.dma_start(head_of[:, :], d["head_of"]).then_inc(loaded, 16)

        @block.gpsimd
        def _(pool):
            ln.pool(pool)
            nc.gpsimd.memset(probsT[:, :, :, :], 0.0).then_inc(probsT_zero, 1)
            pool.wait_ge(loaded, 16 * LOADS)
            for t in range(TILES):
                pool.wait_ge(qk_ready, 4 if t < 4 else 8)
                if t >= 2:
                    pool.wait_ge(scores_done, t - 1)
                spread_keys(nc.gpsimd, t, 1).then_inc(k1_ready, 1)

        @block.tensor
        def _(pe):
            ln.pe(pe)
            pe.wait_ge(loaded, 16 * LOADS)
            for n in range(2):
                pe.wait_ge(ln.xnT_ready, CD * (n + 1))
                for f in range(4):
                    k = 4 * n + f
                    if k >= 2:
                        pe.wait_ge(qk_ready, k - 1)
                    for c in range(CD):
                        mm = nc.tensor.matmul(bank[4 + k % 2], w[:, c, f * P:(f + 1) * P], core.xnT[:, c, n * HALF:(n + 1) * HALF],
                                              start=(c == 0), stop=(c == CD - 1))
                    mm.then_inc(qk_done, 1)
                    if k >= 2:
                        pe.wait_ge(v_ready, k - 1)
                    out = bank[6 + k % 2][:, 0:D]
                    for c in range(CD):
                        nc.tensor.matmul(out, core.xnT[:, c, k * P:(k + 1) * P], w[:, c, 2 * D:3 * D], start=(c == 0), stop=False)
                    nc.tensor.matmul(out, core.ones[:, 0:P], bv[:, :], start=False, stop=True).then_inc(v_done, 1)
            pe.wait_ge(qk_ready, 8)
            pe.wait_ge(v_ready, 8)
            for s in range(TILES + 3):
                if s < TILES:
                    t = s
                    pe.wait_ge(k0_ready, t + 1)
                    pe.wait_ge(k1_ready, t + 1)
                    if t >= 2:
                        pe.wait_ge(sub_ready, t - 1)
                    for c in range(CD):
                        for b in range(PER_TILE):
                            q = qT[:, c, t * P + b * SEQ:t * P + (b + 1) * SEQ]
                            mm = nc.tensor.matmul(bank[t % 2][b * SEQ:(b + 1) * SEQ, c * D:(c + 1) * D], q, k_heads[:, t % 2, c, b],
                                                  start=True, stop=True, tile_position=(0, b * SEQ))
                    mm.then_inc(scores_done, 1)
                if 1 <= s <= TILES:
                    t = s - 1
                    pe.wait_ge(probsT_ready, t + 1)
                    if t >= 2:
                        pe.wait_ge(o_ready, t - 1)
                    for h in range(HEADS):
                        mm = nc.tensor.matmul(bank[2 + t % 2][:, h * HD:(h + 1) * HD], probsT[:, t % 2, h, :],
                                              v[:, t, h * HD:(h + 1) * HD], start=True, stop=True)
                    mm.then_inc(pv_done, 1)
                if 2 <= s <= TILES + 1:
                    t = s - 2
                    pe.wait_ge(o_ready, t + 1)
                    if t >= 2:
                        pe.wait_ge(oT_ready, t - 1)
                    for c in range(CD):
                        mm = nc.tensor.transpose(bank[4 + t % 2][:, c * P:(c + 1) * P], o[:, t % 2, c * P:(c + 1) * P], core.ident[:, :])
                    mm.then_inc(o_turned, 1)
                if s >= 3:
                    t = s - 3
                    pe.wait_ge(oT_ready, t + 1)
                    if t >= 2:
                        pe.wait_ge(x_done, t - 1)
                    y = bank[6 + t % 2][:, 0:D]
                    for c in range(CD):
                        nc.tensor.matmul(y, oT[:, t % 2, c, :], wo[:, c, :], start=(c == 0), stop=False)
                    nc.tensor.matmul(y, core.ones[:, 0:P], bo[:, :], start=False, stop=True).then_inc(y_done, 1)

        @block.scalar
        def _(act):
            ln.act(act)
            for t in range(TILES):
                act.wait_ge(v_done, t + 1)
                nc.scalar.copy(v[:, t, :], bank[6 + t % 2][:, 0:D]).then_inc(v_ready, 1)
            for s in range(TILES + 2):
                if s < TILES:
                    t = s
                    act.wait_ge(sub_ready, t + 1)
                    if t >= 2:
                        act.wait_ge(probsT_ready, t - 1)
                    nc.scalar.activation(probs[:, t % 2], s_sub[:, t % 2], ACT.Exp).then_inc(probs_ready, 1)
                if s >= 2:
                    t = s - 2
                    act.wait_ge(o_turned, t + 1)
                    if t >= 2:
                        act.wait_ge(y_done, t - 1)
                    nc.scalar.copy(oT[:, t % 2], bank[4 + t % 2][:, 0:D].rearrange("p (c n) -> p c n", c=CD)).then_inc(oT_ready, 1)

        @block.vector
        def _(dve):
            ln.dve(dve)
            step = Chain(dve, steps)
            dve.wait_ge(loaded, 16 * LOADS)
            for k in range(8):
                n, f = divmod(k, 4)
                dve.wait_ge(qk_done, k + 1)
                to = [qT, kT][f // 2][:, f % 2, n * HALF:(n + 1) * HALF]
                nc.vector.tensor_scalar(to, bank[4 + k % 2], b_cols[:, f:f + 1], SCALE if f < 2 else 1.0,
                                        ALU.add, ALU.mult).then_inc(qk_ready, 1)
            dve.wait_ge(qk_ready, 8)
            dve.wait_ge(probsT_zero, 1)
            for s in range(TILES + 3):
                if s < TILES:
                    t = s
                    if t >= 2:
                        dve.wait_ge(scores_done, t - 1)
                    spread_keys(nc.vector, t, 0).then_inc(k0_ready, 1)
                if 1 <= s <= TILES:
                    t = s - 1
                    z = t % 2
                    dve.wait_ge(scores_done, t + 1)
                    step(nc.vector.tensor_tensor(s_rel[:, z], bank[z].rearrange("p (h k) -> p h k", h=HEADS), rel[:, :, :], ALU.add))
                    step(nc.vector.tensor_reduce(s_max[:, z], s_rel[:, z], AX.X, ALU.max))
                    if t >= 2:
                        dve.wait_ge(probs_ready, t - 1)
                    nc.vector.tensor_tensor(s_sub[:, z], s_rel[:, z], s_max[:, z].unsqueeze(2).broadcast_to([P, HEADS, SEQ]),
                                            ALU.subtract).then_inc(sub_ready, 1)
                    dve.wait_ge(probs_ready, t + 1)
                    if t >= 2:
                        dve.wait_ge(pv_done, t - 1)
                    step(nc.vector.tensor_reduce(psum[:, z], probs[:, z], AX.X, ALU.add))
                    step(nc.vector.reciprocal(rsum[:, z], psum[:, z]))
                    for b in range(PER_TILE):
                        r = slice(b * SEQ, (b + 1) * SEQ)
                        last = nc.vector.transpose(probsT[r, z, :, r], probs[r, z])
                    last.then_inc(probsT_ready, 1)
                if 2 <= s <= TILES + 1:
                    t = s - 2
                    z = t % 2
                    dve.wait_ge(pv_done, t + 1)
                    if t >= 2:
                        dve.wait_ge(o_turned, t - 1)
                    nc.vector.tensor_tensor(o[:, z].rearrange("p (h e) -> p h e", h=HEADS),
                                            bank[2 + z][:, 0:D].rearrange("p (h e) -> p h e", h=HEADS),
                                            rsum[:, z].unsqueeze(2).broadcast_to([P, HEADS, HD]), ALU.mult).then_inc(o_ready, 1)
                if s >= 3:
                    t = s - 3
                    dve.wait_ge(y_done, t + 1)
                    nc.vector.tensor_tensor(core.x[:, t, :], core.x[:, t, :], bank[6 + t % 2][:, 0:D], ALU.add).then_inc(x_done, 1)


def stage_one_head(core, name, wq, wk, wv, wo, b_qk, bv, bo, gamma):
    nc, d = core.nc, core.dram
    soft_theta = gamma is None
    with ExitStack() as ctx:
        st = Stage(core, ctx, name)
        ln = Norm(st)
        w = st.sb("w", [P, CD, 3 * D])
        qT = st.sb("qT", [P, CD, TOKENS])
        kT = st.sb("kT", [P, CD, TOKENS])
        v = st.sb("v", [P, TILES, D])
        sub = st.sb("sub", [P, TILES, SEQ])
        smax = st.sb("smax", [P, TILES])
        probs = st.sb("probs", [P, TILES, SEQ])
        psum = st.sb("psum", [P, TILES])
        rsum = st.sb("rsum", [P, TILES])
        probsT = st.sb("probsT", [P, TILES, P])
        loaded = st.sem("loaded")
        qk_done, qk_ready = st.sem("qk_done"), st.sem("qk_ready")
        v_done, v_ready = st.sem("v_done"), st.sem("v_ready")
        scores_done = st.sem("scores_done")
        sub_ready = st.sem("sub_ready")
        probs_ready = st.sem("probs_ready")
        probsT_zero = st.sem("probsT_zero")
        probsT_ready = st.sem("probsT_ready")
        pv_done = st.sem("pv_done")
        x_done = st.sem("x_done")
        steps = st.sem("dve_steps")
        if soft_theta:
            wo_s, bo_s, bv_s, b_s = st.sb("wo", [P, CD, D]), st.sb("bo", [1, D]), st.sb("bv", [1, D]), st.sb("b", [P, 2 * CD])
            th_half, th_full = st.sb("th_half", [P, TILES * SEQ]), st.sb("th_full", [P, TILES * SEQ])
            relu, theta = st.sb("relu", [P, TILES * SEQ]), st.sb("theta", [P, TILES * SEQ])
            o, oT = st.sb("o", [P, 2, D]), st.sb("oT", [P, 2, CD, P])
            tanh_ready, o_ready, o_turned = st.sem("tanh_ready"), st.sem("o_ready"), st.sem("o_turned")
            oT_ready, y_done = st.sem("oT_ready"), st.sem("y_done")
            LOADS = 8
        else:
            gamma_s, x_plus, rgamma = st.sb("gamma", [P, 1]), st.sb("x_plus", [P, TILES, D]), st.sb("rgamma", [P, TILES])
            x_plus_ready = st.sem("x_plus_ready")
            LOADS = 4
        bank = [b[:, :] for b in core.bank]
        S = bank[0][:, 0:TILES * SEQ]
        block = ctx.enter_context(nc.Block())

        @block.sync
        def _(sp):
            for n, m in enumerate([wq, wk, wv]):
                sp.dma_start(w[:, :, n * D:(n + 1) * D], m.rearrange("(c p) n -> p c n", p=P)).then_inc(loaded, 16)
            if soft_theta:
                sp.dma_start(wo_s[:, :, :], wo.rearrange("(c p) n -> p c n", p=P)).then_inc(loaded, 16)
                sp.dma_start(bo_s[:, :], bo.rearrange("(a n) -> a n", a=1)).then_inc(loaded, 16)
                sp.dma_start(bv_s[:, :], bv.rearrange("(a n) -> a n", a=1)).then_inc(loaded, 16)
                for n in range(2):
                    sp.dma_start(b_s[:, n * CD:(n + 1) * CD], b_qk[n]).then_inc(loaded, 16)
            else:
                sp.dma_start(gamma_s[:, :], gamma.partition_broadcast(P)).then_inc(loaded, 16)

        @block.gpsimd
        def _(pool):
            ln.pool(pool)
            nc.gpsimd.memset(probsT[:, :, :], 0.0).then_inc(probsT_zero, 1)
            if not soft_theta:
                pool.wait_ge(ln.xn_ready, TILES)
                nc.gpsimd.tensor_tensor(x_plus[:, :, :], core.x[:, :, :], core.xn[:, :, :], ALU.add).then_inc(x_plus_ready, 1)

        @block.tensor
        def _(pe):
            ln.pe(pe)
            pe.wait_ge(loaded, 16 * LOADS)
            for n in range(2):
                pe.wait_ge(ln.xnT_ready, CD * (n + 1))
                for f in range(4):
                    k = 4 * n + f
                    if k >= 2:
                        pe.wait_ge(qk_ready, k - 1)
                    for c in range(CD):
                        mm = nc.tensor.matmul(bank[4 + k % 2], w[:, c, f * P:(f + 1) * P], core.xnT[:, c, n * HALF:(n + 1) * HALF],
                                              start=(c == 0), stop=(c == CD - 1))
                    mm.then_inc(qk_done, 1)
                    if k >= 2:
                        pe.wait_ge(v_ready, k - 1)
                    out = bank[6 + k % 2][:, 0:D]
                    for c in range(CD):
                        mm = nc.tensor.matmul(out, core.xnT[:, c, k * P:(k + 1) * P], w[:, c, 2 * D:3 * D], start=(c == 0),
                                              stop=(c == CD - 1 and not soft_theta))
                    if soft_theta:
                        mm = nc.tensor.matmul(out, core.ones[:, 0:P], bv_s[:, :], start=False, stop=True)
                    mm.then_inc(v_done, 1)
            pe.wait_ge(qk_ready, 8)
            pe.wait_ge(v_ready, 8)
            for t in range(TILES):
                for c in range(CD):
                    for b in range(PER_TILE):
                        own = slice(t * P + b * SEQ, t * P + (b + 1) * SEQ)
                        mm = nc.tensor.matmul(S[b * SEQ:(b + 1) * SEQ, t * SEQ:(t + 1) * SEQ], qT[:, c, own], kT[:, c, own],
                                              start=(c == 0), stop=(c == CD - 1), tile_position=(0, b * SEQ))
            mm.then_inc(scores_done, 1)
            pe.wait_ge(probsT_ready, 1)
            for s in range(TILES + (2 if soft_theta else 0)):
                if s < TILES:
                    t = s
                    if t >= 2:
                        pe.wait_ge(o_ready if soft_theta else x_done, t - 1)
                    nc.tensor.matmul(bank[2 + t % 2][:, 0:D], probsT[:, t, :], v[:, t, :], start=True, stop=True).then_inc(pv_done, 1)
                if soft_theta and 1 <= s <= TILES:
                    t = s - 1
                    pe.wait_ge(o_ready, t + 1)
                    if t >= 2:
                        pe.wait_ge(oT_ready, t - 1)
                    for c in range(CD):
                        mm = nc.tensor.transpose(bank[4 + t % 2][:, c * P:(c + 1) * P], o[:, t % 2, c * P:(c + 1) * P], core.ident[:, :])
                    mm.then_inc(o_turned, 1)
                if soft_theta and s >= 2:
                    t = s - 2
                    pe.wait_ge(oT_ready, t + 1)
                    if t >= 2:
                        pe.wait_ge(x_done, t - 1)
                    y = bank[6 + t % 2][:, 0:D]
                    for c in range(CD):
                        nc.tensor.matmul(y, oT[:, t % 2, c, :], wo_s[:, c, :], start=(c == 0), stop=False)
                    nc.tensor.matmul(y, core.ones[:, 0:P], bo_s[:, :], start=False, stop=True).then_inc(y_done, 1)

        @block.scalar
        def _(act):
            ln.act(act)
            for t in range(TILES):
                act.wait_ge(v_done, t + 1)
                nc.scalar.copy(v[:, t, :], bank[6 + t % 2][:, 0:D]).then_inc(v_ready, 1)
            if soft_theta:
                act.wait_ge(scores_done, 1)
                nc.scalar.activation(th_half[:, :], S, ACT.Tanh, scale=0.5).then_inc(tanh_ready, 1)
                nc.scalar.activation(th_full[:, :], S, ACT.Tanh).then_inc(tanh_ready, 1)
            act.wait_ge(sub_ready, 1)
            nc.scalar.activation(probs[:, :, :], sub[:, :, :], ACT.Exp).then_inc(probs_ready, 1)
            if soft_theta:
                for t in range(TILES):
                    act.wait_ge(o_turned, t + 1)
                    if t >= 2:
                        act.wait_ge(y_done, t - 1)
                    nc.scalar.copy(oT[:, t % 2], bank[4 + t % 2][:, 0:D].rearrange("p (c n) -> p c n", c=CD)).then_inc(oT_ready, 1)

        @block.vector
        def _(dve):
            ln.dve(dve)
            step = Chain(dve, steps)
            dve.wait_ge(loaded, 16 * LOADS)
            for k in range(8):
                n, f = divmod(k, 4)
                dve.wait_ge(qk_done, k + 1)
                to = [qT, kT][f // 2][:, f % 2, n * HALF:(n + 1) * HALF]
                if soft_theta:
                    nc.vector.tensor_scalar(to, bank[4 + k % 2], b_s[:, f:f + 1], None, ALU.add).then_inc(qk_ready, 1)
                else:
                    nc.vector.tensor_copy(to, bank[4 + k % 2]).then_inc(qk_ready, 1)
            dve.wait_ge(scores_done, 1)
            logits = S
            if soft_theta:
                dve.wait_ge(tanh_ready, 2)
                step(nc.vector.tensor_scalar(relu[:, :], S, 0.0, 0.1, ALU.max, ALU.mult))
                step(nc.vector.tensor_scalar(theta[:, :], th_half[:, :], 0.1, 0.6, ALU.mult, ALU.add))
                step(nc.vector.scalar_tensor_tensor(theta[:, :], th_full[:, :], 0.15, theta[:, :], ALU.mult, ALU.add))
                step(nc.vector.tensor_tensor(theta[:, :], theta[:, :], relu[:, :], ALU.add))
                logits = theta[:, :]
            logits = logits.rearrange("p (t k) -> p t k", t=TILES)
            step(nc.vector.tensor_reduce(smax[:, :], logits, AX.X, ALU.max))
            nc.vector.tensor_tensor(sub[:, :, :], logits, smax[:, :].unsqueeze(2).broadcast_to([P, TILES, SEQ]),
                                    ALU.subtract).then_inc(sub_ready, 1)
            dve.wait_ge(probs_ready, 1)
            dve.wait_ge(probsT_zero, 1)
            for b in range(PER_TILE):
                r = slice(b * SEQ, (b + 1) * SEQ)
                last = nc.vector.transpose(probsT[r, :, r], probs[r, :, :])
            last.then_inc(probsT_ready, 1)
            step(nc.vector.tensor_reduce(psum[:, :], probs[:, :, :], AX.X, ALU.add))
            step(nc.vector.reciprocal(rsum[:, :], psum[:, :]))
            if not soft_theta:
                step(nc.vector.tensor_scalar(rgamma[:, :], rsum[:, :], gamma_s[:, 0:1], None, ALU.mult))
                dve.wait_ge(x_plus_ready, 1)
                for t in range(TILES):
                    dve.wait_ge(pv_done, t + 1)
                    nc.vector.scalar_tensor_tensor(core.x[:, t, :], bank[2 + t % 2][:, 0:D], rgamma[:, t:t + 1], x_plus[:, t, :],
                                                   ALU.mult, ALU.add).then_inc(x_done, 1)
                return
            for s in range(TILES + 2):
                if s < TILES:
                    t = s
                    dve.wait_ge(pv_done, t + 1)
                    if t >= 2:
                        dve.wait_ge(o_turned, t - 1)
                    nc.vector.tensor_scalar(o[:, t % 2], bank[2 + t % 2][:, 0:D], rsum[:, t:t + 1], None, ALU.mult).then_inc(o_ready, 1)
                if s >= 2:
                    t = s - 2
                    dve.wait_ge(y_done, t + 1)
                    nc.vector.tensor_tensor(core.x[:, t, :], core.x[:, t, :], bank[6 + t % 2][:, 0:D], ALU.add).then_inc(x_done, 1)


def stage_attn1(core):
    d = core.dram
    stage_one_head(core, "attn1", d["L1_attn_Wk_T"], d["L1_attn_Wq_T"], d["L1_attn_Wv_T"], None, None, None, None, d["L1_attn_gamma"])


def stage_attn3(core):
    d = core.dram
    stage_one_head(core, "attn3", d["L3_attn_Wq_T"], d["L3_attn_Wk_T"], d["L3_attn_Wv_T"], d["L3_attn_Wo_T"],
                   (d["L3_attn_bq_cols"], d["L3_attn_bk_cols"]), d["L3_attn_bv"], d["L3_attn_bo"], None)


class Fp4:
    BLOCK = 16
    SIXTH = 1.0 / 6.0

    def __init__(self, st, n):
        self.nc, blocks = st.core.nc, n // self.BLOCK
        self.amax, self.scale = st.sb("fp4_amax", [P, blocks]), st.sb("fp4_scale", [P, blocks])
        self.rscale, self.half = st.sb("fp4_rscale", [P, blocks]), st.sb("fp4_half", [P, blocks])
        self.mag = st.sb("fp4_mag", [P, n])
        self.high, self.low = st.sb("fp4_high", [P, n], BF16), st.sb("fp4_low", [P, n], BF16)

    def __call__(self, dve, step, src, size, sign, sign_ready, item, out, n):
        nc, blocks = self.nc, n // self.BLOCK
        by_block = lambda a: a.rearrange("p (k i) -> p k i", i=self.BLOCK)
        wide = lambda a: a[:, 0:blocks].unsqueeze(2).broadcast_to([P, blocks, self.BLOCK])
        mag, high, low = self.mag[:, 0:n], self.high[:, 0:n], self.low[:, 0:n]
        step(nc.vector.tensor_reduce(self.amax[:, 0:blocks], by_block(src), AX.X, ALU.max, apply_absolute_value=True))
        step(nc.vector.tensor_scalar(self.scale[:, 0:blocks], self.amax[:, 0:blocks], self.SIXTH, 1e-12, ALU.mult, ALU.max))
        step(nc.vector.reciprocal(self.rscale[:, 0:blocks], self.scale[:, 0:blocks]))
        step(nc.vector.tensor_scalar(self.half[:, 0:blocks], self.scale[:, 0:blocks], 0.5, None, ALU.mult))
        dve.wait_ge(sign_ready, 2 * item + 1)
        step(nc.vector.tensor_tensor(by_block(mag), by_block(size), wide(self.rscale), ALU.mult))
        step(nc.vector.tensor_scalar(high, mag, 5.0, 2.0, ALU.is_gt, ALU.mult))
        step(nc.vector.scalar_tensor_tensor(high, mag, 3.5, high, ALU.is_gt, ALU.add))
        step(nc.vector.scalar_tensor_tensor(high, mag, 2.5, high, ALU.is_gt, ALU.add))
        step(nc.vector.tensor_scalar(low, mag, 1.75, None, ALU.is_gt))
        for mid in (1.25, 0.75, 0.25):
            step(nc.vector.scalar_tensor_tensor(low, mag, mid, low, ALU.is_gt, ALU.add))
        step(nc.vector.scalar_tensor_tensor(high, high, 2.0, low, ALU.mult, ALU.add))
        dve.wait_ge(sign_ready, 2 * item + 2)
        step(nc.vector.tensor_tensor(low, high, sign, ALU.mult))
        return nc.vector.tensor_tensor(by_block(out), by_block(low), wide(self.half), ALU.mult)


def stage_fp4_ffn(core):
    nc, d = core.nc, core.dram
    FF = d["L0_ffn_w_gate"].shape[0]
    WG = 2 * FF // P
    WN = WG * D
    FCH = -(-FF // P)
    LAST = FF - (FCH - 1) * P
    HN = FF // 2
    XN = TILES // 2 * D
    with ExitStack() as ctx:
        st = Stage(core, ctx, "fp4")
        ln = Norm(st)
        fp4 = Fp4(st, max(FF * 2, XN))
        w = st.sb("w", [P, WN + CD * FF])
        w_size = st.sb("w_size", [P, WN + CD * FF])
        w_sign = st.sb("w_sign", [P, WN + CD * FF], BF16)
        x_size = st.sb("x_size", [P, TILES * D])
        x_sign = st.sb("x_sign", [P, TILES * D], BF16)
        wguT = st.sb("wguT", [P, CD, 2 * FF])
        wdT = st.sb("wdT", [P, FCH, D])
        xqT = st.sb("xqT", [P, CD, TOKENS])
        gated = st.sb("gated", [P, FF])
        h = st.sb("h", [P, FF])
        h_size = st.sb("h_size", [P, FF])
        h_sign = st.sb("h_sign", [P, FF], BF16)
        hq = st.sb("hq", [P, 2, FF])
        hT = st.sb("hT", [P, 2, FCH, P])
        loaded = st.sem("loaded")
        w_sign_ready, x_sign_ready, h_sign_ready = st.sem("w_sign_ready"), st.sem("x_sign_ready"), st.sem("h_sign_ready")
        wq_ready, xq_ready, hq_ready = st.sem("wq_ready"), st.sem("xq_ready"), st.sem("hq_ready")
        turned, turned_ready = st.sem("turned"), st.sem("turned_ready")
        gu_done, silu_ready, h_ready = st.sem("gu_done"), st.sem("silu_ready"), st.sem("h_ready")
        h_turned, hT_ready = st.sem("h_turned"), st.sem("hT_ready")
        y_done, x_done = st.sem("y_done"), st.sem("x_done")
        steps = st.sem("dve_steps")
        bank = [b[:, :] for b in core.bank]
        w_up = w[:, 0:WN].rearrange("p (j k) -> p j k", k=D)
        w_down = w[:, WN:].rearrange("p (j k) -> p j k", k=FF)
        WCHUNK = FF * 2
        WCHUNKS = (WN + CD * FF) // WCHUNK

        jobs = []
        for g in range(TILES // 4):
            for c in range(CD):
                jobs.append(([core.xn[:, t, c * P:(c + 1) * P] for t in range(4 * g, 4 * g + 4)], xqT[:, c, g * HALF:(g + 1) * HALF], P))
        XJOBS = len(jobs)
        for c in range(CD):
            for j in range(0, WG, 4):
                e = min(j + 4, WG)
                jobs.append(([w_up[:, k, c * P:(c + 1) * P] for k in range(j, e)], wguT[:, c, j * P:e * P], P))
        for k in range(FCH):
            r = P if k < FCH - 1 else LAST
            jobs.append(([w_down[:, j, k * P:k * P + r] for j in range(CD)], wdT[0:r, k, :], r))
        block = ctx.enter_context(nc.Block())

        @block.sync
        def _(sp):
            sp.dma_start(w_up[:, :, :], d["L0_ffn_up"].rearrange("(j p) k -> p j k", p=P)).then_inc(loaded, 16)
            sp.dma_start(w_down[:, :, :], d["L0_ffn_w_down"].rearrange("(j p) k -> p j k", p=P)).then_inc(loaded, 16)

        @block.gpsimd
        def _(pool):
            ln.pool(pool)

        @block.tensor
        def _(pe):
            for n, (sources, to, rows) in enumerate(jobs):
                if n == 0:
                    pe.wait_ge(xq_ready, 2)
                if n == XJOBS:
                    pe.wait_ge(wq_ready, WCHUNKS)
                if n >= 2:
                    pe.wait_ge(turned_ready, n - 1)
                for k, source in enumerate(sources):
                    mm = nc.tensor.transpose(bank[6 + n % 2][0:rows, k * P:(k + 1) * P], source, core.ident[:, :])
                mm.then_inc(turned, 1)
            pe.wait_ge(turned_ready, len(jobs))
            for s in range(TILES + 2):
                if s < TILES:
                    t = s
                    if t >= 1:
                        pe.wait_ge(silu_ready, 2 * t)
                        pe.wait_ge(h_ready, t)
                    for k in range(4):
                        for c in range(CD):
                            mm = nc.tensor.matmul(bank[k][:, 0:HN], xqT[:, c, t * P:(t + 1) * P], wguT[:, c, k * HN:(k + 1) * HN],
                                                  start=(c == 0), stop=(c == CD - 1))
                    mm.then_inc(gu_done, 1)
                if 1 <= s <= TILES:
                    t = s - 1
                    pe.wait_ge(hq_ready, t + 1)
                    if t >= 1:
                        pe.wait_ge(hT_ready, 2 * t)
                    for k in range(FCH):
                        r = P if k < FCH - 1 else LAST
                        mm = nc.tensor.transpose(bank[5 + k // 4][0:r, (k % 4) * P:(k % 4 + 1) * P], hq[:, t % 2, k * P:k * P + r], core.ident[:, :])
                    mm.then_inc(h_turned, 1)
                if s >= 2:
                    t = s - 2
                    pe.wait_ge(hT_ready, 2 * (t + 1))
                    if t >= 2:
                        pe.wait_ge(x_done, t - 1)
                    y = bank[4 if t % 2 == 0 else 7][:, 0:D]
                    for k in range(FCH):
                        r = P if k < FCH - 1 else LAST
                        mm = nc.tensor.matmul(y, hT[0:r, t % 2, k, :], wdT[0:r, k, :], start=(k == 0), stop=(k == FCH - 1))
                    mm.then_inc(y_done, 1)

        @block.scalar
        def _(act):
            act.wait_ge(loaded, 32)
            nc.scalar.activation(w_size[:, :], w[:, :], ACT.Abs).then_inc(w_sign_ready, 1)
            nc.scalar.sign(w_sign[:, :], w[:, :]).then_inc(w_sign_ready, 1)
            act.wait_ge(ln.xn_ready, TILES)
            flat = core.xn[:, :, :].rearrange("p t k -> p (t k)")
            nc.scalar.activation(x_size[:, :], flat, ACT.Abs).then_inc(x_sign_ready, 1)
            nc.scalar.sign(x_sign[:, :], flat).then_inc(x_sign_ready, 1)
            for n, (sources, to, rows) in enumerate(jobs):
                act.wait_ge(turned, n + 1)
                nc.scalar.copy(to, bank[6 + n % 2][0:rows, 0:len(sources) * P]).then_inc(turned_ready, 1)
            for s in range(TILES + 1):
                if s < TILES:
                    t = s
                    act.wait_ge(gu_done, t + 1)
                    if t >= 1:
                        act.wait_ge(h_ready, t)
                    for k in range(2):
                        nc.scalar.activation(gated[:, k * HN:(k + 1) * HN], bank[k][:, 0:HN], ACT.Silu).then_inc(silu_ready, 1)
                if s >= 1:
                    t = s - 1
                    act.wait_ge(h_turned, t + 1)
                    if t >= 2:
                        act.wait_ge(y_done, t - 1)
                    nc.scalar.copy(hT[:, t % 2, 0:4, :], bank[5].rearrange("p (k n) -> p k n", k=4)).then_inc(hT_ready, 1)
                    for k in range(4, FCH):
                        r = P if k < FCH - 1 else LAST
                        cp = nc.scalar.copy(hT[0:r, t % 2, k, :], bank[6][0:r, (k % 4) * P:(k % 4 + 1) * P])
                    cp.then_inc(hT_ready, 1)
                if s < TILES:
                    act.wait_ge(h_ready, s + 1)
                    nc.scalar.activation(h_size[:, :], h[:, :], ACT.Abs).then_inc(h_sign_ready, 1)
                    nc.scalar.sign(h_sign[:, :], h[:, :]).then_inc(h_sign_ready, 1)

        @block.vector
        def _(dve):
            step = Chain(dve, steps)
            ln.dve(dve)
            dve.wait_ge(ln.xn_ready, TILES)
            flat = core.xn[:, :, :].rearrange("p t k -> p (t k)")
            for k in range(2):
                r = slice(k * XN, (k + 1) * XN)
                step(fp4(dve, step, flat[:, r], x_size[:, r], x_sign[:, r], x_sign_ready, 0, flat[:, r], XN))
                dve.sem_inc(xq_ready, 1)
            dve.wait_ge(loaded, 32)
            for k in range(WCHUNKS):
                r = slice(k * WCHUNK, (k + 1) * WCHUNK)
                step(fp4(dve, step, w[:, r], w_size[:, r], w_sign[:, r], w_sign_ready, 0, w[:, r], WCHUNK))
                dve.sem_inc(wq_ready, 1)
            for s in range(TILES + 2):
                if s < TILES:
                    t = s
                    dve.wait_ge(silu_ready, 2 * (t + 1))
                    if t >= 1:
                        dve.wait_ge(h_sign_ready, 2 * t)
                    for k in range(2):
                        mul = nc.vector.tensor_tensor(h[:, k * HN:(k + 1) * HN], gated[:, k * HN:(k + 1) * HN], bank[2 + k][:, 0:HN], ALU.mult)
                        if k == 1:
                            mul.then_inc(h_ready, 1)
                    dve.wait_ge(h_ready, t + 1)
                    if t >= 2:
                        dve.wait_ge(h_turned, t - 1)
                    fp4(dve, step, h[:, :], h_size[:, :], h_sign[:, :], h_sign_ready, t, hq[:, t % 2, :], FF).then_inc(hq_ready, 1)
                    dve.wait_ge(hq_ready, t + 1)
                if s >= 2:
                    t = s - 2
                    dve.wait_ge(y_done, t + 1)
                    yb = bank[4 if t % 2 == 0 else 7][:, 0:D]
                    nc.vector.tensor_tensor(core.x[:, t, :], core.x[:, t, :], yb, ALU.add).then_inc(x_done, 1)


def stage_scan(core):
    nc, d = core.nc, core.dram
    HD = 16
    HALVES = CD * 2
    RING = 2
    with ExitStack() as ctx:
        st = Stage(core, ctx, "scan")
        ln = Norm(st)
        w = st.sb("w", [P, CD, 3 * D])
        wo = st.sb("wo", [P, CD, D])
        bk = st.sb("bk", [P, CD])
        bo = st.sb("bo", [1, D])
        spread = st.sb("spread", [P, HD, P])
        gather = st.sb("gather", [P, HD, P])
        decay = st.sb("decay", [P, CD * TOKENS])
        rest = st.sb("rest", [P, CD * TOKENS])
        vT = st.sb("vT", [P, CD * TOKENS])
        qT = st.sb("qT", [P, CD * TOKENS])
        q_now = st.sb("q_now", [P, HALF])
        update = st.sb("update", [P, RING, HALF])
        state = st.sb("state", [P, RING, HALF])
        product = st.sb("product", [P, RING, HALF])
        hT = st.sb("hT", [P, CD, TOKENS])
        loaded = st.sem("loaded")
        k_done, k_ready, rest_ready, decay_ready = st.sem("k_done"), st.sem("k_ready"), st.sem("rest_ready"), st.sem("decay_ready")
        vq_done, vq_ready = st.sem("vq_done"), st.sem("vq_ready")
        spread_done, update_ready = st.sem("spread_done"), st.sem("update_ready")
        state_ready = st.sem("state_ready")
        product_ready = st.sem("product_ready")
        gathered = st.sem("gathered")
        hT_ready = st.sem("hT_ready")
        q_now_ready = st.sem("q_now_ready")
        y_done, x_done = st.sem("y_done"), st.sem("x_done")
        bank = [b[:, :] for b in core.bank]
        block = ctx.enter_context(nc.Block())

        @block.sync
        def _(sp):
            sp.dma_start(w[:, :, 0:D], d["L2_attn_key_w_T"].rearrange("(c p) n -> p c n", p=P)).then_inc(loaded, 16)
            sp.dma_start(w[:, :, D:3 * D], d["L2_attn_vq_w_T"].rearrange("(c p) n -> p c n", p=P)).then_inc(loaded, 16)
            sp.dma_start(bk[:, :], d["L2_attn_key_b_cols"]).then_inc(loaded, 16)
            sp.dma_start(bo[:, :], d["L2_attn_out_b"].rearrange("(a n) -> a n", a=1)).then_inc(loaded, 16)
            sp.dma_start(spread[:, :, :], d["spread"]).then_inc(loaded, 16)
            sp.dma_start(gather[:, :, :], d["gather"]).then_inc(loaded, 16)
            sp.dma_start(wo[:, :, :], d["L2_attn_out_w_T"].rearrange("(c p) n -> p c n", p=P)).then_inc(loaded, 16)

        @block.gpsimd
        def _(pool):
            ln.pool(pool)
            pool.sem_inc(product_ready, RING)
            with pool.Fori(0, HALVES) as i:
                pool.wait_ge(q_now_ready, i + 1)
                for e in range(HD):
                    pool.wait_ge(state_ready, i * HD + e + 1)
                    pool.wait_ge(gathered, i * HD + e + 1)
                    nc.gpsimd.tensor_tensor(product[:, e % RING, :], state[:, e % RING, :], q_now[:, :], ALU.mult).then_inc(product_ready, 1)

        @block.tensor
        def _(pe):
            ln.pe(pe)
            pe.wait_ge(loaded, 16 * 7)
            for n in range(2):
                pe.wait_ge(ln.xnT_ready, CD * (n + 1))
                for f in range(6):
                    if f < 2:
                        k, done, ready, b0 = 2 * n + f, k_done, k_ready, 4
                    else:
                        k, done, ready, b0 = 4 * n + f - 2, vq_done, vq_ready, 6
                    if k >= 2:
                        pe.wait_ge(ready, k - 1)
                    for c in range(CD):
                        mm = nc.tensor.matmul(bank[b0 + k % 2], w[:, c, f * P:(f + 1) * P], core.xnT[:, c, n * HALF:(n + 1) * HALF],
                                              start=(c == 0), stop=(c == CD - 1))
                    mm.then_inc(done, 1)
            pe.wait_ge(vq_ready, 8)
            with pe.Fori(0, HALVES) as i:
                now = bass.ds(i * HALF, HALF)
                for e in range(HD + 2):
                    if e < HD:
                        pe.wait_ge(update_ready, i * HD + e + 1)
                        nc.tensor.matmul(bank[e % 2], spread[:, e, :], vT[:, now], start=True, stop=True).then_inc(spread_done, 1)
                    if e == 2:
                        pe.wait_ge(hT_ready, i + 1)
                    if e >= 2:
                        pe.wait_ge(product_ready, i * HD + e - 2 + 1 + RING)
                        nc.tensor.matmul(bank[2], gather[:, e - 2, :], product[:, (e - 2) % RING, :], start=(e == 2),
                                         stop=(e == HD + 1)).then_inc(gathered, 1)
            pe.wait_ge(hT_ready, HALVES + 1)
            for t in range(TILES):
                if t >= 4:
                    pe.wait_ge(x_done, t - 3)
                y = bank[4 + t % 4][:, 0:D]
                for c in range(CD):
                    nc.tensor.matmul(y, hT[:, c, t * P:(t + 1) * P], wo[:, c, :], start=(c == 0), stop=False)
                nc.tensor.matmul(y, core.ones[:, 0:P], bo[:, :], start=False, stop=True).then_inc(y_done, 1)

        @block.scalar
        def _(act):
            ln.act(act)
            act.sem_inc(gathered, RING)
            act.sem_inc(hT_ready, 1)
            act.wait_ge(loaded, 16 * 7)
            for n in range(2):
                for c in range(CD):
                    act.wait_ge(k_done, 2 * n + c + 1)
                    at = c * TOKENS + n * HALF
                    nc.scalar.activation(decay[:, at:at + HALF], bank[4 + c], ACT.Sigmoid, bias=bk[:, c:c + 1]).then_inc(k_ready, 1)
                for f in range(4):
                    act.wait_ge(vq_done, 4 * n + f + 1)
                    at = (f % 2) * TOKENS + n * HALF
                    nc.scalar.copy([vT, qT][f // 2][:, at:at + HALF], bank[6 + f % 2]).then_inc(vq_ready, 1)
            act.wait_ge(vq_ready, 8)
            with act.Fori(0, HALVES) as i:
                act.wait_ge(product_ready, i * HD + RING)
                nc.scalar.copy(q_now[:, :], qT[:, bass.ds(i * HALF, HALF)]).then_inc(q_now_ready, 1)
                act.wait_ge(gathered, (i + 1) * HD + RING)
                nc.scalar.copy(hT[:, :, :].rearrange("p c n -> p (c n)")[:, bass.ds(i * HALF, HALF)], bank[2]).then_inc(hT_ready, 1)

        @block.vector
        def _(dve):
            ln.dve(dve)
            dve.sem_inc(update_ready, 2)
            dve.wait_ge(k_ready, 2 * CD)
            nc.vector.tensor_scalar(rest[:, :], decay[:, :], -1.0, 1.0, ALU.mult, ALU.add).then_inc(rest_ready, 1)
            dve.wait_ge(rest_ready, 1)
            nc.vector.memset(decay[:, :].rearrange("p (b s) -> p b s", s=SEQ)[:, :, 0:1], 0.0).then_inc(decay_ready, 1)
            dve.wait_ge(decay_ready, 1)
            with dve.Fori(0, HALVES) as i:
                now = bass.ds(i * HALF, HALF)
                for e in range(HD):
                    dve.wait_ge(spread_done, i * HD + e + 1)
                    nc.vector.tensor_tensor(update[:, e % RING, :], rest[:, now], bank[e % 2], ALU.mult).then_inc(update_ready, 1)
                    dve.wait_ge(update_ready, i * HD + e + 1 + 2)
                    dve.wait_ge(product_ready, i * HD + e + 1)
                    nc.vector.tensor_tensor_scan(state[:, e % RING, :], decay[:, now], update[:, e % RING, :], 0.0,
                                                 ALU.mult, ALU.add).then_inc(state_ready, 1)
            for t in range(TILES):
                dve.wait_ge(y_done, t + 1)
                nc.vector.tensor_tensor(core.x[:, t, :], core.x[:, t, :], bank[4 + t % 4][:, 0:D], ALU.add).then_inc(x_done, 1)


class Gate:

    def __init__(self, st, experts, wg, bg, logits):
        self.core, self.E, self.wg_dram, self.bg_dram, self.logits = st.core, experts, wg, bg, logits
        full = [P, TILES, experts]
        self.wg, self.bg = st.sb("gate_w", [P, CD, experts]), st.sb("gate_b", [1, experts])
        self.number = st.sb("gate_number", [P, experts])
        self.sub, self.probs, self.mask = st.sb("gate_sub", full), st.sb("gate_probs", full), st.sb("gate_mask", full)
        self.second, self.weight = st.sb("gate_second", full), st.sb("gate_weight", full)
        self.most, self.total = st.sb("gate_most", [P, TILES]), st.sb("gate_total", [P, TILES])
        self.top, self.index = st.sb("gate_top", [P, TILES, 8]), st.sb("gate_index", [P, TILES, 8], U32)
        self.place = st.sb("gate_place", [P, TILES, 8])
        self.loaded = st.sem("gate_loaded")
        self.logits_done, self.sub_ready = st.sem("gate_logits_done"), st.sem("gate_sub_ready")
        self.exp_ready, self.ready = st.sem("gate_exp_ready"), st.sem("gate_ready")

    def sp(self, sp):
        sp.dma_start(self.wg[:, :, :], self.wg_dram.rearrange("(c p) e -> p c e", p=P)).then_inc(self.loaded, 16)
        sp.dma_start(self.bg[:, :], self.bg_dram.rearrange("(a e) -> a e", a=1)).then_inc(self.loaded, 16)
        sp.dma_start(self.number[:, :], self.core.dram["number"][0:self.E].partition_broadcast(P)).then_inc(self.loaded, 16)

    def pe(self, pe):
        core, nc = self.core, self.core.nc
        pe.wait_ge(self.loaded, 48)
        for t in range(TILES):
            out = self.logits[:, t * self.E:(t + 1) * self.E]
            for c in range(CD):
                nc.tensor.matmul(out, core.xnT[:, c, t * P:(t + 1) * P], self.wg[:, c, :], start=(c == 0), stop=False)
            mm = nc.tensor.matmul(out, core.ones[:, 0:P], self.bg[:, :], start=False, stop=True)
        mm.then_inc(self.logits_done, 1)

    def act(self, act):
        act.wait_ge(self.sub_ready, 1)
        self.core.nc.scalar.activation(self.probs[:, :, :], self.sub[:, :, :], ACT.Exp).then_inc(self.exp_ready, 1)

    def dve(self, dve, step):
        nc, full = self.core.nc, [P, TILES, self.E]
        by_token = lambda a: a.unsqueeze(2).broadcast_to(full)
        dve.wait_ge(self.loaded, 48)
        dve.wait_ge(self.logits_done, 1)
        logits = self.logits.rearrange("p (t e) -> p t e", t=TILES)
        step(nc.vector.tensor_reduce(self.most[:, :], logits, AX.X, ALU.max))
        nc.vector.tensor_tensor(self.sub[:, :, :], logits, by_token(self.most[:, :]), ALU.subtract).then_inc(self.sub_ready, 1)
        dve.wait_ge(self.exp_ready, 1)
        step(nc.vector.tensor_reduce(self.total[:, :], self.probs[:, :, :], AX.X, ALU.add))
        step(nc.vector.reciprocal(self.total[:, :], self.total[:, :]))
        step(nc.vector.tensor_tensor(self.probs[:, :, :], self.probs[:, :, :], by_token(self.total[:, :]), ALU.mult))
        for t in range(TILES):
            step(nc.vector.max(self.top[:, t, :], self.probs[:, t, :]))
        for t in range(TILES):
            step(nc.vector.max_index(self.index[:, t, :], self.top[:, t, :], self.probs[:, t, :]))
        step(nc.vector.tensor_copy(self.place[:, :, :], self.index[:, :, :]))
        number = self.number[:, :].unsqueeze(1).broadcast_to(full)
        step(nc.vector.tensor_tensor(self.mask[:, :, :], number, by_token(self.place[:, :, 0]), ALU.is_equal))
        step(nc.vector.tensor_tensor(self.second[:, :, :], number, by_token(self.place[:, :, 1]), ALU.is_equal))
        step(nc.vector.tensor_tensor(self.mask[:, :, :], self.mask[:, :, :], self.second[:, :, :], ALU.add))
        step(nc.vector.tensor_tensor(self.weight[:, :, :], self.probs[:, :, :], self.mask[:, :, :], ALU.mult))
        step(nc.vector.tensor_reduce(self.total[:, :], self.weight[:, :, :], AX.X, ALU.add))
        step(nc.vector.tensor_scalar(self.total[:, :], self.total[:, :], 1e-12, None, ALU.max))
        step(nc.vector.reciprocal(self.total[:, :], self.total[:, :]))
        step(nc.vector.tensor_tensor(self.weight[:, :, :], self.weight[:, :, :], by_token(self.total[:, :]), ALU.mult))
        dve.sem_inc(self.ready, 1)


def stage_moe_capacity(core):
    nc, d = core.nc, core.dram
    E, _, FF = d["L2_ffn_w1"].shape
    TOP = 2
    RING = 4
    CAPACITY = int(1.25 * TOKENS / E)
    SLOTS = E * CAPACITY
    FCH = FF // P
    PARTS = 2
    HC = CAPACITY // PARTS
    with ExitStack() as ctx:
        st = Stage(core, ctx, "moecap")
        ln = Norm(st)
        bank = [b[:, :] for b in core.bank]
        UP, XT, YT, YO = bank[0:4], bank[4], bank[5], bank[6]
        gate = Gate(st, E, d["L2_ffn_gate_w"], d["L2_ffn_gate_b"], bank[6][:, 0:TILES * E])
        xin = nc.dram_tensor("moecap_xin", (SLOTS + TOP * TOKENS, D), F32, kind="Internal").ap()
        y = nc.dram_tensor("moecap_y", (SLOTS + P, D), F32, kind="Internal").ap()
        w1, w2 = st.sb("w1", [P, RING, CD, FF]), st.sb("w2", [P, RING, FCH, D])
        b1, b2 = st.sb("b1", [P, RING, FCH]), st.sb("b2", [P, RING, CD])
        up_to = st.sb("up_to", [P, 2, P])
        number, row = st.sb("number", [P, TOP * TILES]), st.sb("row", [P, 1])
        zeros = st.sb("zeros", [P, D])
        before = st.sb("before", [P, TILES, E])
        first, keep, chosen = st.sb("first", [P, TILES, E]), st.sb("keep", [P, TILES, E]), st.sb("chosen", [P, TILES, E])
        start = st.sb("start", [P, E])
        all_slots, kept_weight = st.sb("all_slots", [P, TILES, E]), st.sb("kept_weight", [P, TILES, E])
        slot, slot_u = st.sb("slot", [P, TOP, TILES]), st.sb("slot_u", [P, TOP, TILES], U32)
        found, own = st.sb("found", [P, TOP, TILES]), st.sb("own", [P, TOP, TILES])
        from_u = st.sb("from_u", [P, TOP, TILES], U32)
        share = st.sb("share", [P, TOP, TILES])
        x_slots = st.sb("x_slots", [HC, 2, PARTS, D])
        xinT = st.sb("xinT", [P, 2, CD, CAPACITY])
        hT = st.sb("hT", [P, 2, FCH, CAPACITY])
        yT = st.sb("yT", [P, 2, CD, CAPACITY])
        y_slots = st.sb("y_slots", [HC, 2, PARTS, D])
        mine = [core.xn[:, :, :], core.xnT[:, :, :].rearrange("p c (t f) -> p (c t) f", f=D)]
        loaded = st.sem("loaded")
        w_loaded = [st.sem(f"w_loaded{k}") for k in range(RING)]
        zeros_ready, cleared = st.sem("zeros_ready"), st.sem("cleared")
        before_ready, ranked, slots_ready = st.sem("before_ready"), st.sem("ranked"), st.sem("slots_ready")
        from_ready = st.sem("from_ready")
        scattered = st.sem("scattered")
        x_loaded = [st.sem(f"x_loaded{k}") for k in range(2)]
        x_turned = st.sem("x_turned")
        xT_ready = st.sem("xT_ready")
        up_done = st.sem("up_done")
        hT_ready = st.sem("hT_ready")
        down_done = st.sem("down_done")
        yT_ready = st.sem("yT_ready")
        y_turned = st.sem("y_turned")
        y_copied = st.sem("y_copied")
        y_written = [st.sem(f"y_written{k}") for k in range(2)]
        brought = [st.sem(f"brought{t}") for t in range(TILES)]
        added = st.sem("added")
        steps = st.sem("dve_steps")
        block = ctx.enter_context(nc.Block())

        def every_group(eng, body):
            with eng.Fori(0, E // RING) as i:
                for s in range(RING + 2):
                    body(i, s)

        @block.sync
        def _(sp):
            gate.sp(sp)
            sp.dma_start(up_to[:, :, :], d["up_to"]).then_inc(loaded, 16)
            sp.dma_start(number[:, :], d["number"][0:TOP * TILES].partition_broadcast(P)).then_inc(loaded, 16)
            sp.dma_start(row[:, :], d["number"][0:P].rearrange("(p a) -> p a", a=1)).then_inc(loaded, 16)
            sp.wait_ge(zeros_ready, 1)
            sp.dma_start(xin[0:SLOTS, :].rearrange("(n p) f -> p n f", p=P),
                         zeros[:, :].unsqueeze(1).broadcast_to([P, SLOTS // P, D])).then_inc(cleared, 16)
            sp.dma_start(y[SLOTS:SLOTS + P, :], zeros[:, :]).then_inc(cleared, 16)

            def load(e, k):
                e = bass.ds(e, 1)
                sp.dma_start(w1[:, k], d["L2_ffn_w1"][e].rearrange("a (c p) f -> p (a c) f", p=P)).then_inc(w_loaded[k], 16)
                sp.dma_start(w2[:, k], d["L2_ffn_w2"][e].rearrange("a (c p) n -> p (a c) n", p=P)).then_inc(w_loaded[k], 16)
                sp.dma_start(b1[:, k], d["L2_ffn_b1_cols"][e].rearrange("a p f -> p (a f)")).then_inc(w_loaded[k], 16)
                sp.dma_start(b2[:, k], d["L2_ffn_b2_cols"][e].rearrange("a p f -> p (a f)")).then_inc(w_loaded[k], 16)

            def write(n, z):
                sp.wait_ge(y_copied, n + 2)
                sp.dma_start(y[bass.ds(n * CAPACITY, CAPACITY), :].rearrange("(a p) f -> p a f", p=HC),
                             y_slots[:, z, :, :]).then_inc(y_written[z], 16)

            for k in range(RING):
                load(k, k)
            with sp.Fori(0, E // RING - 1) as i:
                for k in range(RING):
                    sp.wait_ge(yT_ready, i * RING + k + 2)
                    load((i + 1) * RING + k, k)
                    write(i * RING + k, k % 2)
            for k in range(RING):
                write(E - RING + k, k % 2)

        @block.gpsimd
        def _(pool):
            nc.gpsimd.memset(zeros[:, :], 0.0).then_inc(zeros_ready, 1)
            ln.pool(pool)
            pool.wait_ge(cleared, 32)
            pool.wait_ge(slots_ready, 1)
            pool.wait_ge(ln.xn_ready, TILES)
            for t in range(TILES):
                for k in range(TOP):
                    nc.gpsimd.indirect_dma_start(xin, bass.IndirectOffsetOnAxis(ap=slot_u[:, k, t:t + 1], axis=0),
                                                 core.xn[:, t, :], None).then_inc(scattered, 16)
            pool.wait_ge(scattered, TILES * TOP * 16)

            def load(i, k):
                rows = xin[bass.ds((i * 2 + k) * CAPACITY, CAPACITY), :]
                pool.dma_start(x_slots[:, k, :, :], rows.rearrange("(a p) f -> p a f", p=HC)).then_inc(x_loaded[k], 16)

            for k in range(2):
                load(0, k)
            with pool.Fori(1, E // 2) as i:
                for k in range(2):
                    pool.wait_ge(x_turned, i * 2 + k - 1)
                    load(i, k)
            pool.wait_ge(from_ready, 1)
            for k in range(2):
                pool.wait_ge(y_written[k], (E // 2 + 1) * 16)
            for t in range(TILES):
                for k in range(TOP):
                    nc.gpsimd.indirect_dma_start(mine[k][:, t, :], None, y,
                                                 bass.IndirectOffsetOnAxis(ap=from_u[:, k, t:t + 1], axis=0)).then_inc(brought[t], 16)

        @block.tensor
        def _(pe):
            ln.pe(pe)
            pe.wait_ge(ln.xnT_ready, 2 * CD)
            gate.pe(pe)
            pe.wait_ge(loaded, 48)
            pe.wait_ge(before_ready, 1)
            rank = bank[7][:, 0:TILES * E]
            nc.tensor.matmul(rank, up_to[:, 0, :], gate.mask[:, :, :], start=True, stop=False)
            nc.tensor.matmul(rank, up_to[:, 1, :], before[:, :, :], start=False, stop=True).then_inc(ranked, 1)

            def turn_x(i, k):
                n, z = i * RING + k, k % 2
                pe.wait_ge(x_loaded[z], (i * (RING // 2) + k // 2) * 16 + 16)
                pe.wait_ge(xT_ready, n + 1)
                for c in range(CD):
                    for a in range(PARTS):
                        o = (c * PARTS + a) * HC
                        mm = nc.tensor.transpose(XT[:, o:o + HC], x_slots[:, z, a, c * P:(c + 1) * P], core.ident[0:HC, 0:HC])
                mm.then_inc(x_turned, 1)

            def up(i, k):
                n, z = i * RING + k, k % 2
                pe.wait_ge(w_loaded[k], i * 64 + 64)
                pe.wait_ge(xT_ready, n + 2)
                for f in range(FCH):
                    pe.wait_ge(hT_ready, n * FCH + f + 1)
                    for c in range(CD):
                        mm = nc.tensor.matmul(UP[f % 4][:, 0:CAPACITY], w1[:, k, c, f * P:(f + 1) * P], xinT[:, z, c, :],
                                              start=(c == 0), stop=(c == CD - 1))
                    mm.then_inc(up_done, 1)

            def down(i, k):
                n, z = i * RING + k, k % 2
                pe.wait_ge(hT_ready, (n + 1) * FCH + 4)
                pe.wait_ge(yT_ready, n + 1)
                for c in range(CD):
                    for f in range(FCH):
                        mm = nc.tensor.matmul(YT[:, c * CAPACITY:(c + 1) * CAPACITY], w2[:, k, f, c * P:(c + 1) * P], hT[:, z, f, :],
                                              start=(f == 0), stop=(f == FCH - 1))
                mm.then_inc(down_done, 1)

            def turn_y(i, k):
                n, z = i * RING + k, k % 2
                pe.wait_ge(yT_ready, n + 2)
                pe.wait_ge(y_copied, n + 1)
                for a in range(PARTS):
                    for c in range(CD):
                        o = a * D + c * P
                        mm = nc.tensor.transpose(YO[0:HC, o:o + P], yT[:, z, c, a * HC:(a + 1) * HC], core.ident[:, :])
                mm.then_inc(y_turned, 1)

            def step(i, s):
                if s == 0:
                    turn_x(i, 0)
                if s < RING:
                    up(i, s)
                if s < RING - 1:
                    turn_x(i, s + 1)
                if s >= 2:
                    turn_y(i, s - 2)
                if 1 <= s <= RING:
                    down(i, s - 1)

            every_group(pe, step)

        @block.scalar
        def _(act):
            ln.act(act)
            gate.act(act)
            act.sem_inc(xT_ready, 1)
            act.sem_inc(up_done, 2 * FCH)
            act.sem_inc(hT_ready, 4)
            act.sem_inc(down_done, 2)

            def turned_x(i, k):
                n, z = i * RING + k, k % 2
                act.wait_ge(x_turned, n + 1)
                act.wait_ge(up_done, (n + 1) * FCH)
                nc.scalar.copy(xinT[:, z, :, :], XT[:, 0:CD * CAPACITY].rearrange("p (c n) -> p c n", c=CD)).then_inc(xT_ready, 1)

            def hidden(i, k):
                n, z = i * RING + k, k % 2
                act.wait_ge(w_loaded[k], i * 64 + 64)
                act.wait_ge(down_done, n + 1)
                for f in range(FCH):
                    act.wait_ge(up_done, (n + 2) * FCH + f + 1)
                    nc.scalar.activation(hT[:, z, f, :], UP[f % 4][:, 0:CAPACITY], ACT.Relu, bias=b1[:, k, f:f + 1]).then_inc(hT_ready, 1)

            def step(i, s):
                if s == 0:
                    turned_x(i, 0)
                if s < RING:
                    hidden(i, s)
                if s < RING - 1:
                    turned_x(i, s + 1)

            every_group(act, step)

        @block.vector
        def _(dve):
            ln.dve(dve)
            step = Chain(dve, steps)
            gate.dve(dve, step)
            tiles = [P, TILES, E]
            step(nc.vector.memset(before[:, 0, :], 0.0))
            for t in range(1, TILES):
                add = nc.vector.tensor_tensor(before[:, t, :], before[:, t - 1, :], gate.mask[:, t - 1, :], ALU.add)
                if t < TILES - 1:
                    step(add)
            add.then_inc(before_ready, 1)
            step(nc.vector.tensor_tensor(first[:, :, :], gate.mask[:, :, :], gate.second[:, :, :], ALU.subtract))
            dve.wait_ge(loaded, 48)
            step(nc.vector.tensor_scalar(row[:, :], row[:, :], float(SLOTS), None, ALU.add))
            step(nc.vector.tensor_scalar(own[:, :, :].rearrange("p k t -> p (k t)"), number[:, :], float(P), row[:, 0:1], ALU.mult, ALU.add))
            step(nc.vector.tensor_scalar(start[:, :], number[:, 0:E], float(CAPACITY), -1.0, ALU.mult, ALU.add))
            dve.wait_ge(ranked, 1)
            rank = bank[7][:, 0:TILES * E].rearrange("p (t e) -> p t e", t=TILES)
            step(nc.vector.scalar_tensor_tensor(keep[:, :, :], rank, float(CAPACITY), gate.mask[:, :, :], ALU.is_le, ALU.mult))
            step(nc.vector.tensor_tensor(all_slots[:, :, :], rank, start[:, :].unsqueeze(1).broadcast_to(tiles), ALU.add))
            for k, picked in enumerate([first, gate.second]):
                step(nc.vector.tensor_tensor(chosen[:, :, :], keep[:, :, :], picked[:, :, :], ALU.mult))
                step(nc.vector.tensor_reduce(found[:, k, :], chosen[:, :, :], AX.X, ALU.add))
                step(nc.vector.tensor_tensor(chosen[:, :, :], chosen[:, :, :], all_slots[:, :, :], ALU.mult))
                step(nc.vector.tensor_reduce(slot[:, k, :], chosen[:, :, :], AX.X, ALU.add))
            step(nc.vector.tensor_tensor(found[:, :, :], found[:, :, :], own[:, :, :], ALU.mult))
            step(nc.vector.tensor_tensor(own[:, :, :], own[:, :, :], found[:, :, :], ALU.subtract))
            step(nc.vector.tensor_tensor(slot[:, :, :], slot[:, :, :], own[:, :, :], ALU.add))
            step(nc.vector.tensor_copy(slot_u[:, :, :], slot[:, :, :]))
            dve.sem_inc(slots_ready, 1)
            step(nc.vector.tensor_scalar(slot[:, :, :], slot[:, :, :], row[:, 0:1], None, ALU.min))
            step(nc.vector.tensor_copy(from_u[:, :, :], slot[:, :, :]))
            step(nc.vector.tensor_tensor(kept_weight[:, :, :], gate.weight[:, :, :], keep[:, :, :], ALU.mult))
            for k, picked in enumerate([first, gate.second]):
                step(nc.vector.tensor_tensor(chosen[:, :, :], kept_weight[:, :, :], picked[:, :, :], ALU.mult))
                step(nc.vector.tensor_reduce(share[:, k, :], chosen[:, :, :], AX.X, ALU.add))
            dve.sem_inc(from_ready, 1)
            dve.sem_inc(yT_ready, 1)
            dve.sem_inc(y_turned, 2)
            dve.sem_inc(y_copied, 1)
            for k in range(2):
                dve.sem_inc(y_written[k], 16)

            def results(i, k):
                n, z = i * RING + k, k % 2
                dve.wait_ge(w_loaded[k], i * 64 + 64)
                dve.wait_ge(y_turned, n + 1)
                dve.wait_ge(down_done, n + 3)
                for c in range(CD):
                    bias = nc.vector.tensor_scalar(yT[:, z, c, :], YT[:, c * CAPACITY:(c + 1) * CAPACITY], b2[:, k, c:c + 1], None, ALU.add)
                bias.then_inc(yT_ready, 1)

            def turned_results(i, k):
                n, z = i * RING + k, k % 2
                dve.wait_ge(y_written[z], (i * (RING // 2) + k // 2) * 16 + 16)
                dve.wait_ge(y_turned, n + 3)
                nc.vector.tensor_copy(y_slots[:, z, :, :], YO[0:HC, 0:PARTS * D].rearrange("p (a f) -> p a f", a=PARTS)).then_inc(y_copied, 1)

            def group_step(i, s):
                if s >= 2:
                    turned_results(i, s - 2)
                if 1 <= s <= RING:
                    results(i, s - 1)

            every_group(dve, group_step)
            for t in range(TILES):
                dve.wait_ge(brought[t], TOP * 16)
                for k in range(TOP):
                    if k:
                        dve.wait_ge(added, t * TOP + k)
                    nc.vector.scalar_tensor_tensor(core.x[:, t, :], mine[k][:, t, :], share[:, k, t:t + 1], core.x[:, t, :],
                                                   ALU.mult, ALU.add).then_inc(added, 1)


def stage_moe(core):
    nc, d = core.nc, core.dram
    E, _, FF = d["L3_ffn_W1"].shape
    TOP = 2
    EARLY = 4
    FCH = FF // P
    BLOCKS = (TOP * TOKENS + E + E * (P - 1)) // P
    assert BLOCKS % 2 == 0
    with ExitStack() as ctx:
        st = Stage(core, ctx, "moe")
        ln = Norm(st)
        bank = [b[:, :] for b in core.bank]
        H, HT, Y, XT = bank[0:2], bank[2:4], bank[4:6], bank[6]
        gate = Gate(st, E, d["L3_ffn_Wg"], d["L3_ffn_bg"], bank[6][:, 0:TILES * E])
        xin = nc.dram_tensor("moe_xin", (BLOCKS * P, D), F32, kind="Internal").ap()
        y = nc.dram_tensor("moe_y", (BLOCKS * P, D), F32, kind="Internal").ap()
        w1, w2 = st.sb("w1", [P, E, CD, FF]), st.sb("w2", [P, E, FCH, D])
        b1, b2 = st.sb("b1", [P, E, FCH]), st.sb("b2", [P, E, D])
        b1_now = st.sb("b1_now", [P, 2, FCH])
        up_to = st.sb("up_to", [P, 2, P])
        not_behind = st.sb("not_behind", [P, E, E])
        number = st.sb("number", [P, BLOCKS])
        zeros = st.sb("zeros", [P, D])
        before = st.sb("before", [P, TILES + 1, E])
        first = st.sb("first", [P, TILES, E])
        chosen = st.sb("chosen", [P, TILES, E])
        count = st.sb("count", [P, E])
        square = st.sb("square", [P, E, E])
        blocks, end, start = st.sb("blocks", [P, E]), st.sb("end", [P, E]), st.sb("start", [P, E])
        all_slots = st.sb("all_slots", [P, TILES, E])
        slot, slot_u = st.sb("slot", [P, TOP, TILES]), st.sb("slot_u", [P, TOP, TILES], U32)
        share = st.sb("share", [P, TOP, TILES])
        ended = st.sb("ended", [P, BLOCKS, E])
        expert, expert_u = st.sb("expert", [P, BLOCKS]), st.sb("expert_u", [P, BLOCKS], U32)
        x_slots = st.sb("x_slots", [P, 2, D])
        xinT = st.sb("xinT", [P, 2, CD, P])
        h = st.sb("h", [P, FF])
        hT = st.sb("hT", [P, 2, FCH, P])
        y_slots = st.sb("y_slots", [P, 2, D])
        mine = [core.xn[:, :, :], core.xnT[:, :, :].rearrange("p c (t f) -> p (c t) f", f=D)]
        loaded = st.sem("loaded")
        w_loaded = [st.sem(f"w_loaded{e}") for e in range(E)]
        w_ready = st.sem("w_ready")
        zeros_ready, cleared = st.sem("zeros_ready"), st.sem("cleared")
        before_ready, ranked = st.sem("before_ready"), st.sem("ranked")
        slots_ready, experts_ready = st.sem("slots_ready"), st.sem("experts_ready")
        scattered = st.sem("scattered")
        x_loaded = [st.sem(f"x_loaded{k}") for k in range(2)]
        x_turned = st.sem("x_turned")
        xT_ready = st.sem("xT_ready")
        b1_ready = st.sem("b1_ready")
        up_done = st.sem("up_done")
        h_copied = st.sem("h_copied")
        h_turned = st.sem("h_turned")
        gelu_done = st.sem("gelu_done")
        down_done = st.sem("down_done")
        y_copied = st.sem("y_copied")
        y_written = [st.sem(f"y_written{k}") for k in range(2)]
        brought = [st.sem(f"brought{t}") for t in range(TILES)]
        added = st.sem("added")
        steps = st.sem("dve_steps")
        block = ctx.enter_context(nc.Block())

        def every_block(eng, body):
            body(0, 0, 0)
            with eng.Fori(0, BLOCKS // 2 - 1) as i:
                for k in (1, 2):
                    body(i * 2 + k, k % 2, i + k // 2)
            body(BLOCKS - 1, 1, BLOCKS // 2 - 1)
            body(BLOCKS, 0, BLOCKS // 2)

        def known(n, m):
            return isinstance(n, int) and n == m

        def expert_of(eng, n):
            return eng.value_load(expert_u[0:1, bass.ds(n, 1)], min_val=0, max_val=E - 1)

        @block.sync
        def _(sp):
            gate.sp(sp)
            sp.dma_start(up_to[:, :, :], d["up_to"]).then_inc(loaded, 16)
            sp.dma_start(number[:, :], d["number"][0:BLOCKS].partition_broadcast(P)).then_inc(loaded, 16)
            sp.dma_start(not_behind[:, :, :], d["not_behind"].partition_broadcast(P)).then_inc(loaded, 16)
            sp.dma_start(b1[:, :, :], d["L3_ffn_b1_cols"].rearrange("e p f -> p e f")).then_inc(loaded, 16)
            sp.dma_start(b2[:, :, :], d["L3_ffn_b2"].partition_broadcast(P)).then_inc(loaded, 16)
            sp.wait_ge(zeros_ready, 1)
            sp.dma_start(xin.rearrange("(n p) f -> p n f", p=P),
                         zeros[:, :].unsqueeze(1).broadcast_to([P, BLOCKS, D])).then_inc(cleared, 16)
            for e in range(E):
                if e == EARLY:
                    sp.wait_ge(scattered, TILES * TOP * 16)
                sp.dma_start(w1[:, e], d["L3_ffn_W1"][e].rearrange("(c p) f -> p c f", p=P)).then_inc(w_loaded[e], 16)
                sp.dma_start(w2[:, e], d["L3_ffn_W2"][e].rearrange("(c p) n -> p c n", p=P)).then_inc(w_loaded[e], 16)
            for e in range(E):
                sp.wait_ge(w_loaded[e], 32)
                sp.sem_inc(w_ready, 1 if e < E - 1 else 1 + BLOCKS - E)
            with sp.Fori(0, BLOCKS // 2) as i:
                for k in range(2):
                    sp.wait_ge(y_copied, i * 2 + k + 3)
                    sp.dma_start(y[bass.ds((i * 2 + k) * P, P), :], y_slots[:, k, :]).then_inc(y_written[k], 16)

        @block.gpsimd
        def _(pool):
            nc.gpsimd.memset(zeros[:, :], 0.0).then_inc(zeros_ready, 1)
            ln.pool(pool)
            pool.wait_ge(cleared, 16)
            pool.wait_ge(slots_ready, 1)
            pool.wait_ge(ln.xn_ready, TILES)
            for t in range(TILES):
                for k in range(TOP):
                    nc.gpsimd.indirect_dma_start(xin, bass.IndirectOffsetOnAxis(ap=slot_u[:, k, t:t + 1], axis=0),
                                                 core.xn[:, t, :], None).then_inc(scattered, 16)
            pool.wait_ge(scattered, TILES * TOP * 16)
            def load(i, k):
                rows = xin[bass.ds((i * 2 + k) * P, P), :]
                pool.dma_start(x_slots[:, k, :], rows).then_inc(x_loaded[k], 16)

            for k in range(2):
                load(0, k)
            with pool.Fori(1, BLOCKS // 2) as i:
                for k in range(2):
                    pool.wait_ge(x_turned, i * 2 + k - 1)
                    load(i, k)
            for k in range(2):
                pool.wait_ge(y_written[k], (BLOCKS // 2 + 1) * 16)
            for t in range(TILES):
                for k in range(TOP):
                    nc.gpsimd.indirect_dma_start(mine[k][:, t, :], None, y,
                                                 bass.IndirectOffsetOnAxis(ap=slot_u[:, k, t:t + 1], axis=0)).then_inc(brought[t], 16)

        @block.tensor
        def _(pe):
            ln.pe(pe)
            pe.wait_ge(ln.xnT_ready, 2 * CD)
            gate.pe(pe)
            pe.wait_ge(loaded, 80)
            pe.wait_ge(before_ready, 1)
            rank = bank[7][:, 0:TILES * E]
            nc.tensor.matmul(rank, up_to[:, 0, :], gate.mask[:, :, :], start=True, stop=False)
            nc.tensor.matmul(rank, up_to[:, 1, :], before[:, 0:TILES, :], start=False, stop=True)
            nc.tensor.matmul(bank[7][:, TILES * E:(TILES + 1) * E], up_to[:, 1, :], before[:, TILES, :],
                             start=True, stop=True).then_inc(ranked, 1)

            def turn_x(n, z, q):
                pe.wait_ge(x_loaded[z], q * 16 + 16)
                pe.wait_ge(xT_ready, n + 1)
                for c in range(CD):
                    mm = nc.tensor.transpose(XT[:, c * P:(c + 1) * P], x_slots[:, z, c * P:(c + 1) * P], core.ident[:, :])
                mm.then_inc(x_turned, 1)

            def up(n, z):
                e = expert_of(pe, n)
                pe.wait_ge(w_ready, n + 1)
                pe.wait_ge(xT_ready, n + 2)
                for k in range(2):
                    pe.wait_ge(h_copied, n * 2 + k + 1)
                    for c in range(CD):
                        mm = nc.tensor.matmul(H[k], xinT[:, z, c, :], w1[:, bass.ds(e, 1), c, k * HALF:(k + 1) * HALF].rearrange("p a f -> p (a f)"),
                                              start=(c == 0), stop=(c == CD - 1))
                    mm.then_inc(up_done, 1)

            def turn_h(n):
                for k in range(2):
                    pe.wait_ge(h_copied, n * 2 + k + 3)
                    pe.wait_ge(gelu_done, n * FCH + (k + 1) * FCH // 2)
                    for f in range(FCH // 2):
                        c = k * FCH // 2 + f
                        mm = nc.tensor.transpose(HT[k][:, f * P:(f + 1) * P], h[:, c * P:(c + 1) * P], core.ident[:, :])
                    mm.then_inc(h_turned, 1)

            def down(n, z):
                e = expert_of(pe, n)
                pe.wait_ge(gelu_done, (n + 2) * FCH)
                pe.wait_ge(y_copied, n + 1)
                for f in range(FCH):
                    mm = nc.tensor.matmul(Y[z][:, 0:D], hT[:, z, f, :], w2[:, bass.ds(e, 1), f, :].rearrange("p a f -> p (a f)"),
                                          start=(f == 0), stop=(f == FCH - 1))
                mm.then_inc(down_done, 1)

            pe.wait_ge(experts_ready, 1)
            turn_x(0, 0, 0)

            def step(n, z, q):
                if not known(n, BLOCKS):
                    up(n, z)
                    if not known(n, BLOCKS - 1):
                        turn_x(n + 1, 1 - z, q + z)
                if not known(n, 0):
                    down(n - 1, 1 - z)
                if not known(n, BLOCKS):
                    turn_h(n)

            every_block(pe, step)

        @block.scalar
        def _(act):
            ln.act(act)
            gate.act(act)
            act.sem_inc(xT_ready, 1)
            act.sem_inc(gelu_done, FCH)
            act.sem_inc(down_done, 1)
            act.sem_inc(up_done, 2)

            def turned_x(n, z):
                act.wait_ge(x_turned, n + 1)
                act.wait_ge(up_done, n * 2)
                nc.scalar.copy(xinT[:, z, :, :], XT[:, 0:D].rearrange("p (c n) -> p c n", c=CD)).then_inc(xT_ready, 1)

            turned_x(0, 0)

            def step(n, z, q):
                if not known(n, BLOCKS):
                    if not known(n, BLOCKS - 1):
                        turned_x(n + 1, 1 - z)
                    act.wait_ge(b1_ready, n + 1)
                    act.wait_ge(down_done, n)
                    for f in range(FCH):
                        k, c = divmod(f, FCH // 2)
                        if c == 0:
                            act.wait_ge(h_turned, n * 2 + k + 3)
                        nc.scalar.activation(hT[:, z, f, :], HT[k][:, c * P:(c + 1) * P], ACT.Gelu,
                                             bias=b1_now[:, z, f:f + 1]).then_inc(gelu_done, 1)

            every_block(act, step)

        @block.vector
        def _(dve):
            ln.dve(dve)
            step = Chain(dve, steps)
            gate.dve(dve, step)
            tiles = [P, TILES, E]
            step(nc.vector.memset(before[:, 0, :], 0.0))
            for t in range(TILES):
                add = nc.vector.tensor_tensor(before[:, t + 1, :], before[:, t, :], gate.mask[:, t, :], ALU.add)
                if t < TILES - 1:
                    step(add)
            add.then_inc(before_ready, 1)
            step(nc.vector.tensor_tensor(first[:, :, :], gate.mask[:, :, :], gate.second[:, :, :], ALU.subtract))
            dve.wait_ge(loaded, 80)
            dve.wait_ge(ranked, 1)
            rank = bank[7][:, 0:TILES * E].rearrange("p (t e) -> p t e", t=TILES)
            step(nc.vector.tensor_scalar(count[:, :], bank[7][:, TILES * E:(TILES + 1) * E], 1.0, 1.0 / P, ALU.max, ALU.mult))
            numbers = number[:, 0:E].unsqueeze(1).broadcast_to([P, E, E])
            step(nc.vector.tensor_tensor(square[:, :, :], count[:, :].unsqueeze(2).broadcast_to([P, E, E]), numbers, ALU.is_gt))
            step(nc.vector.tensor_reduce(blocks[:, :], square[:, :, :], AX.X, ALU.add))
            step(nc.vector.tensor_tensor(square[:, :, :], blocks[:, :].unsqueeze(1).broadcast_to([P, E, E]), not_behind[:, :, :], ALU.mult))
            step(nc.vector.tensor_reduce(end[:, :], square[:, :, :], AX.X, ALU.add))
            step(nc.vector.tensor_tensor(start[:, :], end[:, :], blocks[:, :], ALU.subtract))
            step(nc.vector.tensor_scalar(start[:, :], start[:, :], float(P), -1.0, ALU.mult, ALU.add))
            step(nc.vector.tensor_tensor(all_slots[:, :, :], rank, start[:, :].unsqueeze(1).broadcast_to(tiles), ALU.add))
            for k, picked in enumerate([first, gate.second]):
                step(nc.vector.tensor_tensor(chosen[:, :, :], all_slots[:, :, :], picked[:, :, :], ALU.mult))
                step(nc.vector.tensor_reduce(slot[:, k, :], chosen[:, :, :], AX.X, ALU.add))
            step(nc.vector.tensor_copy(slot_u[:, :, :], slot[:, :, :]))
            dve.sem_inc(slots_ready, 1)
            step(nc.vector.tensor_tensor(ended[:, :, :], end[:, :].unsqueeze(1).broadcast_to([P, BLOCKS, E]),
                                         number[:, :].unsqueeze(2).broadcast_to([P, BLOCKS, E]), ALU.is_le))
            step(nc.vector.tensor_reduce(expert[:, :], ended[:, :, :], AX.X, ALU.add))
            step(nc.vector.tensor_scalar(expert[:, :], expert[:, :], float(E - 1), None, ALU.min))
            step(nc.vector.tensor_copy(expert_u[:, :], expert[:, :]))
            dve.sem_inc(experts_ready, 1)
            for k, picked in enumerate([first, gate.second]):
                step(nc.vector.tensor_tensor(chosen[:, :, :], gate.weight[:, :, :], picked[:, :, :], ALU.mult))
                step(nc.vector.tensor_reduce(share[:, k, :], chosen[:, :, :], AX.X, ALU.add))
            dve.sem_inc(h_copied, 2)
            dve.sem_inc(h_turned, 2)
            dve.sem_inc(y_copied, 2)
            for k in range(2):
                dve.sem_inc(y_written[k], 16)

            def block_step(n, z, q):
                if not known(n, BLOCKS):
                    e = expert_of(dve, n)
                    dve.wait_ge(gelu_done, n * FCH)
                    nc.vector.tensor_copy(b1_now[:, z, :].unsqueeze(1), b1[:, bass.ds(e, 1), :]).then_inc(b1_ready, 1)
                    for k in range(2):
                        dve.wait_ge(up_done, n * 2 + k + 3)
                        dve.wait_ge(h_turned, n * 2 + k + 1)
                        nc.vector.tensor_copy(h[:, k * HALF:(k + 1) * HALF], H[k]).then_inc(h_copied, 1)
                if not known(n, 0):
                    e = expert_of(dve, n - 1)
                    dve.wait_ge(down_done, n + 1)
                    dve.wait_ge(y_written[1 - z], (q + z) * 16)
                    nc.vector.tensor_tensor(y_slots[:, 1 - z, :].unsqueeze(1), Y[1 - z][:, 0:D].unsqueeze(1), b2[:, bass.ds(e, 1), :],
                                            ALU.add).then_inc(y_copied, 1)

            every_block(dve, block_step)
            for t in range(TILES):
                dve.wait_ge(brought[t], TOP * 16)
                for k in range(TOP):
                    if k:
                        dve.wait_ge(added, t * TOP + k)
                    nc.vector.scalar_tensor_tensor(core.x[:, t, :], mine[k][:, t, :], share[:, k, t:t + 1], core.x[:, t, :],
                                                   ALU.mult, ALU.add).then_inc(added, 1)


def stage_xattn3(core):
    nc, d = core.nc, core.dram
    KV, CTX = d["ctx_768"].shape[1:]
    C1, C2, AUG = P, CTX - P, CTX + 1
    K2 = AUG - C1
    KCH = 3
    KP = -(-KV // KCH)
    LAST = KV - (KCH - 1) * KP
    rows_of = lambda c: KP if c < KCH - 1 else LAST
    SCALE = D ** -0.5
    with ExitStack() as ctx:
        st = Stage(core, ctx, "xattn3")
        ln = Norm(st, twice=True)
        wq, wo = st.sb("wq", [P, CD, D]), st.sb("wo", [P, CD, D])
        wkT = st.sb("wkT", [P, CD, AUG])
        wk1, wk2 = st.sb("wk1", [P, D]), st.sb("wk2", [C2, D])
        wv1, wv2 = st.sb("wv1", [P, D]), st.sb("wv2", [C2, D])
        cols = st.sb("cols", [P, 4 * CD])
        g1, s1 = st.sb("g1", [P, 1]), st.sb("s1", [P, 1])
        g2, s2 = st.sb("g2", [K2, 1]), st.sb("s2", [C2, 1])
        gx, sx = st.sb("gx", [P, CD]), st.sb("sx", [P, CD])
        bo = st.sb("bo", [1, D])
        raw = st.sb("raw", [KP, PER_TILE, KCH, CTX])
        stats = st.sb("stats", [KP, PER_TILE, KCH, 6])
        small = [KP, PER_TILE, KCH]
        mean, msum, diff, dsq = st.sb("mean", small), st.sb("msum", small), st.sb("diff", small), st.sb("dsq", small)
        m2, var, veps, rstd = st.sb("m2", small), st.sb("var", small), st.sb("veps", small), st.sb("rstd", small)
        neghalf = st.sb("neghalf", [KP, PER_TILE, KCH])
        norm = st.sb("norm", [KP, PER_TILE, KCH, AUG])
        nT1, nT2 = st.sb("nT1", [P, PER_TILE, KCH * KP]), st.sb("nT2", [K2, PER_TILE, KCH * KP])
        xT = st.sb("xT", [P, CD, TOKENS])
        qT = st.sb("qT", [P, CD, P])
        qk1, qk2 = st.sb("qk1", [P, P]), st.sb("qk2", [K2, P])
        negmax, rsum = st.sb("negmax", [P, 1]), st.sb("rsum", [P, 1])
        probs = st.sb("probs", [P, KV])
        probsT = st.sb("probsT", [KP, KCH, P])
        o_norm = st.sb("o_norm", [P, CTX])
        oT1, oT2 = st.sb("oT1", [P, P]), st.sb("oT2", [C2, P])
        aT = st.sb("aT", [P, CD, P])

        loaded = st.sem("loaded")
        raw_loaded = [st.sem(f"raw_loaded{b}") for b in range(PER_TILE)]
        raw_zero, norm_one, nT2_one = st.sem("raw_zero"), st.sem("norm_one"), st.sem("nT2_one")
        xT_ready = st.sem("xT_ready")
        shift_done, shift_ready = st.sem("shift_done"), st.sem("shift_ready")
        stats_done, parts_done, mean_ready = st.sem("stats_done"), st.sem("parts_done"), st.sem("mean_ready")
        neghalf_ready, veps_ready, rstd_ready = st.sem("neghalf_ready"), st.sem("veps_ready"), st.sem("rstd_ready")
        norm_ready = st.sem("norm_ready")
        n_turned, nT_ready = st.sem("n_turned"), st.sem("nT_ready")
        q_done, qT_ready, qk_done, qk_ready = st.sem("q_done"), st.sem("qT_ready"), st.sem("qk_done"), st.sem("qk_ready")
        scores_done, negmax_ready, probs_ready = st.sem("scores_done"), st.sem("negmax_ready"), st.sem("probs_ready")
        turned, probsT_ready, pv_done = st.sem("turned"), st.sem("probsT_ready"), st.sem("pv_done")
        rsum_ready, o_ready = st.sem("rsum_ready"), st.sem("o_ready")
        o_turned, oT_ready = st.sem("o_turned"), st.sem("oT_ready")
        a_done, aT_ready = st.sem("a_done"), st.sem("aT_ready")
        y_done, x_done = st.sem("y_done"), st.sem("x_done")
        bank = [b[:, :] for b in core.bank]
        WORK, SCORES, OUT, TURN = bank[4], bank[5], bank[6], bank[7]
        LOADS = 17
        block = ctx.enter_context(nc.Block())

        @block.sync
        def _(sp):
            w = lambda to, of: sp.dma_start(to, of).then_inc(loaded, 16)
            p = "L3_xattn_"
            w(wq[:, :, :], d[p + "Wq"].rearrange("(c p) n -> p c n", p=P))
            w(wo[:, :, :], d[p + "Wo"].rearrange("(c p) n -> p c n", p=P))
            w(wkT[:, :, :], d[p + "Wk_T"].rearrange("(c p) n -> p c n", p=P))
            w(wk1[:, :], d[p + "Wk"][0:C1, :])
            w(wk2[:, :], d[p + "Wk"][C1:CTX, :])
            w(wv1[:, :], d[p + "Wv"][0:C1, :])
            w(wv2[:, :], d[p + "Wv"][C1:CTX, :])
            for n, name in enumerate(["bq", "bk", "bv"]):
                w(cols[:, n * CD:(n + 1) * CD], d[p + name + "_cols"])
            column = lambda name, a, b: d[p + name][a:b].rearrange("(p a) -> p a", a=1)
            w(g1[:, :], column("ln2_g", 0, C1))
            w(s1[:, :], column("ln2_b", 0, C1))
            w(g2[0:C2, :], column("ln2_g", C1, CTX))
            w(s2[:, :], column("ln2_b", C1, CTX))
            w(gx[:, :], d[p + "ln1_g_cols"])
            w(sx[:, :], d[p + "ln1_b_cols"])
            w(bo[:, :], d[p + "bo"].rearrange("(a n) -> a n", a=1))
            sp.wait_ge(raw_zero, 1)

            def load(i, b):
                rows = d["ctx_768"][bass.ds(i * PER_TILE + b, 1)]
                head, tail = rows[:, 0:(KCH - 1) * KP, :], rows[:, (KCH - 1) * KP:KV, :]
                sp.dma_start(raw[:, b, 0:KCH - 1, :], head.rearrange("a (c p) f -> p (a c) f", p=KP)).then_inc(raw_loaded[b], 16)
                sp.dma_start(raw[0:LAST, b, KCH - 1, :], tail.rearrange("a p f -> p (a f)")).then_inc(raw_loaded[b], 16)

            for b in range(PER_TILE):
                load(0, b)
            with sp.Fori(1, TILES) as i:
                for b in range(PER_TILE):
                    sp.wait_ge(norm_ready, (i - 1) * PER_TILE + b + 1)
                    load(i, b)

        @block.gpsimd
        def _(pool):
            ln.pool(pool)
            pool.wait_ge(neghalf_ready, 1)
            with pool.Fori(0, TILES) as i:
                pool.wait_ge(veps_ready, i + 1)
                nc.gpsimd.tensor_tensor(rstd[:, :, :], veps[:, :, :], neghalf[:, :, :], ALU.pow).then_inc(rstd_ready, 1)

        @block.tensor
        def _(pe):
            ln.pe(pe)
            pe.wait_ge(loaded, 16 * LOADS)
            for c in range(CD):
                f = slice(c * P, (c + 1) * P)
                nc.tensor.matmul(bank[4 + c][:, 0:1], wk1[:, f], s1[:, :], start=True, stop=False)
                nc.tensor.matmul(bank[4 + c][:, 0:1], wk2[:, f], s2[:, :], start=False, stop=True).then_inc(shift_done, 1)
            pe.wait_ge(shift_ready, CD)
            pe.wait_ge(xT_ready, 2 * CD)
            pe.wait_ge(nT2_one, 2)
            with pe.Fori(0, TILES) as i:
                for b in range(PER_TILE):
                    pe.wait_ge(norm_ready, i * PER_TILE + b + 1)
                    pe.wait_ge(nT_ready, (i * PER_TILE + b + 1) * 2)
                    for c in range(KCH):
                        nc.tensor.transpose(bank[2 * (b % 2)][:, c * KP:(c + 1) * KP], norm[:, b, c, 0:C1], core.ident[0:KP, 0:KP])
                        mm = nc.tensor.transpose(bank[2 * (b % 2) + 1][0:C2, c * KP:(c + 1) * KP], norm[:, b, c, C1:CTX], core.ident[0:KP, 0:KP])
                    mm.then_inc(n_turned, 1)
                    if b == 0:
                        pe.wait_ge(x_done, i + 1)
                        for j in range(CD):
                            for c in range(CD):
                                mm = nc.tensor.matmul(WORK[:, j * P:(j + 1) * P], wq[:, c, j * P:(j + 1) * P], xT[:, c, bass.ds(i * P, P)],
                                                      start=(c == 0), stop=(c == CD - 1))
                        mm.then_inc(q_done, 1)
                    if b == 1:
                        pe.wait_ge(qT_ready, (i + 1) * CD)
                        for c in range(CD):
                            nc.tensor.matmul(OUT[:, 0:P], wkT[:, c, 0:C1], qT[:, c, :], start=(c == 0), stop=(c == CD - 1))
                        for c in range(CD):
                            mm = nc.tensor.matmul(TURN[0:K2, 0:P], wkT[:, c, C1:AUG], qT[:, c, :], start=(c == 0), stop=(c == CD - 1))
                        mm.then_inc(qk_done, 1)
                pe.wait_ge(qk_ready, (i + 1) * 2)
                for b in range(PER_TILE):
                    pe.wait_ge(nT_ready, (i * PER_TILE + b + 1) * 2 + 4)
                    r = slice(b * SEQ, (b + 1) * SEQ)
                    nc.tensor.matmul(SCORES[r, 0:KV], qk1[:, r], nT1[:, b, 0:KV], start=True, stop=False, tile_position=(0, b * SEQ))
                    mm = nc.tensor.matmul(SCORES[r, 0:KV], qk2[:, r], nT2[:, b, 0:KV], start=False, stop=True, tile_position=(0, b * SEQ))
                mm.then_inc(scores_done, 1)
                pe.wait_ge(probs_ready, i + 1)
                for c in range(KCH):
                    mm = nc.tensor.transpose(TURN[0:rows_of(c), c * P:(c + 1) * P], probs[:, c * KP:c * KP + rows_of(c)], core.ident[:, :])
                mm.then_inc(turned, 1)
                pe.wait_ge(probsT_ready, (i + 1) * 2)
                for b in range(PER_TILE):
                    r = slice(b * SEQ, (b + 1) * SEQ)
                    for c in range(KCH):
                        mm = nc.tensor.matmul(OUT[r, 0:AUG], probsT[0:rows_of(c), c, r], norm[0:rows_of(c), b, c, :], start=(c == 0),
                                              stop=(c == KCH - 1), tile_position=(0, b * SEQ))
                mm.then_inc(pv_done, 1)
                pe.wait_ge(o_ready, i + 1)
                nc.tensor.transpose(TURN[:, 0:P], o_norm[:, 0:C1], core.ident[:, :])
                nc.tensor.transpose(TURN[0:C2, P:2 * P], o_norm[:, C1:CTX], core.ident[:, :]).then_inc(o_turned, 1)
                pe.wait_ge(oT_ready, (i + 1) * 2)
                for j in range(CD):
                    nc.tensor.matmul(WORK[:, j * P:(j + 1) * P], wv1[:, j * P:(j + 1) * P], oT1[:, :], start=True, stop=False)
                    mm = nc.tensor.matmul(WORK[:, j * P:(j + 1) * P], wv2[:, j * P:(j + 1) * P], oT2[:, :], start=False, stop=True)
                mm.then_inc(a_done, 1)
                pe.wait_ge(aT_ready, (i + 1) * CD)
                for c in range(CD):
                    nc.tensor.matmul(WORK[:, 0:D], aT[:, c, :], wo[:, c, :], start=(c == 0), stop=False)
                nc.tensor.matmul(WORK[:, 0:D], core.ones[:, 0:P], bo[:, :], start=False, stop=True).then_inc(y_done, 1)

        @block.scalar
        def _(act):
            act.sem_inc(nT_ready, 4)
            act.sem_inc(scores_done, 1)
            act.sem_inc(pv_done, 1)
            act.wait_ge(loaded, 16 * LOADS)
            for g in range(TILES // 4):
                act.wait_ge(ln.turned, g + 1)
                for c in range(CD):
                    nc.scalar.activation(xT[:, c, g * HALF:(g + 1) * HALF], bank[2 * g + c], ACT.Identity, bias=sx[:, c:c + 1],
                                         scale=gx[:, c:c + 1]).then_inc(xT_ready, 1)
            with act.Fori(0, TILES) as i:
                for b in range(PER_TILE):
                    act.wait_ge(n_turned, i * PER_TILE + b + 1)
                    if b == 0:
                        act.wait_ge(scores_done, i + 1)
                    nc.scalar.copy(nT1[:, b, :], bank[2 * (b % 2)][:, 0:KCH * KP]).then_inc(nT_ready, 1)
                    nc.scalar.copy(nT2[0:C2, b, :], bank[2 * (b % 2) + 1][0:C2, 0:KCH * KP]).then_inc(nT_ready, 1)
                act.wait_ge(negmax_ready, i + 1)
                nc.scalar.activation(probs[:, :], SCORES[:, 0:KV], ACT.Exp, bias=negmax[:, 0:1]).then_inc(probs_ready, 1)
                act.wait_ge(rsum_ready, i + 1)
                nc.scalar.mul(o_norm[:, :], OUT[:, 0:CTX], rsum[:, 0:1]).then_inc(o_ready, 1)
                for c in range(CD):
                    act.wait_ge(a_done, i + 1)
                    nc.scalar.activation(aT[:, c, :], WORK[:, c * P:(c + 1) * P], ACT.Identity,
                                         bias=cols[:, 2 * CD + c:2 * CD + c + 1]).then_inc(aT_ready, 1)

        @block.vector
        def _(dve):
            nc.vector.memset(raw[:, :, :, :], 0.0).then_inc(raw_zero, 1)
            nc.vector.memset(neghalf[:, :, :], -0.5).then_inc(neghalf_ready, 1)
            nc.vector.memset(norm[:, :, :, CTX:AUG], 1.0).then_inc(norm_one, 1)
            nc.vector.memset(nT2[C2:K2, :, :], 1.0).then_inc(nT2_one, 1)
            nc.vector.memset(g2[C2:K2, :], 1.0).then_inc(nT2_one, 1)
            ln.dve(dve)
            dve.sem_inc(x_done, 1)
            dve.wait_ge(loaded, 16 * LOADS)
            for c in range(CD):
                dve.wait_ge(shift_done, CD)
                nc.vector.tensor_tensor(wkT[:, c, CTX:AUG], bank[4 + c][:, 0:1], cols[:, CD + c:CD + c + 1], ALU.add).then_inc(shift_ready, 1)
            dve.wait_ge(norm_one, 1)
            dve.wait_ge(nT2_one, 2)

            def rows_stats(i, b):
                dve.wait_ge(raw_loaded[b], (i + 1) * 32)
                for c in range(KCH):
                    nc.vector.bn_stats(stats[:, b, c, :], raw[:, b, c, :]).then_inc(stats_done, 1)

            with dve.Fori(0, TILES) as i:
                for b in range(PER_TILE):
                    rows_stats(i, b)
                dve.wait_ge(stats_done, (i + 1) * PER_TILE * KCH)
                PARTS = 5
                nc.vector.tensor_tensor(msum[:, :, :], stats[:, :, :, 1], stats[:, :, :, 4], ALU.add).then_inc(parts_done, 1)
                nc.vector.tensor_tensor(diff[:, :, :], stats[:, :, :, 1], stats[:, :, :, 4], ALU.subtract).then_inc(parts_done, 1)
                nc.vector.tensor_tensor(m2[:, :, :], stats[:, :, :, 2], stats[:, :, :, 5], ALU.add).then_inc(parts_done, 1)
                dve.wait_ge(parts_done, i * PARTS + 2)
                nc.vector.scalar_tensor_tensor(dsq[:, :, :], diff[:, :, :], 0.25, diff[:, :, :], ALU.mult, ALU.mult).then_inc(parts_done, 1)
                dve.wait_ge(parts_done, i * PARTS + 4)
                nc.vector.scalar_tensor_tensor(var[:, :, :], m2[:, :, :], 1.0 / CTX, dsq[:, :, :], ALU.mult, ALU.add).then_inc(parts_done, 1)
                dve.wait_ge(parts_done, i * PARTS + 5)
                nc.vector.tensor_scalar(veps[:, :, :], var[:, :, :], EPS, None, ALU.add).then_inc(veps_ready, 1)
                nc.vector.tensor_scalar(mean[:, :, :], msum[:, :, :], 0.5, None, ALU.mult).then_inc(mean_ready, 1)
                dve.wait_ge(mean_ready, i + 1)
                dve.wait_ge(rstd_ready, i + 1)
                dve.wait_ge(pv_done, i + 1)
                for b in range(PER_TILE):
                    for c in range(KCH):
                        last = nc.vector.tensor_scalar(norm[:, b, c, 0:CTX], raw[:, b, c, :], mean[:, b, c:c + 1], rstd[:, b, c:c + 1],
                                                       ALU.subtract, ALU.mult)
                    last.then_inc(norm_ready, 1)
                dve.wait_ge(q_done, i + 1)
                for j in range(CD):
                    nc.vector.tensor_scalar(qT[:, j, :], WORK[:, j * P:(j + 1) * P], cols[:, j:j + 1], SCALE, ALU.add,
                                            ALU.mult).then_inc(qT_ready, 1)
                dve.wait_ge(qk_done, i + 1)
                nc.vector.tensor_scalar(qk1[:, :], OUT[:, 0:P], g1[:, 0:1], None, ALU.mult).then_inc(qk_ready, 1)
                nc.vector.tensor_scalar(qk2[:, :], TURN[0:K2, 0:P], g2[:, 0:1], None, ALU.mult).then_inc(qk_ready, 1)
                dve.wait_ge(scores_done, i + 2)
                nc.vector.tensor_reduce(negmax[:, 0:1], SCORES[:, 0:KV], AX.X, ALU.max, negate=True).then_inc(negmax_ready, 1)
                dve.wait_ge(turned, i + 1)
                nc.vector.tensor_copy(probsT[:, 0:KCH - 1, :], TURN[0:KP, 0:(KCH - 1) * P].rearrange("p (c n) -> p c n", n=P)).then_inc(probsT_ready, 1)
                nc.vector.tensor_copy(probsT[0:LAST, KCH - 1, :], TURN[0:LAST, (KCH - 1) * P:KCH * P]).then_inc(probsT_ready, 1)
                dve.wait_ge(pv_done, i + 2)
                nc.vector.reciprocal(rsum[:, 0:1], OUT[:, CTX:AUG]).then_inc(rsum_ready, 1)
                dve.wait_ge(o_turned, i + 1)
                nc.vector.tensor_scalar(oT1[:, :], TURN[:, 0:P], g1[:, 0:1], s1[:, 0:1], ALU.mult, ALU.add).then_inc(oT_ready, 1)
                nc.vector.tensor_scalar(oT2[:, :], TURN[0:C2, P:2 * P], g2[0:C2, 0:1], s2[:, 0:1], ALU.mult, ALU.add).then_inc(oT_ready, 1)
                dve.wait_ge(y_done, i + 1)
                xi = core.x[:, bass.ds(i, 1), :].rearrange("p a n -> p (a n)")
                nc.vector.tensor_tensor(xi, xi, WORK[:, 0:D], ALU.add).then_inc(x_done, 1)


def program(nc, dram, out, stages):
    with ExitStack() as ctx:
        core = Core(nc, ctx, dram)
        loaded = ctx.enter_context(nc.semaphore("x_loaded"))
        with nc.Block() as block:
            @block.sync
            def _(sp):
                sp.dma_start(core.x[:, :, :], dram["x"].rearrange("(t b) s n -> (b s) t n", t=TILES)).then_inc(loaded, 16)
                sp.dma_start(core.ident[:, :], dram["ident"]).then_inc(loaded, 16)
                sp.wait_ge(loaded, 32)

            @block.vector
            def _(dve):
                nc.vector.memset(core.ones[:, :], 1.0)
                nc.vector.memset(core.neghalf[:, :], -0.5)
        todo = {0: stage_xattn0, 1: stage_attn0, 2: stage_fp4_ffn, 3: stage_xattn1, 4: stage_attn1, 5: stage_low_rank, 6: stage_xattn2, 7: stage_scan, 8: stage_moe_capacity, 9: stage_xattn3, 10: stage_attn3, 11: stage_moe}
        for s in stages:
            todo[s](core)
        stored = ctx.enter_context(nc.semaphore("stored"))
        with nc.Block() as block:
            @block.sync
            def _(sp):
                sp.dma_start(out.rearrange("(t b) s n -> (b s) t n", t=TILES), core.x[:, :, :]).then_inc(stored, 16)
                sp.wait_ge(stored, 16)


def kernel(**inputs):
    import concourse.bacc as _bacc
    from concourse import mybir as _mybir
    from concourse.bass_utils import run_bass_kernel_spmd as _run

    def turn(name):
        return np.ascontiguousarray(np.swapaxes(np.asarray(inputs[name]), -1, -2))

    data = {k: np.ascontiguousarray(np.asarray(v)) for k, v in inputs.items()}
    for name in ["L0_xattn_Wk", "L1_xattn_Wk", "L2_xattn_w_k", "L1_ffn_W", "L1_ffn_C", "L1_attn_Wq", "L1_attn_Wk", "L1_attn_Wv",
                 "L3_attn_Wq", "L3_attn_Wk", "L3_attn_Wv", "L3_attn_Wo"]:
        data[name + "_T"] = turn(name)
    for name in ["L0_xattn_Wk_T", "L2_xattn_w_k_T"]:
        data[name] = np.concatenate([data[name], data[name][:, P:]], axis=1)
    data["ident"] = np.eye(P, dtype=np.float32)

    ctx = data["ctx_768"]
    ones = np.ones(ctx.shape[:2] + (1,), np.float32)
    data["ctxA"] = np.concatenate([ctx, ones], axis=2)
    data["ctxT"] = np.ascontiguousarray(np.swapaxes(data["ctxA"], 1, 2))
    HEADS, HD = 16, 16
    wkT, bk = data["L1_xattn_Wk_T"], data["L1_xattn_bk"]
    wk_heads = np.zeros((HEADS, P, 2 * P), np.float32)
    wv_heads = np.zeros((wkT.shape[1], HEADS, P), np.float32)
    for h in range(HEADS):
        r, o = slice(h * HD, (h + 1) * HD), slice(h * HD % P, h * HD % P + HD)
        wk_heads[h, o, :wkT.shape[1]] = wkT[r]
        wk_heads[h, o, wkT.shape[1]] = bk[r]
        wv_heads[:, h, o] = data["L1_xattn_Wv"][:, r]
    data["L1_wv_heads"] = wv_heads
    data["L1_wk_heads"] = wk_heads.reshape(HEADS * P, 2 * P)
    for name in ["L1_xattn_bv", "L0_attn_b_qkv", "L3_attn_bq", "L3_attn_bk"]:
        data[name + "_cols"] = np.ascontiguousarray(data[name].reshape(-1, P).T)
    rel = np.clip(np.arange(SEQ)[:, None] - np.arange(SEQ)[None, :] + 256, 0, 512)
    data["L0_rel"] = np.ascontiguousarray(np.tile(data["L0_attn_rel_bias"][rel].transpose(0, 2, 1), (PER_TILE, 1, 1)))
    data["head_of"] = np.repeat(np.eye(P // HD, dtype=np.float32), HD, axis=0)
    data["L0_ffn_up"] = np.concatenate([data["L0_ffn_w_gate"], data["L0_ffn_w_up"]], axis=0)
    for name in ["L2_attn_key_w", "L2_attn_vq_w", "L2_attn_out_w"]:
        data[name + "_T"] = turn(name)
    data["L2_attn_key_b_cols"] = np.ascontiguousarray(data["L2_attn_key_b"].reshape(-1, P).T)
    p = np.arange(P)
    same_head = p[:, None] // HD == p[None, :] // HD
    spread = same_head[:, None, :] & (p[:, None, None] % HD == np.arange(HD)[None, :, None])
    data["spread"] = np.ascontiguousarray(spread, dtype=np.float32)
    data["gather"] = np.ascontiguousarray(spread.transpose(2, 1, 0), dtype=np.float32)
    data["number"] = np.arange(512, dtype=np.float32)
    data["up_to"] = np.ascontiguousarray(np.stack([np.triu(np.ones((P, P), np.float32)), np.ones((P, P), np.float32)], axis=1))
    data["not_behind"] = np.tril(np.ones((8, 8), np.float32))
    for name in ["L2_ffn_b1", "L2_ffn_b2", "L3_ffn_b1"]:
        data[name + "_cols"] = np.ascontiguousarray(data[name].reshape(data[name].shape[0], -1, P).transpose(0, 2, 1))
    data["L3_xattn_Wk_T"] = np.pad(turn("L3_xattn_Wk"), ((0, 0), (0, 1)))
    for name in ["bq", "bk", "bv", "ln1_g", "ln1_b"]:
        data[f"L3_xattn_{name}_cols"] = np.ascontiguousarray(data[f"L3_xattn_{name}"].reshape(-1, P).T)

    nc = _bacc.Bacc("TRN2", target_bir_lowering=False, num_devices=1)
    arrays, dram = {}, {}
    for name, a in data.items():
        arrays[f"in_{name}"] = a
        dram[name] = nc.dram_tensor(f"in_{name}", a.shape, _mybir.dt.from_np(a.dtype), kind="ExternalInput").ap()
    out = nc.dram_tensor("out_0_dram", (BATCH, SEQ, D), F32, kind="ExternalOutput").ap()
    program(nc, dram, out, STAGES)
    r = _run(nc, [arrays], core_ids=[0])
    return r.results[0]["out_0_dram"]
```
